# Optimizing a Trainium2 kernel written in Bass

```python
import numpy as np
import jax
import jax.numpy as jnp

def _softmax(x, axis=-1):
    return jax.nn.softmax(x, axis=axis)

def _gelu(x):
    return jax.nn.gelu(x, approximate=True)

def _silu(x):
    return jax.nn.silu(x)

def _sigmoid(x):
    return jax.nn.sigmoid(x)

def _layernorm(x, axis=-1, eps=1e-05):
    m = jnp.mean(x, axis=axis, keepdims=True)
    v = jnp.var(x, axis=axis, keepdims=True)
    return (x - m) / jnp.sqrt(v + eps)

def _scatter_add(tgt, idx, src, axis=0):
    return tgt.at[idx].add(src)

def _segment_sum(src, seg, n):
    return jax.ops.segment_sum(src, seg, n)
kernel_name = 'mk_adaln_d2_jaxref_r8_30acf8'

def setup_inputs(seed: int=0):
    np.random.seed(seed)
    _w = jnp.asarray

    def _L0_attn_setup():
        import jax, jax.numpy as jnp
        import numpy as np
        B, S, E, H = (2, 256, 256, 16)
        D = E // H
        NEG = -1e+30

        def alibi_slopes(n_heads):
            return jnp.asarray(2.0 ** (-8.0 * np.arange(1, n_heads + 1) / n_heads), dtype=jnp.float32)
        key = jax.random.key(seed)
        ks = jax.random.split(key, 5)
        sc = 0.02
        return {'x': jax.random.normal(ks[0], (B, S, E), dtype=jnp.float32), 'Wq': jax.random.normal(ks[1], (E, E), dtype=jnp.float32) * sc, 'Wk': jax.random.normal(ks[2], (E, E), dtype=jnp.float32) * sc, 'Wv': jax.random.normal(ks[3], (E, E), dtype=jnp.float32) * sc, 'Wo': jax.random.normal(ks[4], (E, E), dtype=jnp.float32) * sc, 'bo': jnp.zeros((E,), dtype=jnp.float32)}
    _L0_attn_in = _L0_attn_setup()

    def _L0_ffn_setup():
        import jax, jax.numpy as jnp
        import numpy as np
        DIM_IN = 256
        DIM_HIDDEN = 1024
        key = jax.random.key(seed)
        k_x, k_g, k_u, k_d = jax.random.split(key, 4)
        s_in = 1.0 / np.sqrt(DIM_IN)
        s_hid = 1.0 / np.sqrt(DIM_HIDDEN)
        x = jax.random.normal(k_x, (4, 256, DIM_IN), dtype=jnp.float32)
        w_gate = jax.random.uniform(k_g, (DIM_HIDDEN, DIM_IN), jnp.float32, -s_in, s_in)
        w_up = jax.random.uniform(k_u, (DIM_HIDDEN, DIM_IN), jnp.float32, -s_in, s_in)
        w_down = jax.random.uniform(k_d, (DIM_IN, DIM_HIDDEN), jnp.float32, -s_hid, s_hid)
        return {'x': x, 'w_gate': w_gate, 'w_up': w_up, 'w_down': w_down}
    _L0_ffn_in = _L0_ffn_setup()
    _L0_c = _w((lambda *s: np.random.randn(*s).astype(np.float32) * 0.05)(4, 256))
    _L0_wmod = _w((lambda *s: np.random.randn(*s).astype(np.float32) * 0.05)(256, 6 * 256) * 256 ** (-0.5))

    def _L1_attn_setup():
        import jax, jax.numpy as jnp
        import numpy as np
        B, N, D = (2, 512, 256)
        H, DH, W = (8, 128, 64)
        SCALE = 8.0

        def _l2norm(t):
            return t / jnp.maximum(jnp.linalg.norm(t, axis=-1, keepdims=True), 1e-12)
        key = jax.random.key(seed)
        ks = jax.random.split(key, 5)
        return {'x': jax.random.normal(ks[0], (B, N, D), jnp.float32), 'Wq': jax.random.normal(ks[1], (H * DH, D), jnp.float32) * 0.02, 'Wkv': jax.random.normal(ks[2], (2 * H * DH, D), jnp.float32) * 0.02, 'q_scale': jnp.ones((DH,), jnp.float32), 'k_scale': jnp.ones((DH,), jnp.float32), 'Wg': jax.random.normal(ks[3], (H, D), jnp.float32) * 0.02, 'bg': jnp.zeros((H,), jnp.float32), 'Wo': jax.random.normal(ks[4], (D, H * DH), jnp.float32) * 0.02}
    _L1_attn_in = _L1_attn_setup()

    def _L1_ffn_setup():
        import jax, jax.numpy as jnp
        import numpy as np
        E, H, I = (8, 256, 512)
        TOP_K = 1
        B, S = (1, 256)
        key = jax.random.key(seed)
        ks = jax.random.split(key, 7)
        std = 0.02
        return {'hidden_states': jax.random.normal(ks[0], (B, S, H), dtype=jnp.float32), 'router_w': jax.random.normal(ks[1], (E, H), dtype=jnp.float32) * std, 'gate_up_proj': jax.random.normal(ks[2], (E, H, 2 * I), dtype=jnp.float32) * std, 'down_proj': jax.random.normal(ks[3], (E, I, H), dtype=jnp.float32) * std, 'shared_gate_w': jax.random.normal(ks[4], (H, I), dtype=jnp.float32) * std, 'shared_up_w': jax.random.normal(ks[5], (H, I), dtype=jnp.float32) * std, 'shared_down_w': jax.random.normal(ks[6], (I, H), dtype=jnp.float32) * std}
    _L1_ffn_in = _L1_ffn_setup()
    _L1_c = _w((lambda *s: np.random.randn(*s).astype(np.float32) * 0.05)(4, 256))
    _L1_wmod = _w((lambda *s: np.random.randn(*s).astype(np.float32) * 0.05)(256, 6 * 256) * 256 ** (-0.5))
    _d = {'L0_attn_x': _L0_attn_in['x'], 'L0_attn_Wq': _L0_attn_in['Wq'], 'L0_attn_Wk': _L0_attn_in['Wk'], 'L0_attn_Wv': _L0_attn_in['Wv'], 'L0_attn_Wo': _L0_attn_in['Wo'], 'L0_attn_bo': _L0_attn_in['bo'], 'L0_ffn_w_gate': _L0_ffn_in['w_gate'], 'L0_ffn_w_up': _L0_ffn_in['w_up'], 'L0_ffn_w_down': _L0_ffn_in['w_down'], 'L0_c': _L0_c, 'L0_wmod': _L0_wmod, 'L1_attn_Wq': _L1_attn_in['Wq'], 'L1_attn_Wkv': _L1_attn_in['Wkv'], 'L1_attn_q_scale': _L1_attn_in['q_scale'], 'L1_attn_k_scale': _L1_attn_in['k_scale'], 'L1_attn_Wg': _L1_attn_in['Wg'], 'L1_attn_bg': _L1_attn_in['bg'], 'L1_attn_Wo': _L1_attn_in['Wo'], 'L1_ffn_router_w': _L1_ffn_in['router_w'], 'L1_ffn_gate_up_proj': _L1_ffn_in['gate_up_proj'], 'L1_ffn_down_proj': _L1_ffn_in['down_proj'], 'L1_ffn_shared_gate_w': _L1_ffn_in['shared_gate_w'], 'L1_ffn_shared_up_w': _L1_ffn_in['shared_up_w'], 'L1_ffn_shared_down_w': _L1_ffn_in['shared_down_w'], 'L1_c': _L1_c, 'L1_wmod': _L1_wmod}
    _x0 = _d['L0_attn_x']
    _d['L0_attn_x'] = jax.random.normal(jax.random.fold_in(jax.random.key(seed), 1), (4, 512, 256), dtype=_x0.dtype)
    del _x0
    return _d

def reference(L0_attn_x, L0_attn_Wq, L0_attn_Wk, L0_attn_Wv, L0_attn_Wo, L0_attn_bo, L0_ffn_w_gate, L0_ffn_w_up, L0_ffn_w_down, L0_c, L0_wmod, L1_attn_Wq, L1_attn_Wkv, L1_attn_q_scale, L1_attn_k_scale, L1_attn_Wg, L1_attn_bg, L1_attn_Wo, L1_ffn_router_w, L1_ffn_gate_up_proj, L1_ffn_down_proj, L1_ffn_shared_gate_w, L1_ffn_shared_up_w, L1_ffn_shared_down_w, L1_c, L1_wmod):

    def _L0_attn_ref(x, Wq, Wk, Wv, Wo, bo):
        import jax, jax.numpy as jnp
        import numpy as np
        B, S, E, H = (2, 256, 256, 16)
        D = E // H
        NEG = -1e+30

        def alibi_slopes(n_heads):
            return jnp.asarray(2.0 ** (-8.0 * np.arange(1, n_heads + 1) / n_heads), dtype=jnp.float32)
        b, s, e = x.shape
        q = (x @ Wq).reshape(b, s, H, D).transpose(0, 2, 1, 3)
        k = (x @ Wk).reshape(b, s, H, D).transpose(0, 2, 1, 3)
        v = (x @ Wv).reshape(b, s, H, D).transpose(0, 2, 1, 3)
        scores = jnp.einsum('bhqd,bhkd->bhqk', q, k)
        i = jnp.arange(s)[:, None]
        j = jnp.arange(s)[None, :]
        causal = j <= i
        scores = jnp.where(causal[None, None], scores, NEG)
        bias = alibi_slopes(H)[:, None, None] * (j - i).astype(jnp.float32)
        scores = scores + bias[None]
        scores = scores / jnp.sqrt(jnp.float32(D))
        w = jax.nn.softmax(scores, axis=-1)
        ctx = jnp.einsum('bhqk,bhkd->bqhd', w, v).reshape(b, s, e)
        return ctx @ Wo + bo

    def _L0_ffn_ref(x, w_gate, w_up, w_down):
        import jax, jax.numpy as jnp
        import numpy as np
        DIM_IN = 256
        DIM_HIDDEN = 1024
        gate = jnp.einsum('bsd,hd->bsh', x, w_gate)
        up = jnp.einsum('bsd,hd->bsh', x, w_up)
        gated = jax.nn.silu(gate) * up
        return jnp.einsum('bsh,dh->bsd', gated, w_down)

    def _L1_attn_ref(x, Wq, Wkv, q_scale, k_scale, Wg, bg, Wo):
        import jax, jax.numpy as jnp
        import numpy as np
        B, N, D = (2, 512, 256)
        H, DH, W = (8, 128, 64)
        SCALE = 8.0

        def _l2norm(t):
            return t / jnp.maximum(jnp.linalg.norm(t, axis=-1, keepdims=True), 1e-12)
        b, n, _ = x.shape
        inner = H * DH
        q = (x @ Wq.T).reshape(b, n, H, DH).transpose(0, 2, 1, 3)
        kv = x @ Wkv.T
        k = kv[..., :inner].reshape(b, n, H, DH).transpose(0, 2, 1, 3)
        v = kv[..., inner:].reshape(b, n, H, DH).transpose(0, 2, 1, 3)
        q = _l2norm(q) * q_scale
        k = _l2norm(k) * k_scale
        nb = n // W
        qb = q.reshape(b, H, nb, W, DH)
        kb = k.reshape(b, H, nb, W, DH)
        vb = v.reshape(b, H, nb, W, DH)

        def look_around(t):
            prev = jnp.concatenate([jnp.zeros_like(t[:, :, :1]), t[:, :, :-1]], axis=2)
            return jnp.concatenate([prev, t], axis=3)
        kw, vw = (look_around(kb), look_around(vb))
        pos = jnp.arange(n).reshape(nb, W)
        pos_prev = jnp.concatenate([jnp.full((1, W), -1), pos[:-1]], axis=0)
        posk = jnp.concatenate([pos_prev, pos], axis=1)
        dist = pos[:, :, None] - posk[:, None, :]
        mask = (posk[:, None, :] >= 0) & (dist >= 0) & (dist <= W)
        sim = jnp.einsum('bhnid,bhnjd->bhnij', qb * SCALE, kw)
        sim = jnp.where(mask, sim, jnp.finfo(sim.dtype).min)
        attn = jax.nn.softmax(sim, axis=-1)
        o = jnp.einsum('bhnij,bhnjd->bhnid', attn, vw).reshape(b, H, n, DH)
        gates = jax.nn.sigmoid(jnp.einsum('bnd,hd->bhn', x, Wg) + bg[None, :, None])
        o = o * gates[..., None]
        o = o.transpose(0, 2, 1, 3).reshape(b, n, inner)
        return o @ Wo.T

    def _L1_ffn_ref(hidden_states, router_w, gate_up_proj, down_proj, shared_gate_w, shared_up_w, shared_down_w):
        import jax, jax.numpy as jnp
        import numpy as np
        E, H, I = (8, 256, 512)
        TOP_K = 1
        B, S = (1, 256)
        orig_shape = hidden_states.shape
        x = hidden_states.reshape(-1, H)
        T = x.shape[0]
        logits = x @ router_w.T
        top_vals, top_idx = jax.lax.top_k(logits, TOP_K)
        scores = jnp.full_like(logits, -jnp.inf)
        scores = scores.at[jnp.arange(T)[:, None], top_idx].set(top_vals)
        scores = jax.nn.sigmoid(scores.astype(jnp.float32)).astype(logits.dtype)
        xr = x[None, :, :] * scores.T[:, :, None]
        gate_up = jnp.einsum('eth,ehf->etf', xr, gate_up_proj)
        gate, up = jnp.split(gate_up, 2, axis=-1)
        routed = jnp.einsum('etf,efh->eth', up * jax.nn.silu(gate), down_proj)
        routed_sum = routed.sum(axis=0)
        shared = jax.nn.silu(x @ shared_gate_w) * (x @ shared_up_w) @ shared_down_w
        return (shared + routed_sum).reshape(orig_shape)
    x = L0_attn_x
    mod = (_silu(L0_c) @ L0_wmod).reshape(L0_c.shape[0], 6, 1, -1)
    sa, ca, ga, sb, cb, gb = (mod[:, 0], mod[:, 1], mod[:, 2], mod[:, 3], mod[:, 4], mod[:, 5])
    ga = (2 * (ga >= 0) - 1) * jnp.maximum(jnp.abs(ga), 0.25)
    gb = (2 * (gb >= 0) - 1) * jnp.maximum(jnp.abs(gb), 0.25)
    h = _layernorm(x, axis=-1) * (1 + ca) + sa
    x = x + ga * _L0_attn_ref(h, L0_attn_Wq, L0_attn_Wk, L0_attn_Wv, L0_attn_Wo, L0_attn_bo)
    h = _layernorm(x, axis=-1) * (1 + cb) + sb
    x = x + gb * _L0_ffn_ref(h, L0_ffn_w_gate, L0_ffn_w_up, L0_ffn_w_down)
    mod = (_silu(L1_c) @ L1_wmod).reshape(L1_c.shape[0], 6, 1, -1)
    sa, ca, ga, sb, cb, gb = (mod[:, 0], mod[:, 1], mod[:, 2], mod[:, 3], mod[:, 4], mod[:, 5])
    ga = (2 * (ga >= 0) - 1) * jnp.maximum(jnp.abs(ga), 0.25)
    gb = (2 * (gb >= 0) - 1) * jnp.maximum(jnp.abs(gb), 0.25)
    h = _layernorm(x, axis=-1) * (1 + ca) + sa
    x = x + ga * _L1_attn_ref(h, L1_attn_Wq, L1_attn_Wkv, L1_attn_q_scale, L1_attn_k_scale, L1_attn_Wg, L1_attn_bg, L1_attn_Wo)
    h = _layernorm(x, axis=-1) * (1 + cb) + sb
    x = x + gb * _L1_ffn_ref(h, L1_ffn_router_w, L1_ffn_gate_up_proj, L1_ffn_down_proj, L1_ffn_shared_gate_w, L1_ffn_shared_up_w, L1_ffn_shared_down_w)
    return x

_drawn_inputs = setup_inputs


def setup_inputs(seed=0):
    import zlib

    import numpy as np

    out = dict(_drawn_inputs(seed))
    spreads = {'L0_attn_bo': (0.0, 0.33),
     'L1_attn_q_scale': (1.0, 0.6),
     'L1_attn_k_scale': (1.0, 0.6),
     'L1_attn_bg': (0.0, 0.8)}
    factors = {'L0_attn_Wq': 8.0,
     'L0_attn_Wk': 8.0,
     'L0_attn_Wv': 8.0,
     'L0_attn_Wo': 8.0,
     'L1_attn_Wq': 8.0,
     'L1_attn_Wkv': 8.0,
     'L1_attn_Wg': 8.0,
     'L1_attn_Wo': 8.0,
     'L1_ffn_router_w': 8.0,
     'L1_ffn_gate_up_proj': 8.0,
     'L1_ffn_down_proj': 8.0,
     'L1_ffn_shared_gate_w': 8.0,
     'L1_ffn_shared_up_w': 8.0,
     'L1_ffn_shared_down_w': 8.0,
     'L1_c': 7.226,
     'L1_wmod': 6.837}
    for name, (base, spread) in spreads.items():
        noise = np.random.default_rng([zlib.crc32(name.encode()), seed]).standard_normal(out[name].shape)
        drawn = base * np.exp(spread * noise) if base else spread * noise
        out[name] = jnp.asarray(drawn.astype(out[name].dtype))
    for name, factor in factors.items():
        out[name] = (out[name] * factor).astype(out[name].dtype)
    return out
```

```python
from contextlib import ExitStack

import concourse.bass as bass
from concourse import mybir

ALU = mybir.AluOpType
ACT = mybir.ActivationFunctionType
AX_X = mybir.AxisListType.X
F32 = mybir.dt.float32
BF16 = mybir.dt.bfloat16
I32 = mybir.dt.int32

P = 128
B, S, E = 4, 512, 256
NT = S // P
TILES = B * NT
KE = E // P
H0, D0 = 16, 16
HG = H0 // 2
F0 = 1024
H1, D1 = 8, 128
INNER = H1 * D1
WIN = 64
NEXP, FE = 8, 512
SLOTS = TILES + NEXP
EPS = 1e-5

Q_PARTS = [0, 0, 1, 1, 0, 2]
K_PARTS = [0, 1, 0, 1, 2, 0]
BIAS_ROW = 16 * len(Q_PARTS)
MAX_ROW = BIAS_ROW + 3
STACK = MAX_ROW + 3

KM_W = [S - P * kt for kt in range(NT)]
KM_OFF = [0, 512, 1024, 896]
KM = sum(KM_W)


def program(nc, x_d, cT_d, wmod0_d, wmod1_d, wq0_d, wk0_d, wv0_d, wo0_d, bo_d, wgate_d, wup_d, wdown_d,
            wq1_d, wkv1_d, qs_d, ks_d, wg1_d, bg_d, wo1_d, router_d, gu_d, dn_d, sg_d, su_d, sd_d,
            ident_d, identb_d, maskq_d, maskk_d, maskw_d, before_d, kaug_d, thr_d, iota_d, incl_d, w8_d, out_d):
    rows_d = nc.dram_tensor("routed_rows", (SLOTS * P, E), F32).ap()
    yrows_d = nc.dram_tensor("routed_out", (SLOTS * P, E), F32).ap()

    with ExitStack() as ctx:
        def sb(name, shape, dt=F32):
            return ctx.enter_context(nc.sbuf_tensor(name, shape, dt))

        def sem(name):
            return ctx.enter_context(nc.semaphore(name))

        x_all = sb("x_all", [P, TILES * E])
        xhat = sb("xhat", [P, NT, E])
        hT = sb("hT", [P, KE, S])
        gates_bc = sb("gates_bc", [P, 24, E])
        modT = sb("modT", [P, 2, 12, B])
        ident = sb("ident", [P, P])
        identb = sb("identb", [P, P], BF16)
        maskq = sb("maskq", [P, P], BF16)
        maskk = sb("maskk", [P, P], BF16)
        maskw = sb("maskw", [P, WIN + P], BF16)
        before = sb("before", [P, P], BF16)
        ones_b = sb("ones_b", [P, P], BF16)
        stats = sb("stats", [P, NT, 6])
        lsum = sb("lsum", [P, NT, 2])
        ldif = sb("ldif", [P, NT])
        lvar = sb("lvar", [P, NT])
        lsq = sb("lsq", [P, NT])
        mean = sb("mean", [P, NT])
        vareps = sb("vareps", [P, NT])
        rstd = sb("rstd", [P, NT])
        minus_half = sb("minus_half", [P, 8])
        qscale = sb("qscale", [P, 1])
        kscale = sb("kscale", [P, 1])
        scT = sb("scT", [P, 2, KE, B])
        cT = sb("cT", [P, 2, KE, B])
        small = sb("small", [P, 256])

        AR = 30720
        arena = sb("arena", [P, AR])

        def ar(off, n):
            return arena[:, off:off + n]

        o = 0
        qst = ar(o, 4096).bitcast(BF16).rearrange("p (h n) -> p h n", h=H0); o += 4096
        kst = ar(o, 4096).bitcast(BF16).rearrange("p (h n) -> p h n", h=H0); o += 4096
        parts = ar(o, 3072).bitcast(BF16).rearrange("p (i a n) -> p i a n", i=4, a=3); o += 3072
        resid = ar(o, 2048).rearrange("p (i n) -> p i n", i=4); o += 2048
        vaug = ar(o, 2048).rearrange("p (t h c) -> p t h c", t=NT, h=H0); o += 2048
        probs = ar(o, 8 * KM).rearrange("p (h n) -> p h n", h=8); o += 8 * KM
        ctx0 = ar(o, 1024).rearrange("p (t e) -> p t e", t=NT); o += 1024
        ctxT = ar(o, 1024).rearrange("p (c n) -> p c n", c=KE); o += 1024
        oTs = ar(o, 1024).rearrange("p (i n) -> p i n", i=2); o += 1024
        gabo = ar(o, 1024).rearrange("p (b e) -> p b e", b=B); o += 1024
        rowmax = ar(o, 64).rearrange("p (h t) -> p h t", h=H0); o += 64
        rden = ar(o, 32).rearrange("p (i n) -> p i n", i=2); o += 32
        mres = ar(o, 256).rearrange("p (g n) -> p g n", g=2); o += 256
        mparts = ar(o, 384).bitcast(BF16).rearrange("p (g a n) -> p g a n", g=2, a=3); o += 384
        assert o <= AR
        zero_rows = ar(AR - 256, 256)
        assert o <= AR - 256
        bo_bc = ctxT[:, 0, 0:256]
        wmod = [ar(0, 3072).rearrange("p (c n) -> p c n", c=KE), ar(3072, 3072).rearrange("p (c n) -> p c n", c=KE)]
        sc_bc = ar(6144, 2048).rearrange("p (l c b n) -> p l c b n", l=2, c=KE, b=B)
        guard = [ar(15360 + 2048 * i, 2048).rearrange("p (k e) -> p k e", k=8) for i in range(4)]
        gT = ar(0, 4096).rearrange("p (f n) -> p f n", f=8)
        sgT = ar(4096, 1024).rearrange("p (i n) -> p i n", i=2)
        utmp = sb("utmp", [P, 2, E])
        o = 0
        qT1 = ar(o, 4096).rearrange("p (h n) -> p h n", h=H1); o += 4096
        kT1 = ar(o, 4096).rearrange("p (h n) -> p h n", h=H1); o += 4096
        v1 = ar(o, 4096).rearrange("p (t n) -> p t n", t=NT); o += 4096
        qn = ar(o, 2048).rearrange("p (i n) -> p i n", i=2); o += 2048
        sq = ar(o, 2048).rearrange("p (i n) -> p i n", i=2); o += 2048
        pr1 = ar(o, 2048).rearrange("p (i h n) -> p i h n", i=2, h=4); o += 2048
        pT1 = ar(o, 2048).rearrange("p (i h k n) -> p i h k n", i=2, h=4, k=2); o += 2048
        oT1 = ar(o, 2048).rearrange("p (i h n) -> p i h n", i=2, h=H1); o += 2048
        W1 = o
        assert W1 + 8192 <= AR
        wq1 = ar(W1, 2048).rearrange("p (c n) -> p c n", c=KE)
        wkv1 = ar(W1 + 2048, 4096).rearrange("p (c n) -> p c n", c=KE)
        wo1 = ar(W1 + 6144, 2048).rearrange("p (h n) -> p h n", h=H1)
        wgu = ar(0, 16384).rearrange("p (c n) -> p c n", c=KE)
        wdn = ar(16384, 8192).rearrange("p (c n) -> p c n", c=4)
        h_all = ar(24576, 4096)
        yg = h_all.rearrange("p (t e) -> p t e", t=TILES)

        WA = sb("WA", [P, 8192])

        def wa(off, n):
            return WA[:, off:off + n]

        w0 = [wa(512 * i, 512).rearrange("p (c n) -> p c n", c=KE) for i in range(4)]
        wgate = wa(2048, 2048).rearrange("p (c n) -> p c n", c=KE)
        wup = wa(4096, 2048).rearrange("p (c n) -> p c n", c=KE)
        wdown = wa(6144, 2048).rearrange("p (f n) -> p f n", f=8)
        shg = wa(0, 1024).rearrange("p (c n) -> p c n", c=KE)
        shu = wa(1024, 1024).rearrange("p (c n) -> p c n", c=KE)
        shd = wa(2048, 1024).rearrange("p (f n) -> p f n", f=4)
        hs = wa(3072, 1024).rearrange("p (t e) -> p t e", t=NT)
        gTs = wa(4096, 2048).rearrange("p (f n) -> p f n", f=4)
        sgTs = wa(6144, 1024).rearrange("p (i n) -> p i n", i=2)
        xs = wa(3072, 512).rearrange("p (j e) -> p j e", j=2)
        xsT = wa(3584, 512).rearrange("p (j c n) -> p j c n", j=2, c=KE)
        sgs = wa(4096, 1024).rearrange("p (j n) -> p j n", j=2)
        acts = wa(5120, 1024).rearrange("p (j n) -> p j n", j=2)
        actT = wa(6144, 1024).rearrange("p (j f n) -> p j f n", j=2, f=4)
        ys = wa(7168, 512).rearrange("p (j e) -> p j e", j=2)
        wg1 = sb("wg1", [P, KE, H1])
        bg_bc = sb("bg_bc", [P, H1])
        router = sb("router", [P, KE, NEXP])
        logits = sb("logits", [P, TILES * NEXP])
        g1 = sb("g1", [P, NT * H1])
        ssq = sb("ssq", [P, 2, H1])
        rnorm = sb("rnorm", [P, 2, H1])
        nmax1 = sb("nmax1", [P, 2, 4])
        rsum1 = sb("rsum1", [P, 2, 4])
        rinv1 = sb("rinv1", [P, 2, 4])
        pos_i = sb("pos_i", [P, TILES], I32)
        slot_e = sb("slot_e", [P, SLOTS], I32)
        score = sb("score", [P, TILES])
        r_eq = wa(3072, 128).rearrange("p (t e) -> p t e", t=TILES)
        r_oh = wa(3200, 128).rearrange("p (t e) -> p t e", t=TILES)
        r_ohx = wa(3328, 68).bitcast(BF16).rearrange("p (t e) -> p t e", t=TILES + 1)
        r_thr = wa(3456, 128).rearrange("p (e j) -> p e j", e=NEXP)
        r_iota = wa(3584, SLOTS * NEXP).rearrange("p (s e) -> p s e", e=NEXP)
        r_incl = wa(3840, 64).rearrange("p (e j) -> p e j", e=NEXP)
        r_w8 = wa(3904, 128).rearrange("p (t e) -> p t e", t=TILES)
        r_a = wa(4096, 256)
        r_n = wa(4352, 8)
        r_nt = wa(4360, 8)
        r_end = wa(4368, 8)
        r_base = wa(4376, 8)
        r_m = wa(4384, 16)
        r_f = wa(4400, SLOTS)
        r_pos = wa(4432, 16)

        ps = ctx.enter_context(nc.psum_tensor("ps", [P, 8, 512], F32))
        ps_flat = ps[:, :, :].rearrange("p b n -> p (b n)")

        def banks(i, n=2):
            return ps_flat[:, 512 * i:512 * (i + n)]

        def mod_cols(kind):
            return kind * E, kind * E + E
        G0, G1, SC1 = 0, 8, 16

        names = """in_x0 in_x in_c in_mod in_const in_wqkv in_wo0 in_ffn in_kaug in_bo in_w1 in_sh in_exp in_small1
        in_rt zero_done zfill
        setup_v silu_c scbc_done modT_ps modT_done modT_plus bc_ps bc_sb guard_v gates_done gabo_done pre_pool preset
        ln_stats ln_mv ln_var ln_rstd xhat_ready
        a_xT a_h a_qk a_p1 a_r1 a_p2 a_p3 a_stack0 a_stack1 a_v a_vc a_s1 a_max a_mT a_m1 a_m2 a_m3 a_m4 a_mrow0
        a_mrow1 a_s2 a_exp a_pv a_oT a_oTT a_rc a_ctx a_cT a_cTe a_o a_tmp a_x a_xb
        b_xT b_h b_g b_u b_sg b_gt b_o b_tmp b_x
        c_xT c_h c_gp c_gz c_ge c_g1 c_gate c_p c_sq c_ss c_rk0 c_rk c_qn c_qT c_qe c_v c_ve c_s c_mx c_e c_ri c_pn
        c_pT c_pTe c_o c_oe c_w c_tmp c_x
        d_h0 d_h d_hc d_xT d_hT d_l d_lc d_g d_u d_sg d_gt d_o d_tmp d_x
        r_v r_R r_exp r_xr r_scatter r_pos_ok
        m_in0 m_in1 m_xT m_xTe m_gu m_sg m_a m_aT m_aTe m_d m_y m_out0 m_out1 m_gather f_tmp f_x f_out""".split()
        identb_d, maskq_d, maskk_d, maskw_d, before_d, kaug_d = (
            a.bitcast(BF16) for a in (identb_d, maskq_d, maskk_d, maskw_d, before_d, kaug_d))
        s = {n: sem("s_" + n) for n in names}

        block = ctx.enter_context(nc.Block())

        x_rows = x_d.rearrange("b (t p) e -> p b t e", p=P)
        out_rows = out_d.rearrange("b (t p) e -> p (b t) e", p=P)

        def chunks(w):
            return w.rearrange("(c p) n -> p c n", p=P)

        @block.sync
        def _(sp):
            sp.dma_start(x_all[:, 0:NT * E].rearrange("p (t e) -> p t e", e=E), x_rows[:, 0]).then_inc(s["in_x0"], 16)
            sp.dma_start(cT[:, :, :, :], cT_d).then_inc(s["in_c"], 16)
            sp.dma_start(ident[:, :], ident_d).then_inc(s["in_const"], 16)
            sp.dma_start(wmod[0], chunks(wmod0_d)).then_inc(s["in_mod"], 16)
            sp.dma_start(wmod[1], chunks(wmod1_d)).then_inc(s["in_mod"], 16)
            for dst, src in ((identb[:, :], identb_d), (maskq[:, :], maskq_d), (maskk[:, :], maskk_d),
                             (maskw[:, :], maskw_d), (before[:, :], before_d)):
                sp.dma_start(dst, src).then_inc(s["in_const"], 16)
            for i, w in enumerate((wq0_d, wk0_d, wv0_d)):
                sp.dma_start(w0[i], chunks(w)).then_inc(s["in_wqkv"], 16)
            sp.dma_start(w0[3], chunks(wo0_d)).then_inc(s["in_wo0"], 16)
            sp.dma_start(bo_bc, bo_d).then_inc(s["in_bo"], 16)
            for b in range(1, B):
                sp.dma_start(x_all[:, b * NT * E:(b + 1) * NT * E].rearrange("p (t e) -> p t e", e=E),
                             x_rows[:, b]).then_inc(s["in_x"], 16)
            sp.wait_ge(s["bc_ps"], 12)
            sp.dma_start(kst[BIAS_ROW:STACK], kaug_d).then_inc(s["in_kaug"], 16)
            sp.dma_start(wgate, chunks(wgate_d)).then_inc(s["in_ffn"], 16)
            sp.dma_start(wup, chunks(wup_d)).then_inc(s["in_ffn"], 16)
            sp.dma_start(wdown, chunks(wdown_d)).then_inc(s["in_ffn"], 16)
            for dst, src in ((wg1[:, :, :], chunks(wg1_d)), (bg_bc[:, :], bg_d), (qscale[:, :], qs_d),
                             (kscale[:, :], ks_d), (router[:, :, :], chunks(router_d))):
                sp.dma_start(dst, src).then_inc(s["in_small1"], 16)
            sp.wait_ge(s["zero_done"], 1)
            for j in range(SLOTS):
                sp.dma_start(rows_d[j * P:(j + 1) * P, :], zero_rows).then_inc(s["zfill"], 16)

            with sp.Fori(0, B) as b:
                for i in range(4):
                    g, st, pt = i // 2, (qst, kst)[i % 2], (Q_PARTS, K_PARTS)[i % 2]
                    sp.wait_ge(s["a_p3"], 4 * b + i + 1)
                    for r, part in enumerate(pt):
                        sp.dma_start(st[16 * r:16 * r + 16, HG * g:HG * g + HG, :], parts[:, i, part, :])\
                            .then_inc(s[f"a_stack{g}"], 16)
                for g in range(2):
                    sp.wait_ge(s["a_m4"], 2 * b + g + 1)
                    for a in range(3):
                        sp.dma_start(qst[MAX_ROW + a:MAX_ROW + a + 1, HG * g:HG * g + HG, :],
                                     mparts[0:32, g, a, :]).then_inc(s[f"a_mrow{g}"], 16)

            sp.wait_ge(s["a_x"], 1 + TILES)
            sp.wait_ge(s["zfill"], 16 * SLOTS)
            sp.dma_start(wq1, chunks(wq1_d)).then_inc(s["in_w1"], 16)
            sp.dma_start(wkv1, chunks(wkv1_d)).then_inc(s["in_w1"], 16)
            sp.dma_start(wo1, chunks(wo1_d)).then_inc(s["in_w1"], 16)
            sp.wait_ge(s["b_x"], 1 + TILES)
            sp.dma_start(shg, chunks(sg_d)).then_inc(s["in_sh"], 16)
            sp.dma_start(shu, chunks(su_d)).then_inc(s["in_sh"], 16)
            sp.dma_start(shd, chunks(sd_d)).then_inc(s["in_sh"], 16)
            sp.wait_ge(s["c_x"], 1 + TILES)
            for e in range(NEXP):
                sp.dma_start(wgu[:, :, e * 2 * FE:(e + 1) * 2 * FE], chunks(gu_d[e])).then_inc(s["in_exp"], 16)
                sp.dma_start(wdn[:, :, e * E:(e + 1) * E], chunks(dn_d[e])).then_inc(s["in_exp"], 16)
            sp.wait_ge(s["d_x"], 1 + TILES)
            sp.wait_ge(s["d_hc"], 1 + B)
            for dst, src in ((r_thr, thr_d), (r_iota, iota_d), (r_incl, incl_d), (r_w8, w8_d)):
                sp.dma_start(dst, src).then_inc(s["in_rt"], 16)

            sp.wait_ge(s["r_scatter"], 16 * TILES)

            def rows_in(slot, j):
                sp.wait_ge(s["m_xT"], slot + 1)
                sp.dma_start(xs[:, j, :], rows_d[bass.ds(slot * P, P), :]).then_inc(s[f"m_in{j}"], 16)

            def rows_out(slot, j):
                sp.wait_ge(s["m_y"], slot + 1)
                sp.dma_start(yrows_d[bass.ds(slot * P, P), :], ys[:, j, :]).then_inc(s[f"m_out{j}"], 16)

            rows_in(0, 0)
            rows_in(1, 1)
            with sp.Fori(0, SLOTS // 2 - 1) as i:
                rows_in(2 * i + 2, 0)
                rows_out(2 * i, 0)
                rows_in(2 * i + 3, 1)
                rows_out(2 * i + 1, 1)
            rows_out(SLOTS - 2, 0)
            rows_out(SLOTS - 1, 1)

            for t in range(TILES):
                sp.wait_ge(s["f_x"], t + 1)
                sp.dma_start(out_rows[:, t], x_all[:, t * E:(t + 1) * E]).then_inc(s["f_out"], 16)
            sp.wait_ge(s["f_out"], 16 * TILES)

        @block.gpsimd
        def _(pool):
            gp = nc.gpsimd

            def ln_pool(n):
                pool.wait_ge(s["ln_var"], n + 1)
                gp.tensor_tensor(rstd[:, :], vareps[:, :], minus_half[:, 0:NT], ALU.pow).then_inc(s["ln_rstd"], 1)

            gp.memset(minus_half[:, :], -0.5).then_inc(s["pre_pool"], 1)
            gp.memset(zero_rows, 0.0).then_inc(s["zero_done"], 1)
            gp.memset(ones_b[:, :], 1.0).then_inc(s["pre_pool"], 1)
            pool.wait_ge(s["pre_pool"], 2)
            ln_pool(0)
            pool.wait_ge(s["bc_ps"], 12)
            gp.memset(qst[BIAS_ROW:MAX_ROW], 1.0).then_inc(s["preset"], 1)
            pool.wait_ge(s["preset"], 1)
            gp.memset(vaug[:, :, :, D0:32], 0.0).then_inc(s["preset"], 1)
            pool.wait_ge(s["preset"], 2)
            gp.memset(vaug[:, :, :, D0:D0 + 1], 1.0).then_inc(s["preset"], 1)
            pool.wait_ge(s["gabo_done"], 1)
            with pool.Fori(0, B) as b:
                xb = x_all[:, bass.ds(b * (NT * E), NT * E)].rearrange("p (t e) -> p t e", e=E)
                pool.wait_ge(s["xhat_ready"], NT * b + NT)
                gp.tensor_tensor(xb, xb, gabo[:, bass.ds(b, 1), :].to_broadcast([P, NT, E]), ALU.add)\
                    .then_inc(s["a_xb"], 1)
                for i in range(4):
                    pool.wait_ge(s["a_p2"], 4 * b + i + 1)
                    gp.tensor_tensor(parts[:, i, 2, :], resid[:, i, :], parts[:, i, 1, :], ALU.subtract)\
                        .then_inc(s["a_p3"], 1)
                for g in range(2):
                    pool.wait_ge(s["a_m3"], 2 * b + g + 1)
                    gp.tensor_tensor(mparts[0:32, g, 2, :], mres[0:32, g, :], mparts[0:32, g, 1, :], ALU.subtract)\
                        .then_inc(s["a_m4"], 1)
                ln_pool(b + 1)
            with pool.Fori(0, B) as b:
                ln_pool(B + 1 + b)
            pool.wait_ge(s["b_x"], 1 + TILES)
            for i in range(2):
                gp.memset(pr1[:, i, :, 0:WIN], 0.0).then_inc(s["preset"], 1)
            with pool.Fori(0, B) as b:
                for u in range(2 * NT):
                    pool.wait_ge(s["c_rk0"], 2 * NT * b + u + 1)
                    gp.tensor_tensor(rnorm[:, u % 2, :], ssq[:, u % 2, :], minus_half[:, :], ALU.pow)\
                        .then_inc(s["c_rk"], 1)
                ln_pool(2 * B + 1 + b)
            with pool.Fori(0, B - 1) as b:
                ln_pool(3 * B + 1 + b)
            pool.wait_ge(s["zfill"], 16 * SLOTS)
            pool.wait_ge(s["r_pos_ok"], 1)
            for t in range(TILES):
                pool.wait_ge(s["r_xr"], t + 1)
                gp.indirect_dma_start(rows_d, bass.IndirectOffsetOnAxis(ap=pos_i[:, t:t + 1], axis=0),
                                      h_all[:, t * E:(t + 1) * E], None).then_inc(s["r_scatter"], 16)
            pool.wait_ge(s["r_scatter"], 16 * TILES)
            pool.wait_ge(s["m_out0"], 16 + 16 * (SLOTS // 2))
            pool.wait_ge(s["m_out1"], 16 + 16 * (SLOTS // 2))
            for t in range(TILES):
                gp.indirect_dma_start(yg[:, t, :], None, yrows_d,
                                      bass.IndirectOffsetOnAxis(ap=pos_i[:, t:t + 1], axis=0))\
                    .then_inc(s["m_gather"], 16)

        @block.scalar
        def _(act):
            ac = nc.scalar

            def h_out(n_b, xT_sem, h_sem, base, layer, shift, scale):
                for c in range(KE):
                    act.wait_ge(xT_sem, KE * n_b + c + 1)
                    ac.activation(hT[:, c, :], ps[:, c, :], ACT.Identity,
                                  bias=modT[:, layer, shift + c, bass.ds(n_b, 1)],
                                  scale=modT[:, layer, scale + c, bass.ds(n_b, 1)]).then_inc(h_sem, 1)

            def ffn_act(b, nf, sgbuf, k):
                for f in range(nf):
                    act.wait_ge(s[k + "_g"], nf * b + f + 1)
                    if f >= 2:
                        act.wait_ge(s[k + "_gt"], nf * b + f - 1)
                    ac.activation(sgbuf[:, f % 2, :], ps[:, 2 + 2 * (f % 3), :], ACT.Silu).then_inc(s[k + "_sg"], 1)

            act.wait_ge(s["in_c"], 16)
            ac.activation(scT[:, :, :, :].rearrange("p l c b -> p (l c b)"),
                          cT[:, :, :, :].rearrange("p l c b -> p (l c b)"), ACT.Silu).then_inc(s["silu_c"], 1)
            act.wait_ge(s["modT_plus"], 1)

            with act.Fori(0, B) as b:
                h_out(b, s["a_xT"], s["a_h"], 0, 0, 0, 2)

                def second_part(i):
                    act.wait_ge(s["a_r1"], 4 * b + i + 1)
                    ac.copy(parts[:, i, 1, :], resid[:, i, :]).then_inc(s["a_p2"], 1)

                for i in range(4):
                    act.wait_ge(s["a_qk"], 4 * b + i + 1)
                    ac.copy(parts[:, i, 0, :], ps[:, 2 + i, :]).then_inc(s["a_p1"], 1)
                    if i >= 1:
                        second_part(i - 1)
                second_part(3)
                for g in range(2):
                    act.wait_ge(s["a_mT"], 2 * b + g + 1)
                    ac.copy(mparts[0:32, g, 0, :], ps[0:32, 7, 0:P]).then_inc(s["a_m1"], 1)
                    act.wait_ge(s["a_m2"], 2 * b + g + 1)
                    ac.copy(mparts[0:32, g, 1, :], mres[0:32, g, :]).then_inc(s["a_m3"], 1)
                for h in range(H0):
                    act.wait_ge(s["a_s2"], H0 * b + h + 1)
                    if h >= 8:
                        act.wait_ge(s["a_pv"], 4 * b + (h - 8) // 4 + 1)
                    ac.activation(probs[:, h % 8, :], banks(3 * (h % 2), 3)[:, 0:KM], ACT.Exp,
                                  scale=float(D0) ** -0.5).then_inc(s["a_exp"], 1)
                for c in range(KE):
                    act.wait_ge(s["a_cT"], KE * b + c + 1)
                    ac.copy(ctxT[:, c, :], ps[:, c, :]).then_inc(s["a_cTe"], 1)
            with act.Fori(0, B) as b:
                h_out(b, s["b_xT"], s["b_h"], 0, 0, 6, 8)
                ffn_act(b, 8, sgT, "b")
            with act.Fori(0, B) as b:
                h_out(b, s["c_xT"], s["c_h"], 0, 1, 0, 2)
                act.wait_ge(s["c_gz"], NT * b + NT)
                ac.activation(small[:, 32:64], small[:, 0:32], ACT.Exp, scale=-1.0).then_inc(s["c_ge"], 1)

                def qk_out(u):
                    act.wait_ge(s["c_qT"], 2 * NT * b + u + 1)
                    dst, sc = (qT1, qscale) if u % 2 == 0 else (kT1, kscale)
                    t = u // 2
                    ac.activation(dst[:, :, t * P:(t + 1) * P], banks(6).rearrange("p (h n) -> p h n", h=H1),
                                  ACT.Copy, scale=sc[:, 0:1]).then_inc(s["c_qe"], 1)

                for u in range(2 * NT):
                    act.wait_ge(s["c_p"], 2 * NT * b + u + 1)
                    if u >= 2:
                        act.wait_ge(s["c_ss"], 2 * NT * b + u - 1)
                    ac.activation(sq[:, u % 2, :], banks(2 + 2 * (u % 2)), ACT.Square).then_inc(s["c_sq"], 1)
                    if u % 2 == 1:
                        t = u // 2
                        act.wait_ge(s["c_v"], NT * b + t + 1)
                        ac.copy(v1[:, t, :], banks(0)).then_inc(s["c_ve"], 1)
                    if u >= 2:
                        qk_out(u - 2)
                qk_out(2 * NT - 2)
                qk_out(2 * NT - 1)
                for i in range(2 * NT + 2):
                    if i < 2 * NT:
                        t = i // 2
                        c0 = P if t == 0 else WIN
                        act.wait_ge(s["c_mx"], 2 * NT * b + i + 1)
                        if i >= 2:
                            act.wait_ge(s["c_pT"], 2 * NT * b + i - 1)
                        sc4 = banks(2 * (i % 2)).rearrange("p (h n) -> p h n", h=4)
                        for hh in range(4):
                            ac.activation(pr1[:, i % 2, hh, c0:], sc4[:, hh, c0:], ACT.Exp,
                                          bias=nmax1[:, i % 2, hh:hh + 1],
                                          accum_out=rsum1[:, i % 2, hh:hh + 1]).then_inc(s["c_e"], 1)
                    if i >= 2:
                        v = i - 2
                        act.wait_ge(s["c_o"], 2 * NT * b + v + 1)
                        ac.copy(oT1[:, (v // 2) % 2, 4 * (v % 2):4 * (v % 2) + 4, :].rearrange("p h n -> p (h n)"),
                                ps[:, 6, :]).then_inc(s["c_oe"], 1)
            with act.Fori(0, B) as b:
                act.wait_ge(s["d_h"], b + 1)
                ac.copy(h_all[:, bass.ds(b * (NT * E), NT * E)], hs.rearrange("p t e -> p (t e)"))\
                    .then_inc(s["d_hc"], 1)
                for c in range(KE):
                    act.wait_ge(s["d_xT"], KE * b + c + 1)
                    ac.copy(hT[:, c, :], ps[:, c, :]).then_inc(s["d_hT"], 1)
                ffn_act(b, 4, sgTs, "d")
            act.wait_ge(s["r_v"], 1)
            ac.activation(score[:, :], r_m, ACT.Exp, scale=-1.0).then_inc(s["r_exp"], 1)

            def silu(slot, j):
                act.wait_ge(s["m_gu"], slot + 1)
                ac.activation(sgs[:, j, :], ps[:, 1 + 2 * j, :], ACT.Silu).then_inc(s["m_sg"], 1)

            def xT_out(slot, j):
                act.wait_ge(s["m_xT"], slot + 3)
                ac.copy(xsT[:, j, :, :].rearrange("p c n -> p (c n)"), ps[:, 0, 0:E]).then_inc(s["m_xTe"], 1)

            xT_out(0, 0)
            with act.Fori(0, SLOTS // 2 - 1) as i:
                silu(2 * i, 0)
                xT_out(2 * i + 1, 1)
                silu(2 * i + 1, 1)
                xT_out(2 * i + 2, 0)
            silu(SLOTS - 2, 0)
            xT_out(SLOTS - 1, 1)
            silu(SLOTS - 1, 1)

        @block.vector
        def _(dve):
            v = nc.vector

            def ln_stats(n, tile0):
                for t in range(NT):
                    v.bn_stats(stats[:, t, :], x_all[:, bass.ds((tile0 + t) * E, E)]).then_inc(s["ln_stats"], 1)
                dve.wait_ge(s["ln_stats"], NT * n + NT)
                v.tensor_tensor(lsum[:, :, :], stats[:, :, 1:3], stats[:, :, 4:6], ALU.add).then_inc(s["ln_mv"], 1)
                v.tensor_tensor(ldif[:, :], stats[:, :, 1], stats[:, :, 4], ALU.subtract).then_inc(s["ln_mv"], 1)
                dve.wait_ge(s["ln_mv"], 5 * n + 2)
                v.tensor_scalar(mean[:, :], lsum[:, :, 0], 0.5, None, ALU.mult).then_inc(s["ln_mv"], 1)
                v.tensor_scalar(lvar[:, :], lsum[:, :, 1], 1.0 / E, EPS, ALU.mult, ALU.add).then_inc(s["ln_mv"], 1)
                v.scalar_tensor_tensor(out=lsq[:, :], in0=ldif[:, :], scalar=0.25, in1=ldif[:, :], op0=ALU.mult,
                                       op1=ALU.mult).then_inc(s["ln_mv"], 1)
                dve.wait_ge(s["ln_mv"], 5 * n + 5)
                v.tensor_tensor(vareps[:, :], lvar[:, :], lsq[:, :], ALU.add).then_inc(s["ln_var"], 1)

            def ln_apply(n, tile0):
                dve.wait_ge(s["ln_rstd"], n + 1)
                for t in range(NT):
                    v.tensor_scalar(xhat[:, t, :], x_all[:, bass.ds((tile0 + t) * E, E)], mean[:, t:t + 1],
                                    rstd[:, t:t + 1], ALU.subtract, ALU.mult).then_inc(s["xhat_ready"], 1)

            def x_update(b, tile, src, gate, tmp_sem, x_sem, par, k):
                v.tensor_tensor(utmp[:, par, :], src, gates_bc[:, bass.ds(gate, 1), :].rearrange("p a e -> p (a e)"),
                                ALU.mult).then_inc(tmp_sem, 1)
                dve.wait_ge(tmp_sem, k + 1)
                xt = x_all[:, bass.ds(tile * E, E)]
                v.tensor_tensor(xt, xt, utmp[:, par, :], ALU.add).then_inc(x_sem, 1)

            def ffn_dve(b, nf, gbuf, sgbuf, k, gate0, n_ln, ln_tile):
                for f in range(nf):
                    dve.wait_ge(s[k + "_sg"], nf * b + f + 1)
                    dve.wait_ge(s[k + "_u"], nf * b + f + 1)
                    v.tensor_tensor(gbuf[:, f, :], sgbuf[:, f % 2, :], ps[:, 3 + 2 * (f % 3), :], ALU.mult)\
                        .then_inc(s[k + "_gt"], 1)
                    if f == nf // 2 - 1 and ln_tile is not None:
                        ln_stats(n_ln, ln_tile)
                    if f == nf // 2 and ln_tile is not None:
                        ln_apply(n_ln, ln_tile)
                for t in range(NT):
                    dve.wait_ge(s[k + "_o"], 2 * b + t // 2 + 1)
                    x_update(b, NT * b + t, ps[:, 6 + t // 2, (t % 2) * E:(t % 2 + 1) * E], gate0 + 2 * b,
                             s[k + "_tmp"], s[k + "_x"], t % 2, NT * b + t)

            for k in "abcd":
                dve.sem_inc(s[k + "_x"], 1)
            dve.sem_inc(s["d_hc"], 1)
            dve.sem_inc(s["m_out0"], 16)
            dve.sem_inc(s["m_out1"], 16)
            dve.wait_ge(s["in_x0"], 16)
            ln_stats(0, 0)
            ln_apply(0, 0)
            dve.wait_ge(s["silu_c"], 1)
            v.tensor_copy(sc_bc.rearrange("p l c b n -> p (l c b) n"),
                          scT[:, :, :, :].rearrange("p l c b -> p (l c b)").unsqueeze(2).to_broadcast([P, 16, P]))\
                .then_inc(s["scbc_done"], 1)
            dve.wait_ge(s["modT_ps"], 1)
            v.tensor_copy(modT[:, :, :, :].rearrange("p l j b -> p (l j b)"), ps[:, 0, 0:96]).then_inc(s["modT_done"], 1)
            dve.wait_ge(s["modT_done"], 1)
            v.tensor_scalar(small[:, 0:64].rearrange("p (l j b) -> p l j b", l=2, j=8)[:, :, 0:8, :],
                            modT[:, :, 2:10, :], 1.0, None, ALU.add).then_inc(s["setup_v"], 1)
            dve.wait_ge(s["setup_v"], 1)
            plus = small[:, 0:64].rearrange("p (l j b) -> p l j b", l=2, j=8)
            v.tensor_copy(modT[:, :, 2:4, :], plus[:, :, 0:2, :]).then_inc(s["setup_v"], 1)
            v.tensor_copy(modT[:, :, 8:10, :], plus[:, :, 6:8, :]).then_inc(s["setup_v"], 1)
            dve.wait_ge(s["setup_v"], 3)
            v.sem_inc(s["modT_plus"], 1)
            for u in range(12):
                dve.wait_ge(s["bc_ps"], u + 1)
                row = 2 * u
                v.tensor_copy(gates_bc[:, row:row + 2, :].rearrange("p k e -> p (k e)"), ps[:, 1 + u % 7, :])\
                    .then_inc(s["bc_sb"], 1)
            dve.wait_ge(s["bc_sb"], 12)
            for half in range(2):
                g = gates_bc[:, 8 * half:8 * half + 8, :]
                k = 5 * half
                v.tensor_scalar(guard[0], g, 0.0, None, ALU.is_ge).then_inc(s["guard_v"], 1)
                v.tensor_scalar(guard[1], g, 0.0, None, ALU.is_lt).then_inc(s["guard_v"], 1)
                dve.wait_ge(s["guard_v"], k + 2)
                v.scalar_tensor_tensor(out=guard[2], in0=g, scalar=0.25, in1=guard[0], op0=ALU.max, op1=ALU.mult)\
                    .then_inc(s["guard_v"], 1)
                v.scalar_tensor_tensor(out=guard[3], in0=g, scalar=-0.25, in1=guard[1], op0=ALU.min, op1=ALU.mult)\
                    .then_inc(s["guard_v"], 1)
                dve.wait_ge(s["guard_v"], k + 4)
                v.tensor_tensor(g, guard[2], guard[3], ALU.add).then_inc(s["guard_v"], 1)
            v.tensor_scalar(gates_bc[:, SC1 + 1:SC1 + 8:2, :], gates_bc[:, SC1 + 1:SC1 + 8:2, :], 1.0, None, ALU.add)\
                .then_inc(s["gates_done"], 1)
            dve.wait_ge(s["guard_v"], 10)
            dve.wait_ge(s["gates_done"], 1)
            dve.wait_ge(s["in_bo"], 16)
            v.tensor_tensor(gabo, gates_bc[:, 0:8:2, :], bo_bc.unsqueeze(1).to_broadcast([P, B, E]), ALU.mult)\
                .then_inc(s["gabo_done"], 1)
            dve.wait_ge(s["gabo_done"], 1)
            dve.wait_ge(s["preset"], 3)
            dve.wait_ge(s["in_x"], 16 * (B - 1))

            with dve.Fori(0, B) as b:
                for i in range(4):
                    dve.wait_ge(s["a_p1"], 4 * b + i + 1)
                    v.tensor_tensor(resid[:, i, :], ps[:, 2 + i, :], parts[:, i, 0, :], ALU.subtract)\
                        .then_inc(s["a_r1"], 1)
                for i in range(2):
                    dve.wait_ge(s["a_v"], 2 * b + i + 1)
                    v.tensor_copy(vaug[:, 2 * i:2 * i + 2, :, 0:D0],
                                  ps[:, 6 + i, :].rearrange("p (t h d) -> p t h d", t=2, h=H0)).then_inc(s["a_vc"], 1)
                for g in range(2):
                    for u in range(16 * g, 16 * g + 16):
                        h, qt = HG * g + 2 * ((u % 16) // 4), u % 4
                        dve.wait_ge(s["a_s1"], 32 * b + u + 1)
                        v.reduce_max(rowmax[:, h:h + 2, qt], ps[:, 2 * (u % 2):2 * (u % 2) + 2, 0:(qt + 1) * P], AX_X)\
                            .then_inc(s["a_max"], 1)
                    dve.wait_ge(s["a_m1"], 2 * b + g + 1)
                    v.tensor_tensor(mres[0:32, g, :], ps[0:32, 7, 0:P], mparts[0:32, g, 0, :], ALU.subtract)\
                        .then_inc(s["a_m2"], 1)
                ln_stats(b + 1, ((b + 1) % B) * NT)
                for n in range(4):
                    if n == 1:
                        ln_apply(b + 1, ((b + 1) % B) * NT)
                    dve.wait_ge(s["a_pv"], 4 * b + n + 1)
                    v.tensor_copy(oTs[:, n % 2, :], ps[:, 6, :]).then_inc(s["a_oT"], 1)
                    dve.wait_ge(s["a_oTT"], 4 * b + n + 1)
                    tok = ps[:, 7, :].rearrange("p (t j c) -> p t j c", t=NT, j=4)
                    rd = rden[:, n % 2, :].rearrange("p (t j) -> p t j", t=NT)
                    v.reciprocal(rd, tok[:, :, :, D0]).then_inc(s["a_rc"], 1)
                    dve.wait_ge(s["a_rc"], 4 * b + n + 1)
                    v.tensor_tensor(ctx0[:, :, 4 * n * D0:4 * (n + 1) * D0].rearrange("p t (j d) -> p t j d", j=4),
                                    tok[:, :, :, 0:D0], rd.unsqueeze(3).to_broadcast([P, NT, 4, D0]), ALU.mult)\
                        .then_inc(s["a_ctx"], 1)
                dve.wait_ge(s["a_xb"], b + 1)
                for t in range(NT):
                    dve.wait_ge(s["a_o"], 2 * b + t // 2 + 1)
                    x_update(b, NT * b + t, ps[:, 6 + t // 2, (t % 2) * E:(t % 2 + 1) * E], G0 + 2 * b,
                             s["a_tmp"], s["a_x"], t % 2, NT * b + t)
            dve.wait_ge(s["a_x"], 1 + TILES)
            with dve.Fori(0, B) as b:
                ffn_dve(b, 8, gT, sgT, "b", G0 + 1, B + 1 + b, ((b + 1) % B) * NT)
            dve.wait_ge(s["b_x"], 1 + TILES)
            dve.wait_ge(s["in_small1"], 16 * 5)
            v.tensor_scalar(qscale[:, :], qscale[:, :], 8.0, None, ALU.mult).then_inc(s["setup_v"], 1)
            dve.wait_ge(s["setup_v"], 4)
            with dve.Fori(0, B) as b:
                dve.wait_ge(s["c_gp"], b + 1)
                for t in range(NT):
                    v.tensor_tensor(small[:, 8 * t:8 * t + 8], ps[:, 0, 8 * t:8 * t + 8], bg_bc[:, :], ALU.add)\
                        .then_inc(s["c_gz"], 1)
                dve.wait_ge(s["c_ge"], b + 1)
                v.tensor_scalar(small[:, 64:96], small[:, 32:64], 1.0, None, ALU.add).then_inc(s["c_g1"], 1)
                dve.wait_ge(s["c_g1"], b + 1)
                v.reciprocal(g1[:, :], small[:, 64:96]).then_inc(s["c_gate"], 1)

                def normalise(u):
                    dve.wait_ge(s["c_rk"], 2 * NT * b + u + 1)
                    if u >= 2:
                        dve.wait_ge(s["c_qT"], 2 * NT * b + u - 1)
                    v.tensor_tensor(qn[:, u % 2, :].rearrange("p (h d) -> p h d", h=H1),
                                    banks(2 + 2 * (u % 2)).rearrange("p (h d) -> p h d", h=H1),
                                    rnorm[:, u % 2, :].unsqueeze(2).to_broadcast([P, H1, D1]), ALU.mult)\
                        .then_inc(s["c_qn"], 1)

                for u in range(2 * NT):
                    dve.wait_ge(s["c_sq"], 2 * NT * b + u + 1)
                    v.reduce_sum(ssq[:, u % 2, :], sq[:, u % 2, :].rearrange("p (h d) -> p h d", h=H1), AX_X)\
                        .then_inc(s["c_ss"], 1)
                    if u >= 1:
                        normalise(u - 1)
                    dve.wait_ge(s["c_ss"], 2 * NT * b + u + 1)
                    v.tensor_scalar(ssq[:, u % 2, :], ssq[:, u % 2, :], 1e-24, None, ALU.max)\
                        .then_inc(s["c_rk0"], 1)
                normalise(2 * NT - 1)
                for i in range(2 * NT + 3):
                    if i < 2 * NT:
                        c0 = P if i < 2 else WIN
                        dve.wait_ge(s["c_s"], 2 * NT * b + i + 1)
                        v.reduce_max(nmax1[:, i % 2, :],
                                     banks(2 * (i % 2)).rearrange("p (h n) -> p h n", h=4)[:, :, c0:], AX_X,
                                     negate=True).then_inc(s["c_mx"], 1)
                    if 1 <= i <= 2 * NT:
                        w = i - 1
                        k0 = 1 if w < 2 else 0
                        dve.wait_ge(s["c_e"], 8 * NT * b + 4 * w + 4)
                        v.reciprocal(rinv1[:, w % 2, :], rsum1[:, w % 2, :]).then_inc(s["c_ri"], 1)
                        dve.wait_ge(s["c_ri"], 2 * NT * b + w + 1)
                        t, hg = w // 2, w % 2
                        w0c = P if t == 0 else WIN
                        for hh in range(4):
                            g = g1[:, t * H1 + 4 * hg + hh:t * H1 + 4 * hg + hh + 1]
                            v.tensor_scalar(pr1[:, w % 2, hh, w0c:], pr1[:, w % 2, hh, w0c:],
                                            rinv1[:, w % 2, hh:hh + 1], g, ALU.mult, ALU.mult).then_inc(s["c_pn"], 1)
                        dve.wait_ge(s["c_pT"], 2 * NT * b + w + 1)
                        v.tensor_copy(pT1[:, w % 2, :, k0:, :],
                                      banks(4).rearrange("p (h k n) -> p h k n", h=4, k=2)[:, :, k0:, :])\
                            .then_inc(s["c_pTe"], 1)
                    if i >= 4 and i % 2 == 0:
                        t = i // 2 - 2
                        dve.wait_ge(s["c_w"], NT * b + t + 1)
                        x_update(b, NT * b + t, ps[:, 7, 0:E], G1 + 2 * b, s["c_tmp"], s["c_x"], t % 2, NT * b + t)
                    if i == 5:
                        ln_stats(2 * B + 1 + b, ((b + 1) % B) * NT)
                    if i == 6:
                        ln_apply(2 * B + 1 + b, ((b + 1) % B) * NT)
            dve.wait_ge(s["c_x"], 1 + TILES)

            def shared(b, ln_tile):
                dve.wait_ge(s["xhat_ready"], 3 * NT * B + NT * b + NT)
                dve.wait_ge(s["d_hc"], 1 + b)
                row = SC1 + 2 * b
                v.tensor_tensor(hs, xhat[:, :, :], gates_bc[:, bass.ds(row + 1, 1), :].to_broadcast([P, NT, E]),
                                ALU.mult).then_inc(s["d_h0"], 1)
                dve.wait_ge(s["d_h0"], b + 1)
                v.tensor_tensor(hs, hs, gates_bc[:, bass.ds(row, 1), :].to_broadcast([P, NT, E]), ALU.add)\
                    .then_inc(s["d_h"], 1)
                dve.wait_ge(s["d_l"], b + 1)
                v.tensor_copy(logits[:, bass.ds(b * (NT * NEXP), NT * NEXP)], ps[:, 0, 0:NT * NEXP])\
                    .then_inc(s["d_lc"], 1)
                ffn_dve(b, 4, gTs, sgTs, "d", G1 + 1, 3 * B + 1 + b, ln_tile)

            with dve.Fori(0, B - 1) as b:
                shared(b, (b + 1) * NT)
            shared(B - 1, None)

            dve.wait_ge(s["d_lc"], B)
            dve.wait_ge(s["d_x"], 1 + TILES)
            dve.wait_ge(s["in_rt"], 16 * 4)
            step = [0]

            def then(ins):
                step[0] += 1
                ins.then_inc(s["r_v"], 1)
                dve.wait_ge(s["r_v"], step[0])

            lg = logits[:, :].rearrange("p (t e) -> p t e", e=NEXP)

            def over_e(a, n=TILES):
                return a.unsqueeze(2).to_broadcast([P, n, NEXP])

            def over_t(a, n=TILES):
                return a.unsqueeze(1).to_broadcast([P, n, NEXP])

            then(v.reduce_max(r_m, lg, AX_X))
            then(v.tensor_tensor(r_eq, lg, over_e(r_m), ALU.is_equal))
            then(v.tensor_tensor(r_eq, r_eq, r_w8, ALU.mult))
            then(v.reduce_max(r_pos, r_eq, AX_X))
            then(v.tensor_tensor(r_oh, r_eq, over_e(r_pos), ALU.is_equal))
            then(v.memset(r_ohx[:, TILES, :], 0.0))
            then(v.tensor_copy(r_ohx[:, 0:TILES, :], r_oh))
            dve.wait_ge(s["r_R"], 1)
            rank = ps[:, 0, 0:(TILES + 1) * NEXP].rearrange("p (t e) -> p t e", e=NEXP)
            then(v.tensor_copy(r_n, rank[:, TILES, :]))
            a128 = r_a[:, 0:128].rearrange("p (e j) -> p e j", e=NEXP)
            then(v.tensor_tensor(a128, r_n.unsqueeze(2).to_broadcast([P, NEXP, TILES]), r_thr, ALU.is_gt))
            then(v.reduce_sum(r_nt, a128, AX_X))
            a64 = r_a[:, 0:64].rearrange("p (e j) -> p e j", e=NEXP)
            then(v.tensor_tensor(a64, over_t(r_nt, NEXP), r_incl, ALU.mult))
            then(v.reduce_sum(r_end, a64, AX_X))
            then(v.tensor_tensor(r_base, r_end, r_nt, ALU.subtract))
            then(v.tensor_scalar(r_base, r_base, float(P), None, ALU.mult))
            then(v.tensor_tensor(r_eq, rank[:, 0:TILES, :], over_t(r_base), ALU.add))
            then(v.tensor_tensor(r_eq, r_eq, r_oh, ALU.mult))
            then(v.reduce_sum(r_pos, r_eq, AX_X))
            then(v.tensor_copy(pos_i[:, :], r_pos))
            a192 = r_a[:, 0:SLOTS * NEXP].rearrange("p (s e) -> p s e", e=NEXP)
            then(v.tensor_tensor(a192, r_iota, over_t(r_end, SLOTS), ALU.is_ge))
            then(v.reduce_sum(r_f, a192, AX_X))
            then(v.tensor_scalar(r_f, r_f, float(NEXP - 1), None, ALU.min))
            then(v.tensor_copy(slot_e[:, :], r_f))
            dve.wait_ge(s["r_exp"], 1)
            then(v.tensor_scalar(score[:, :], score[:, :], 1.0, None, ALU.add))
            then(v.reciprocal(score[:, :], score[:, :]))
            v.sem_inc(s["r_pos_ok"], 1)
            dve.wait_ge(s["d_hc"], 1 + B)
            for t in range(TILES):
                ht = h_all[:, t * E:(t + 1) * E]
                v.tensor_scalar(ht, ht, score[:, t:t + 1], None, ALU.mult).then_inc(s["r_xr"], 1)

            dve.wait_ge(s["r_xr"], TILES)

            def slot_dve(slot, j, i):
                dve.wait_ge(s["m_sg"], slot + 1)
                v.tensor_tensor(acts[:, j, :], sgs[:, j, :], ps[:, 2 + 2 * j, :], ALU.mult).then_inc(s["m_a"], 1)
                dve.wait_ge(s["m_aT"], slot + 1)
                v.tensor_copy(actT[:, j, :, :].rearrange("p f n -> p (f n)"), ps[:, 5, :]).then_inc(s["m_aTe"], 1)
                dve.wait_ge(s["m_d"], slot + 1)
                dve.wait_ge(s[f"m_out{j}"], 16 * i + 16)
                v.tensor_copy(ys[:, j, :], ps[:, 6 + j, 0:E]).then_inc(s["m_y"], 1)

            with dve.Fori(0, SLOTS // 2) as i:
                slot_dve(2 * i, 0, i)
                slot_dve(2 * i + 1, 1, i)
            for t in range(TILES):
                b = t // NT
                dve.wait_ge(s["m_gather"], 16 * TILES)
                x_update(b, t, yg[:, t, :], G1 + 1 + 2 * b, s["f_tmp"], s["f_x"], t % 2, t)

        @block.tensor
        def _(pe):
            mm, tr = nc.tensor.matmul, nc.tensor.transpose

            def xhat_T(b, n, src, xT_sem):
                for c in range(KE):
                    for t in range(NT):
                        last = tr(ps[:, c, t * P:(t + 1) * P], src[:, t, c * P:(c + 1) * P], ident[:, :])
                    last.then_inc(xT_sem, 1)

            def ffn_pe(b, nf, gw, uw, dw, gbuf, k):
                for f in range(nf):
                    if f >= 3:
                        pe.wait_ge(s[k + "_gt"], nf * b + f - 2)
                    if f == 2:
                        pe.wait_ge(s[k + "_x"], NT * b + 1)
                    for w, off, done in ((gw, 2, "_g"), (uw, 3, "_u")):
                        for c in range(KE):
                            last = mm(ps[:, off + 2 * (f % 3), :], w[:, c, f * P:(f + 1) * P], hT[:, c, :],
                                      start=(c == 0), stop=(c == KE - 1))
                        last.then_inc(s[k + done], 1)
                pe.wait_ge(s[k + "_gt"], nf * b + nf)
                for t in range(NT):
                    for f in range(nf):
                        last = mm(ps[:, 6 + t // 2, (t % 2) * E:(t % 2 + 1) * E], gbuf[:, f, t * P:(t + 1) * P],
                                  dw[:, f, :], start=(f == 0), stop=(f == nf - 1))
                    if t % 2 == 1:
                        last.then_inc(s[k + "_o"], 1)

            pe.wait_ge(s["in_mod"], 32)
            pe.wait_ge(s["silu_c"], 1)
            for layer in range(2):
                for j in range(12):
                    for c in range(KE):
                        at = (layer * 12 + j) * B
                        last = mm(ps[:, 0, at:at + B], wmod[layer][:, c, j * P:(j + 1) * P], scT[:, layer, c, :],
                                  start=(c == 0), stop=(c == KE - 1))
            last.then_inc(s["modT_ps"], 1)
            pe.wait_ge(s["scbc_done"], 1)
            jobs = [(0, b, (2, 5)) for b in range(B)] + [(1, b, (2, 5)) for b in range(B)]
            jobs += [(1, b, (3, 4)) for b in range(B)]
            for u, (layer, b, kinds) in enumerate(jobs):
                if u >= 7:
                    pe.wait_ge(s["bc_sb"], u - 6)
                for i, kind in enumerate(kinds):
                    lo, hi = mod_cols(kind)
                    for c in range(KE):
                        last = mm(ps[:, 1 + u % 7, i * E:(i + 1) * E], sc_bc[:, layer, c, b, :],
                                  wmod[layer][:, c, lo:hi], start=(c == 0), stop=(c == KE - 1))
                last.then_inc(s["bc_ps"], 1)
            pe.wait_ge(s["modT_done"], 1)
            pe.wait_ge(s["bc_sb"], 12)
            pe.wait_ge(s["in_const"], 16 * 6)
            pe.wait_ge(s["in_wqkv"], 48)
            pe.wait_ge(s["in_wo0"], 16)
            pe.wait_ge(s["in_kaug"], 16)
            pe.wait_ge(s["preset"], 3)
            pe.wait_ge(s["pre_pool"], 2)

            with pe.Fori(0, B) as b:
                pe.wait_ge(s["xhat_ready"], NT * b + NT)
                xhat_T(b, b, xhat, s["a_xT"])
                pe.wait_ge(s["a_h"], KE * b + KE)
                for i in range(4):
                    for c in range(KE):
                        last = mm(ps[:, 2 + i, :], w0[i % 2][:, c, (i // 2) * P:(i // 2 + 1) * P], hT[:, c, :],
                                  start=(c == 0), stop=(c == KE - 1))
                    last.then_inc(s["a_qk"], 1)
                pe.wait_ge(s["a_x"], NT * b + 1)
                for t in range(NT):
                    for c in range(KE):
                        last = mm(ps[:, 6 + t // 2, (t % 2) * E:(t % 2 + 1) * E], hT[:, c, t * P:(t + 1) * P],
                                  w0[2][:, c, :], start=(c == 0), stop=(c == KE - 1))
                    if t % 2 == 1:
                        last.then_inc(s["a_v"], 1)
                for g in range(2):
                    pe.wait_ge(s[f"a_stack{g}"], (16 * 12) * b + 16 * 12)
                    if g == 0:
                        pe.wait_ge(s["a_r1"], 4 * b + 2)
                    for u in range(16 * g, 16 * g + 16):
                        h0, qt = HG * g + 2 * ((u % 16) // 4), u % 4
                        if u >= 2:
                            pe.wait_ge(s["a_max"], 32 * b + u - 1)
                        for h in (h0, h0 + 1):
                            bank = 2 * (u % 2) + h - h0
                            mm(ps[:, bank, 0:(qt + 1) * P], qst[0:MAX_ROW, h, qt * P:(qt + 1) * P],
                               kst[0:MAX_ROW, h, 0:(qt + 1) * P], start=True, stop=False)
                            last = mm(ps[:, bank, qt * P:(qt + 1) * P], identb[:, :], maskq[:, :],
                                      start=False, stop=True)
                        last.then_inc(s["a_s1"], 1)
                    pe.wait_ge(s["a_max"], 32 * b + 16 * g + 16)
                    if g == 0:
                        pe.wait_ge(s["a_vc"], 2 * b + 2)
                    else:
                        pe.wait_ge(s["a_m2"], 2 * b + 1)
                    tr(ps[0:32, 7, 0:P], rowmax[:, HG * g:HG * g + HG, :].rearrange("p h t -> p (h t)"), ident[:, :])\
                        .then_inc(s["a_mT"], 1)

                def pv(n):
                    pe.wait_ge(s["a_exp"], H0 * b + 4 * n + 4)
                    if n >= 1:
                        pe.wait_ge(s["a_oT"], 4 * b + n)
                    for kt in range(NT):
                        for j in range(4):
                            h = 4 * n + j
                            last = mm(ps[32 * j:32 * j + 32, 6, kt * P:S], vaug[:, kt, h, :],
                                      probs[:, h % 8, KM_OFF[kt]:KM_OFF[kt] + KM_W[kt]],
                                      start=(kt == 0), stop=(kt == NT - 1))
                    last.then_inc(s["a_pv"], 1)

                def turn(n):
                    pe.wait_ge(s["a_oT"], 4 * b + n + 1)
                    if n >= 1:
                        pe.wait_ge(s["a_ctx"], 4 * b + n)
                    else:
                        pe.wait_ge(s["a_m2"], 2 * b + 2)
                    for t in range(NT):
                        last = tr(ps[:, 7, t * P:(t + 1) * P], oTs[:, n % 2, t * P:(t + 1) * P], ident[:, :])
                    last.then_inc(s["a_oTT"], 1)

                for h in range(H0):
                    if h >= 2:
                        pe.wait_ge(s["a_exp"], H0 * b + h - 1)
                    if h % HG == 0:
                        pe.wait_ge(s[f"a_mrow{h // HG}"], 48 * b + 48)
                    sc = banks(3 * (h % 2), 3)
                    for kt in (0, 1, 3, 2):
                        at = KM_OFF[kt]
                        mm(sc[:, at:at + KM_W[kt]], kst[0:STACK, h, kt * P:(kt + 1) * P], qst[0:STACK, h, kt * P:S],
                           start=True, stop=False)
                        last = mm(sc[:, at:at + P], identb[:, :], maskk[:, :], start=False, stop=True)
                    last.then_inc(s["a_s2"], 1)
                    if h % 4 == 1 and h > 1:
                        if h > 5:
                            turn(h // 4 - 2)
                        pv(h // 4 - 1)
                turn(2)
                pv(3)
                turn(3)
                pe.wait_ge(s["a_ctx"], 4 * b + 4)
                xhat_T(b, 0, ctx0, s["a_cT"])
                pe.wait_ge(s["a_cTe"], KE * b + KE)
                for t in range(NT):
                    for c in range(KE):
                        last = mm(ps[:, 6 + t // 2, (t % 2) * E:(t % 2 + 1) * E], ctxT[:, c, t * P:(t + 1) * P],
                                  w0[3][:, c, :], start=(c == 0), stop=(c == KE - 1))
                    if t % 2 == 1:
                        last.then_inc(s["a_o"], 1)

            pe.wait_ge(s["in_ffn"], 48)
            pe.wait_ge(s["a_x"], 1 + TILES)
            with pe.Fori(0, B) as b:
                pe.wait_ge(s["xhat_ready"], NT * B + NT * b + NT)
                xhat_T(b, B + b, xhat, s["b_xT"])
                pe.wait_ge(s["b_h"], KE * b + KE)
                ffn_pe(b, 8, wgate, wup, wdown, gT, "b")

            pe.wait_ge(s["in_w1"], 48)
            pe.wait_ge(s["in_small1"], 16 * 5)
            pe.wait_ge(s["b_x"], 1 + TILES)
            pe.wait_ge(s["preset"], 5)
            with pe.Fori(0, B) as b:
                pe.wait_ge(s["xhat_ready"], 2 * NT * B + NT * b + NT)
                xhat_T(b, 2 * B + b, xhat, s["c_xT"])
                pe.wait_ge(s["c_h"], KE * b + KE)
                for t in range(NT):
                    for c in range(KE):
                        last = mm(ps[:, 0, H1 * t:H1 * t + H1], hT[:, c, t * P:(t + 1) * P], wg1[:, c, :],
                                  start=(c == 0), stop=(c == KE - 1))
                last.then_inc(s["c_gp"], 1)

                def project(bank, w, col, t):
                    for half in range(2):
                        for c in range(KE):
                            last = mm(ps[:, bank + half, :], hT[:, c, t * P:(t + 1) * P],
                                      w[:, c, col + half * 512:col + half * 512 + 512],
                                      start=(c == 0), stop=(c == KE - 1))
                    return last

                def qk_T(u):
                    pe.wait_ge(s["c_qn"], 2 * NT * b + u + 1)
                    if u >= 1:
                        pe.wait_ge(s["c_qe"], 2 * NT * b + u)
                    else:
                        pe.wait_ge(s["c_x"], NT * b + 1)
                    for h in range(H1):
                        last = tr(ps[:, 6 + h // 4, (h % 4) * P:(h % 4 + 1) * P], qn[:, u % 2, h * P:(h + 1) * P],
                                  ident[:, :])
                    last.then_inc(s["c_qT"], 1)

                for t in range(NT):
                    for u, w, col in ((2 * t, wq1, 0), (2 * t + 1, wkv1, 0)):
                        if u >= 2:
                            pe.wait_ge(s["c_qn"], 2 * NT * b + u - 1)
                        project(2 + 2 * (u % 2), w, col, t).then_inc(s["c_p"], 1)
                        if u >= 2:
                            qk_T(u - 2)
                    if t == 0:
                        pe.wait_ge(s["c_gz"], NT * b + NT)
                    else:
                        pe.wait_ge(s["c_ve"], NT * b + t)
                    project(0, wkv1, INNER, t).then_inc(s["c_v"], 1)
                qk_T(2 * NT - 2)
                qk_T(2 * NT - 1)

                pe.wait_ge(s["c_ve"], NT * b + NT)
                for i in range(2 * NT + 3):
                    if i < 2 * NT:
                        t, hg = i // 2, i % 2
                        c0 = P if t == 0 else WIN
                        if i == 0:
                            pe.wait_ge(s["c_qe"], 2 * NT * b + 2 * NT)
                        if i >= 2:
                            pe.wait_ge(s["c_e"], 8 * NT * b + 4 * (i - 1))
                        sc4 = banks(2 * (i % 2)).rearrange("p (h n) -> p h n", h=4)
                        for hh in range(4):
                            h = 4 * hg + hh
                            mm(sc4[:, hh, c0:], qT1[:, h, t * P:(t + 1) * P], kT1[:, h, t * P - (P - c0):(t + 1) * P],
                               start=True, stop=False)
                            last = mm(sc4[:, hh, c0:], identb[:, :], maskw[:, c0 - WIN:], start=False, stop=True)
                        last.then_inc(s["c_s"], 1)
                    if 1 <= i <= 2 * NT:
                        w = i - 1
                        k0 = 1 if w < 2 else 0
                        pe.wait_ge(s["c_pn"], 8 * NT * b + 4 * w + 4)
                        if w >= 1:
                            pe.wait_ge(s["c_pTe"], 2 * NT * b + w)
                        for hh in range(4):
                            for k in range(k0, 2):
                                last = tr(banks(4)[:, (2 * hh + k) * P:(2 * hh + k + 1) * P],
                                          pr1[:, w % 2, hh, k * P:(k + 1) * P], ident[:, :])
                        last.then_inc(s["c_pT"], 1)
                    if 2 <= i <= 2 * NT + 1:
                        w = i - 2
                        t, hg = w // 2, w % 2
                        k0 = 1 if t == 0 else 0
                        pe.wait_ge(s["c_pTe"], 2 * NT * b + w + 1)
                        if w >= 1:
                            pe.wait_ge(s["c_oe"], 2 * NT * b + w)
                        for hh in range(4):
                            h = 4 * hg + hh
                            for k in range(k0, 2):
                                last = mm(ps[:, 6, hh * P:(hh + 1) * P], v1[:, t - 1 + k, h * P:(h + 1) * P],
                                          pT1[:, w % 2, hh, k, :], start=(k == k0), stop=(k == 1))
                        last.then_inc(s["c_o"], 1)
                    if i >= 4 and i % 2 == 0:
                        t = i // 2 - 2
                        pe.wait_ge(s["c_oe"], 2 * NT * b + 2 * t + 2)
                        pe.wait_ge(s["c_x"], NT * b + t + 1)
                        for h in range(H1):
                            last = mm(ps[:, 7, 0:E], oT1[:, t % 2, h, :], wo1[:, h, :],
                                      start=(h == 0), stop=(h == H1 - 1))
                        last.then_inc(s["c_w"], 1)

            pe.wait_ge(s["in_sh"], 48)
            pe.wait_ge(s["c_x"], 1 + TILES)
            with pe.Fori(0, B) as b:
                pe.wait_ge(s["d_h"], b + 1)
                xhat_T(b, 0, hs, s["d_xT"])
                pe.wait_ge(s["d_hT"], KE * b + KE)
                for t in range(NT):
                    for c in range(KE):
                        last = mm(ps[:, 0, NEXP * t:NEXP * t + NEXP], hT[:, c, t * P:(t + 1) * P], router[:, c, :],
                                  start=(c == 0), stop=(c == KE - 1))
                last.then_inc(s["d_l"], 1)
                ffn_pe(b, 4, shg, shu, shd, gTs, "d")
                pe.wait_ge(s["d_lc"], b + 1)
            pe.wait_ge(s["r_v"], 7)
            last = mm(ps[:, 0, 0:(TILES + 1) * NEXP], before[:, :], r_ohx.rearrange("p t e -> p (t e)"),
                      start=True, stop=False)
            for t in range(TILES):
                n = TILES - t
                last = mm(ps[:, 0, (t + 1) * NEXP:(TILES + 1) * NEXP].rearrange("p (t e) -> p t e", e=NEXP),
                          ones_b[:, :], r_ohx[:, t:t + 1, :].to_broadcast([P, n, NEXP]),
                          start=False, stop=(t == TILES - 1))
            last.then_inc(s["r_R"], 1)

            pe.sem_inc(s["m_xT"], 2)
            pe.wait_ge(s["in_exp"], 16 * 2 * NEXP)
            pe.wait_ge(s["r_pos_ok"], 1)

            def slot_T(slot, j, i):
                pe.wait_ge(s[f"m_in{j}"], 16 * i + 16)
                for c in range(KE):
                    last = tr(ps[:, 0, c * P:(c + 1) * P], xs[:, j, c * P:(c + 1) * P], ident[:, :])
                last.then_inc(s["m_xT"], 1)

            def expert_of(slot):
                return pe.value_load(slot_e[0:1, bass.ds(slot, 1)], min_val=0, max_val=NEXP - 1)

            def slot_gu(slot, j):
                e = expert_of(slot)
                pe.wait_ge(s["m_xTe"], slot + 1)
                for half in range(2):
                    for c in range(KE):
                        last = mm(ps[:, 1 + 2 * j + half, :], xsT[:, j, c, :],
                                  wgu[:, c, bass.ds(e * (2 * FE) + half * FE, FE)],
                                  start=(c == 0), stop=(c == KE - 1))
                last.then_inc(s["m_gu"], 1)

            def slot_down(slot, j):
                e = expert_of(slot)
                pe.wait_ge(s["m_a"], slot + 1)
                for f in range(4):
                    last = tr(ps[:, 5, f * P:(f + 1) * P], acts[:, j, f * P:(f + 1) * P], ident[:, :])
                last.then_inc(s["m_aT"], 1)
                pe.wait_ge(s["m_aTe"], slot + 1)
                for f in range(4):
                    last = mm(ps[:, 6 + j, 0:E], actT[:, j, f, :], wdn[:, f, bass.ds(e * E, E)],
                              start=(f == 0), stop=(f == 3))
                last.then_inc(s["m_d"], 1)

            slot_T(0, 0, 0)
            slot_gu(0, 0)
            slot_T(1, 1, 0)
            with pe.Fori(0, SLOTS // 2 - 1) as i:
                slot_gu(2 * i + 1, 1)
                slot_T(2 * i + 2, 0, i + 1)
                slot_down(2 * i, 0)
                slot_gu(2 * i + 2, 0)
                slot_T(2 * i + 3, 1, i + 1)
                slot_down(2 * i + 1, 1)
            slot_gu(SLOTS - 1, 1)
            slot_down(SLOTS - 2, 0)
            slot_down(SLOTS - 1, 1)


def _bf16_bits(v):
    import numpy as np
    return (np.ascontiguousarray(v, dtype=np.float32).view(np.uint32) >> 16).astype(np.uint16)


def _alibi_rows():
    import numpy as np
    slopes = (2.0 ** (-8.0 * np.arange(1, H0 + 1) / H0)).astype(np.float32)
    left = slopes[:, None] * np.arange(S, dtype=np.float32)[None, :]
    rows = np.full((STACK - BIAS_ROW, H0, S), -1.0, dtype=np.float32)
    for a in range(3):
        rows[a] = (left.view(np.uint32) & np.uint32(0xFFFF0000)).view(np.float32)
        left = left - rows[a]
    return _bf16_bits(rows)


def _constants():
    import numpy as np
    i, j = np.arange(P)[:, None], np.arange(P)[None, :]
    far = np.float32(-1e30)
    jw = np.arange(-WIN, P)[None, :]
    cond = {
        "maskq": np.where(j <= i, 0, far),
        "maskk": np.where(i <= j, 0, far),
        "maskw": np.where((i - jw >= 0) & (i - jw <= WIN), 0, far),
        "before": np.where(i < j, 1, 0),
        "identb": np.eye(P),
    }
    c = {k: _bf16_bits(v) for k, v in cond.items()}
    c["ident"] = np.eye(P, dtype=np.float32)
    c["kaug"] = _alibi_rows()

    def rows(a):
        return np.ascontiguousarray(np.broadcast_to(a.astype(np.float32)[None], (P,) + a.shape))

    c["thr"] = rows(np.broadcast_to(P * np.arange(TILES), (NEXP, TILES)))
    c["iota"] = rows(np.broadcast_to(np.arange(SLOTS)[:, None], (SLOTS, NEXP)))
    c["incl"] = rows(np.tril(np.ones((NEXP, NEXP))))
    c["w8"] = rows(np.broadcast_to(NEXP - np.arange(NEXP), (TILES, NEXP)))
    return c


def kernel(**inputs):
    import numpy as np
    import concourse.bacc as bacc
    from concourse.bass_utils import run_bass_kernel_spmd

    a = {k: np.asarray(v) for k, v in inputs.items()}
    c = _constants()

    def by_dim(w):
        return w.reshape(E, 2, HG, D0).transpose(0, 1, 3, 2).reshape(E, E)

    def per_partition(v):
        return np.broadcast_to(v[None, :], (P, v.shape[0]))

    cT = np.stack([a["L0_c"].T.reshape(KE, P, B), a["L1_c"].T.reshape(KE, P, B)]).transpose(2, 0, 1, 3)
    arrays = [
        ("x", a["L0_attn_x"]), ("cT", cT), ("wmod0", a["L0_wmod"]), ("wmod1", a["L1_wmod"]),
        ("wq0", by_dim(a["L0_attn_Wq"])), ("wk0", by_dim(a["L0_attn_Wk"])), ("wv0", a["L0_attn_Wv"]),
        ("wo0", a["L0_attn_Wo"]), ("bo", per_partition(a["L0_attn_bo"])),
        ("wgate", a["L0_ffn_w_gate"].T), ("wup", a["L0_ffn_w_up"].T), ("wdown", a["L0_ffn_w_down"].T),
        ("wq1", a["L1_attn_Wq"].T), ("wkv1", a["L1_attn_Wkv"].T),
        ("qs", a["L1_attn_q_scale"][:, None]), ("ks", a["L1_attn_k_scale"][:, None]),
        ("wg1", a["L1_attn_Wg"].T), ("bg", per_partition(a["L1_attn_bg"])), ("wo1", a["L1_attn_Wo"].T),
        ("router", a["L1_ffn_router_w"].T), ("gu", a["L1_ffn_gate_up_proj"]), ("dn", a["L1_ffn_down_proj"]),
        ("sg", a["L1_ffn_shared_gate_w"]), ("su", a["L1_ffn_shared_up_w"]), ("sd", a["L1_ffn_shared_down_w"]),
        ("ident", c["ident"]), ("identb", c["identb"]), ("maskq", c["maskq"]), ("maskk", c["maskk"]),
        ("maskw", c["maskw"]), ("before", c["before"]), ("kaug", c["kaug"]), ("thr", c["thr"]),
        ("iota", c["iota"]), ("incl", c["incl"]), ("w8", c["w8"]),
    ]
    nc = bacc.Bacc("TRN2", target_bir_lowering=False, num_devices=1)
    feeds, aps = {}, []
    for name, v in arrays:
        v = np.ascontiguousarray(v)
        feeds[f"in_{name}"] = v
        aps.append(nc.dram_tensor(f"in_{name}", v.shape, mybir.dt.from_np(v.dtype), kind="ExternalInput").ap())
    out = nc.dram_tensor("out_x", (B, S, E), F32, kind="ExternalOutput").ap()
    program(nc, *aps, out)
    r = run_bass_kernel_spmd(nc, [feeds], core_ids=[0])
    return r.results[0]["out_x"]
```

```python
from contextlib import ExitStack

import concourse.bass as bass
from concourse import mybir

ALU = mybir.AluOpType
ACT = mybir.ActivationFunctionType
AX_X = mybir.AxisListType.X
F32 = mybir.dt.float32
BF16 = mybir.dt.bfloat16
I32 = mybir.dt.int32

P = 128
B, S, E = 4, 512, 256
NT = S // P
TILES = B * NT
KE = E // P
H0, D0 = 16, 16
HG = H0 // 2
F0 = 1024
H1, D1 = 8, 128
INNER = H1 * D1
WIN = 64
NEXP, FE = 8, 512
SLOTS = TILES + NEXP - 1
SLOT_PAIRS = (SLOTS - 3) // 2
EPS = 1e-5

Q_PARTS = [0, 0, 1, 1, 0, 2]
K_PARTS = [0, 1, 0, 1, 2, 0]
BIAS_ROW = 16 * len(Q_PARTS)
MAX_ROW = BIAS_ROW + 3
STACK = MAX_ROW + 3

KM_W = [S - P * kt for kt in range(NT)]
KM_OFF = [0, 512, 1024, 896]
KM = sum(KM_W)


def program(nc, x_d, cT_d, wmod0_d, wmod1_d, wq0_d, wk0_d, wv0_d, wo0_d, bo_d, wgate_d, wup_d, wdown_d,
            wq1_d, wkv1_d, qs_d, ks_d, wg1_d, bg_d, wo1_d, router_d, gu_d, dn_d, sg_d, su_d, sd_d,
            ident_d, identb_d, maskq_d, maskk_d, maskw_d, before_d, kaug_d, thr_d, iota_d, incl_d, w8_d, out_d):
    rows_d = nc.dram_tensor("routed_rows", (SLOTS * P, E), F32).ap()
    yrows_d = nc.dram_tensor("routed_out", (SLOTS * P, E), F32).ap()

    with ExitStack() as ctx:
        def sb(name, shape, dt=F32):
            return ctx.enter_context(nc.sbuf_tensor(name, shape, dt))

        def sem(name):
            return ctx.enter_context(nc.semaphore(name))

        x_all = sb("x_all", [P, TILES * E])
        xhat = sb("xhat", [P, NT, E])
        hT = sb("hT", [P, KE, S])
        gates_bc = sb("gates_bc", [P, 24, E])
        modT = sb("modT", [P, 2, 12, B])
        ident = sb("ident", [P, P])
        identb = sb("identb", [P, P], BF16)
        maskq = sb("maskq", [P, P], BF16)
        maskk = sb("maskk", [P, P], BF16)
        maskw = sb("maskw", [P, WIN + P], BF16)
        before = sb("before", [P, P], BF16)
        ones_b = sb("ones_b", [P, P], BF16)
        stats = sb("stats", [P, NT, 6])
        lsum = sb("lsum", [P, NT, 2])
        ldif = sb("ldif", [P, NT])
        lvar = sb("lvar", [P, NT])
        lsq = sb("lsq", [P, NT])
        mean = sb("mean", [P, NT])
        vareps = sb("vareps", [P, NT])
        rstd = sb("rstd", [P, NT])
        minus_half = sb("minus_half", [P, 8])
        qscale = sb("qscale", [P, 1])
        kscale = sb("kscale", [P, 1])
        scT = sb("scT", [P, 2, KE, B])
        cT = sb("cT", [P, 2, KE, B])
        small = sb("small", [P, 256])

        AR = 30720
        arena = sb("arena", [P, AR])

        def ar(off, n):
            return arena[:, off:off + n]

        o = 0
        qst = ar(o, 4096).bitcast(BF16).rearrange("p (h n) -> p h n", h=H0); o += 4096
        kst = ar(o, 4096).bitcast(BF16).rearrange("p (h n) -> p h n", h=H0); o += 4096
        parts = ar(o, 3072).bitcast(BF16).rearrange("p (i a n) -> p i a n", i=4, a=3); o += 3072
        resid = ar(o, 2048).rearrange("p (i n) -> p i n", i=4); o += 2048
        vaug = ar(o, 2048).rearrange("p (t h c) -> p t h c", t=NT, h=H0); o += 2048
        probs = ar(o, 8 * KM).rearrange("p (h n) -> p h n", h=8); o += 8 * KM
        ctx0 = ar(o, 1024).rearrange("p (t e) -> p t e", t=NT); o += 1024
        ctxT = ar(o, 1024).rearrange("p (c n) -> p c n", c=KE); o += 1024
        oTs = ar(o, 1024).rearrange("p (i n) -> p i n", i=2); o += 1024
        gabo = ar(o, 1024).rearrange("p (b e) -> p b e", b=B); o += 1024
        rowmax = ar(o, 64).rearrange("p (h t) -> p h t", h=H0); o += 64
        rden = ar(o, 32).rearrange("p (i n) -> p i n", i=2); o += 32
        mres = ar(o, 256).rearrange("p (g n) -> p g n", g=2); o += 256
        mparts = ar(o, 384).bitcast(BF16).rearrange("p (g a n) -> p g a n", g=2, a=3); o += 384
        assert o <= AR
        zero_rows = ar(AR - 256, 256)
        assert o <= AR - 256
        bo_bc = ctxT[:, 0, 0:256]
        wmod = [ar(15360 + 3072 * i, 3072).rearrange("p (c n) -> p c n", c=KE) for i in range(2)]
        sc_bc = ar(21504, 2048).rearrange("p (l c b n) -> p l c b n", l=2, c=KE, b=B)
        guard = [oTs[:, 0, :], oTs[:, 1, :]], [ctx0[:, 0:2, :].rearrange("p t e -> p (t e)"),
                                               ctx0[:, 2:4, :].rearrange("p t e -> p (t e)")]
        gT = ar(15360, 4096).rearrange("p (f n) -> p f n", f=8)
        sgT = ar(19456, 1024).rearrange("p (i n) -> p i n", i=2)
        utmp = sb("utmp", [P, 2, E])
        o = 0
        qT1 = ar(o, 4096).rearrange("p (h n) -> p h n", h=H1); o += 4096
        kT1 = ar(o, 4096).rearrange("p (h n) -> p h n", h=H1); o += 4096
        v1 = ar(o, 4096).rearrange("p (t n) -> p t n", t=NT); o += 4096
        qn = ar(o, 2048).rearrange("p (i n) -> p i n", i=2); o += 2048
        sq = ar(o, 2048).rearrange("p (i n) -> p i n", i=2); o += 2048
        pr1 = ar(o, 2048).rearrange("p (i h n) -> p i h n", i=2, h=4); o += 2048
        pT1 = ar(o, 2048).rearrange("p (i h k n) -> p i h k n", i=2, h=4, k=2); o += 2048
        oT1 = ar(o, 2048).rearrange("p (i h n) -> p i h n", i=2, h=H1); o += 2048
        W1 = o
        assert W1 + 8192 <= AR
        wq1 = ar(W1, 2048).rearrange("p (c n) -> p c n", c=KE)
        wkv1 = ar(W1 + 2048, 4096).rearrange("p (c n) -> p c n", c=KE)
        wo1 = ar(W1 + 6144, 2048).rearrange("p (h n) -> p h n", h=H1)
        wgu = ar(0, 16384).rearrange("p (c n) -> p c n", c=KE)
        wdn = ar(16384, 8192).rearrange("p (c n) -> p c n", c=4)
        gTs = ar(24576, 2048).rearrange("p (f n) -> p f n", f=4)
        xr_all = ar(26624, 4096)

        WA = sb("WA", [P, 8192])

        def wa(off, n):
            return WA[:, off:off + n]

        w0 = [wa(512 * i, 512).rearrange("p (c n) -> p c n", c=KE) for i in range(4)]
        wgate = wa(2048, 2048).rearrange("p (c n) -> p c n", c=KE)
        wup = wa(4096, 2048).rearrange("p (c n) -> p c n", c=KE)
        wdown = wa(6144, 2048).rearrange("p (f n) -> p f n", f=8)
        shg = wa(0, 1024).rearrange("p (c n) -> p c n", c=KE)
        shu = wa(1024, 1024).rearrange("p (c n) -> p c n", c=KE)
        shd = wa(2048, 1024).rearrange("p (f n) -> p f n", f=4)
        hs = wa(3072, 1024).rearrange("p (t e) -> p t e", t=NT)
        h_all = wa(4096, 4096)
        yg = h_all.rearrange("p (t e) -> p t e", t=TILES)
        sgTs = gates_bc[:, 16:20, :].rearrange("p k e -> p (k e)").rearrange("p (i n) -> p i n", i=2)
        sgs = wa(0, 1024).rearrange("p (j n) -> p j n", j=2)
        acts = wa(1024, 1024).rearrange("p (j n) -> p j n", j=2)
        actT = wa(2048, 1024).rearrange("p (j f n) -> p j f n", j=2, f=4)
        old = gates_bc[:, 0:8, :].rearrange("p k e -> p (k e)")
        xs = old[:, 0:512].rearrange("p (j e) -> p j e", j=2)
        xsT = old[:, 512:1024].rearrange("p (j c n) -> p j c n", j=2, c=KE)
        lrows = old[0:NEXP, 1024:1536]
        ys = old[:, 1024:1536].rearrange("p (j e) -> p j e", j=2)
        wg1 = sb("wg1", [P, KE, H1])
        negbg = sb("negbg", [P, 1])
        router = sb("router", [P, KE, NEXP])
        logits = sb("logits", [P, TILES * NEXP])
        g1 = sb("g1", [P, NT * H1])
        ssq = sb("ssq", [P, 2, H1])
        rnorm = sb("rnorm", [P, 2, H1])
        nmax1 = sb("nmax1", [P, 2, 4])
        rsum1 = sb("rsum1", [P, 2, 4])
        rinv1 = sb("rinv1", [P, 2, 4])
        pos_i = sb("pos_i", [P, TILES], I32)
        slot_e = sb("slot_e", [P, SLOTS], I32)
        score = sb("score", [P, TILES])
        r_eq = small[:, 0:128].rearrange("p (t e) -> p t e", t=TILES)
        r_oh = small[:, 128:256].rearrange("p (t e) -> p t e", t=TILES)
        r_ohx = old[:, 0:68].bitcast(BF16).rearrange("p (t e) -> p t e", t=TILES + 1)
        r_a = old[:, 256:512]
        r_n, r_nt, r_end, r_base = (old[:, 512 + 8 * i:520 + 8 * i] for i in range(4))
        r_m, r_pos, r_f = old[:, 544:560], old[:, 560:576], old[:, 576:576 + SLOTS]
        r_thr = old[:, 1536:1664].rearrange("p (e j) -> p e j", e=NEXP)
        r_iota = old[:, 1664:1664 + SLOTS * NEXP].rearrange("p (s e) -> p s e", e=NEXP)
        r_incl = old[:, 1856:1920].rearrange("p (e j) -> p e j", e=NEXP)
        r_w8 = old[:, 1920:2048].rearrange("p (t e) -> p t e", t=TILES)

        ps = ctx.enter_context(nc.psum_tensor("ps", [P, 8, 512], F32))
        ps_flat = ps[:, :, :].rearrange("p b n -> p (b n)")

        def banks(i, n=2):
            return ps_flat[:, 512 * i:512 * (i + n)]

        def mod_cols(kind):
            return kind * E, kind * E + E
        G0, G1, SC1 = 0, 8, 16

        names = """in_x0 in_x in_c in_mod0 in_mod0r in_mod1 in_ident in_const in_wqkv in_wo0 in_ffn in_kaug in_bo in_w1 in_sh in_exp in_small1
        in_rt zero_done zfill
        setup_v x_settled heads_settled silu_c scbc_done modT_ps modT_done bc_ps bc_sb guard_v gabo_done pre_pool preset
        ln_stats ln_mv ln_var ln_rstd xhat_ready
        a_xT a_h a_qk a_p1 a_r1 a_p2 a_p3 a_stack0 a_stack1 a_v a_vc a_s1 a_max a_mT a_m1 a_m2 a_m3 a_m4 a_mrow0
        a_mrow1 a_s2 a_exp a_pv a_oT a_oTT a_rc a_ctx a_cT a_cTe a_o a_tmp a_x a_xb
        b_xT b_h b_g b_u b_sg b_gt b_o b_tmp b_x
        c_xT c_h c_gr c_gx c_gp c_ge c_g1 c_gate c_p c_sq c_ss c_rk0 c_rk c_qn c_qT c_qe c_v c_ve c_s c_mx c_e c_ri c_pn
        c_pT c_pTe c_o c_oe c_w c_tmp c_x
        d_h0 d_h d_hc d_yT d_yh d_lr d_lx d_l d_lc d_hs d_xT d_hT d_g d_u d_sg d_gt d_o d_tmp d_x
        r_v r_read r_R r_exp r_xr r_scatter r_pos_ok
        m_s m_in0 m_in1 m_xT m_xTe m_gu m_sg m_a m_aT m_aTe m_d m_y m_out0 m_out1 m_gather0 m_gather1 m_gather2 m_gather3 f_tmp f_x f_out""".split()
        identb_d, maskq_d, maskk_d, maskw_d, before_d, kaug_d = (
            a.bitcast(BF16) for a in (identb_d, maskq_d, maskk_d, maskw_d, before_d, kaug_d))
        s = {n: sem("s_" + n) for n in names}

        block = ctx.enter_context(nc.Block())

        x_rows = x_d.rearrange("b (t p) e -> p b t e", p=P)
        out_rows = out_d.rearrange("b (t p) e -> p (b t) e", p=P)

        def chunks(w):
            return w.rearrange("(c p) n -> p c n", p=P)

        @block.sync
        def _(sp):
            sp.dma_start(cT[:, :, :, :], cT_d).then_inc(s["in_c"], 16)
            sp.dma_start(x_all[:, 0:NT * E].rearrange("p (t e) -> p t e", e=E), x_rows[:, 0]).then_inc(s["in_x0"], 16)
            sp.dma_start(ident[:, :], ident_d).then_inc(s["in_ident"], 16)
            sp.dma_start(wmod[0][:, :, 0:2 * E], chunks(wmod0_d)[:, :, 0:2 * E]).then_inc(s["in_mod0"], 16)
            for i, w in enumerate((wq0_d, wk0_d, wv0_d)):
                sp.dma_start(w0[i], chunks(w)).then_inc(s["in_wqkv"], 16)
            sp.dma_start(wmod[0][:, :, 2 * E:], chunks(wmod0_d)[:, :, 2 * E:]).then_inc(s["in_mod0r"], 16)
            sp.dma_start(kst[BIAS_ROW:STACK], kaug_d).then_inc(s["in_kaug"], 16)
            for dst, src in ((identb[:, :], identb_d), (maskq[:, :], maskq_d), (maskk[:, :], maskk_d),
                             (maskw[:, :], maskw_d), (before[:, :], before_d)):
                sp.dma_start(dst, src).then_inc(s["in_const"], 16)
            sp.dma_start(wmod[1], chunks(wmod1_d)).then_inc(s["in_mod1"], 16)
            sp.dma_start(w0[3], chunks(wo0_d)).then_inc(s["in_wo0"], 16)
            sp.dma_start(bo_bc, bo_d).then_inc(s["in_bo"], 16)

            def stack(b):
                for i in range(4):
                    g, st, pt = i // 2, (qst, kst)[i % 2], (Q_PARTS, K_PARTS)[i % 2]
                    sp.wait_ge(s["a_p3"], 4 * b + i + 1)
                    for r, part in enumerate(pt):
                        sp.dma_start(st[16 * r:16 * r + 16, HG * g:HG * g + HG, :], parts[:, i, part, :])\
                            .then_inc(s[f"a_stack{g}"], 16)

            def max_rows(b, g):
                sp.wait_ge(s["a_m4"], 2 * b + g + 1)
                for a in range(3):
                    sp.dma_start(qst[MAX_ROW + a:MAX_ROW + a + 1, HG * g:HG * g + HG, :],
                                 mparts[0:32, g, a, :]).then_inc(s[f"a_mrow{g}"], 16)

            stack(0)
            for b in range(1, B):
                sp.dma_start(x_all[:, b * NT * E:(b + 1) * NT * E].rearrange("p (t e) -> p t e", e=E),
                             x_rows[:, b]).then_inc(s["in_x"], 16)
            sp.dma_start(wgate, chunks(wgate_d)).then_inc(s["in_ffn"], 16)
            sp.dma_start(wup, chunks(wup_d)).then_inc(s["in_ffn"], 16)
            sp.dma_start(wdown, chunks(wdown_d)).then_inc(s["in_ffn"], 16)
            max_rows(0, 0)
            for dst, src in ((wg1[:, :, :], chunks(wg1_d)), (negbg[0:H1, :], bg_d), (qscale[:, :], qs_d),
                             (kscale[:, :], ks_d), (router[:, :, :], chunks(router_d))):
                sp.dma_start(dst, src).then_inc(s["in_small1"], 16)
            sp.wait_ge(s["zero_done"], 1)
            for j in range(SLOTS):
                sp.dma_start(rows_d[j * P:(j + 1) * P, :], zero_rows).then_inc(s["zfill"], 16)
            with sp.Fori(0, B - 1) as b:
                max_rows(b, 1)
                stack(b + 1)
                max_rows(b + 1, 0)
            max_rows(B - 1, 1)

            sp.wait_ge(s["a_x"], 1 + TILES)
            sp.wait_ge(s["zfill"], 16 * SLOTS)
            sp.dma_start(wq1, chunks(wq1_d)).then_inc(s["in_w1"], 16)
            sp.dma_start(wkv1, chunks(wkv1_d)).then_inc(s["in_w1"], 16)
            sp.dma_start(wo1, chunks(wo1_d)).then_inc(s["in_w1"], 16)
            sp.wait_ge(s["b_x"], 1 + TILES)
            sp.dma_start(shg, chunks(sg_d)).then_inc(s["in_sh"], 16)
            sp.dma_start(shu, chunks(su_d)).then_inc(s["in_sh"], 16)
            sp.dma_start(shd, chunks(sd_d)).then_inc(s["in_sh"], 16)
            for dst, src in ((r_thr, thr_d), (r_iota, iota_d), (r_incl, incl_d), (r_w8, w8_d)):
                sp.dma_start(dst, src).then_inc(s["in_rt"], 16)
            sp.wait_ge(s["c_x"], 1 + TILES)
            for e in range(NEXP):
                sp.dma_start(wgu[:, :, e * 2 * FE:(e + 1) * 2 * FE], chunks(gu_d[e])).then_inc(s["in_exp"], 16)
                sp.dma_start(wdn[:, :, e * E:(e + 1) * E], chunks(dn_d[e])).then_inc(s["in_exp"], 16)

            sp.wait_ge(s["r_scatter"], 16 * TILES)

            def rows_in(slot, j):
                sp.wait_ge(s["m_xT"], slot + 1)
                sp.dma_start(xs[:, j, :], rows_d[bass.ds(slot * P, P), :]).then_inc(s[f"m_in{j}"], 16)

            for slot in range(3):
                rows_in(slot, slot % 2)
            with sp.Fori(0, SLOT_PAIRS) as i:
                rows_in(2 * i + 3, 1)
                rows_in(2 * i + 4, 0)

            for t in range(TILES):
                sp.wait_ge(s["f_x"], t + 1)
                sp.dma_start(out_rows[:, t], x_all[:, t * E:(t + 1) * E]).then_inc(s["f_out"], 16)
            sp.wait_ge(s["f_out"], 16 * TILES)

        @block.gpsimd
        def _(pool):
            gp = nc.gpsimd

            def ln_pool(n):
                pool.wait_ge(s["ln_var"], n + 1)
                gp.tensor_tensor(rstd[:, :], vareps[:, :], minus_half[:, 0:NT], ALU.pow).then_inc(s["ln_rstd"], 1)

            gp.memset(minus_half[:, :], -0.5).then_inc(s["pre_pool"], 1)
            gp.memset(zero_rows, 0.0).then_inc(s["zero_done"], 1)
            gp.memset(ones_b[:, :], 1.0).then_inc(s["pre_pool"], 1)
            pool.wait_ge(s["pre_pool"], 2)
            ln_pool(0)
            pool.wait_ge(s["ln_rstd"], 1)
            gp.memset(qst[BIAS_ROW:MAX_ROW], 1.0).then_inc(s["preset"], 1)
            pool.wait_ge(s["preset"], 1)
            gp.memset(vaug[:, :, :, D0:32], 0.0).then_inc(s["preset"], 1)
            pool.wait_ge(s["preset"], 2)
            gp.memset(vaug[:, :, :, D0:D0 + 1], 1.0).then_inc(s["preset"], 1)

            def third_parts(b, ln=None):
                for i in range(4):
                    if i == 2 and ln is not None:
                        ln_pool(ln)
                    pool.wait_ge(s["a_p2"], 4 * b + i + 1)
                    gp.tensor_tensor(parts[:, i, 2, :], resid[:, i, :], parts[:, i, 1, :], ALU.subtract)\
                        .then_inc(s["a_p3"], 1)

            def residual_bias(b, ready):
                xb = x_all[:, bass.ds(b * (NT * E), NT * E)].rearrange("p (t e) -> p t e", e=E)
                pool.wait_ge(s["xhat_ready"], ready)
                gp.tensor_tensor(xb, xb, gabo[:, bass.ds(b, 1), :].to_broadcast([P, NT, E]), ALU.add)\
                    .then_inc(s["a_xb"], 1)

            def third_max_part(b, g):
                pool.wait_ge(s["a_m3"], 2 * b + g + 1)
                gp.tensor_tensor(mparts[0:32, g, 2, :], mres[0:32, g, :], mparts[0:32, g, 1, :], ALU.subtract)\
                    .then_inc(s["a_m4"], 1)

            third_parts(0)
            third_max_part(0, 0)
            pool.wait_ge(s["gabo_done"], 1)
            residual_bias(0, NT)
            with pool.Fori(0, B - 1) as b:
                third_max_part(b, 1)
                ln_pool(2 * b + 1)
                third_parts(b + 1, 2 * b + 2)
                residual_bias(b + 1, NT * (2 * b + 2))
                third_max_part(b + 1, 0)
            third_max_part(B - 1, 1)
            ln_pool(2 * B - 1)
            ln_pool(2 * B)
            pool.wait_ge(s["b_x"], 1 + TILES)
            for i in range(2):
                gp.memset(pr1[:, i, :, 0:WIN], 0.0).then_inc(s["preset"], 1)

            def norms(b):
                for u in range(2 * NT):
                    pool.wait_ge(s["c_rk0"], 2 * NT * b + u + 1)
                    gp.tensor_tensor(rnorm[:, u % 2, :], ssq[:, u % 2, :], minus_half[:, :], ALU.pow)\
                        .then_inc(s["c_rk"], 1)

            norms(0)
            with pool.Fori(0, B - 1) as b:
                ln_pool(2 * B + 1 + 2 * b)
                ln_pool(2 * B + 2 + 2 * b)
                norms(b + 1)
            ln_pool(4 * B - 1)
            pool.wait_ge(s["zfill"], 16 * SLOTS)
            pool.wait_ge(s["r_pos_ok"], 1)
            for t in range(TILES):
                pool.wait_ge(s["r_xr"], t + 1)
                gp.indirect_dma_start(rows_d, bass.IndirectOffsetOnAxis(ap=pos_i[:, t:t + 1], axis=0),
                                      xr_all[:, t * E:(t + 1) * E], None).then_inc(s["r_scatter"], 16)

            def rows_out(slot, j):
                pool.wait_ge(s["m_y"], slot + 1)
                gp.dma_start(yrows_d[bass.ds(slot * P, P), :], ys[:, j, :]).then_inc(s[f"m_out{j}"], 16)

            with pool.Fori(0, SLOT_PAIRS + 1) as i:
                rows_out(2 * i, 0)
                rows_out(2 * i + 1, 1)
            rows_out(SLOTS - 1, 0)
            pool.wait_ge(s["r_scatter"], 16 * TILES)
            pool.wait_ge(s["m_out0"], 16 * (SLOTS // 2 + 1))
            pool.wait_ge(s["m_out1"], 16 * (SLOTS // 2))
            for t in range(TILES):
                gp.indirect_dma_start(yg[:, t, :], None, yrows_d,
                                      bass.IndirectOffsetOnAxis(ap=pos_i[:, t:t + 1], axis=0))\
                    .then_inc(s[f"m_gather{t // 4}"], 16)

        @block.scalar
        def _(act):
            ac = nc.scalar

            def h_out(n_b, xT_sem, h_sem, layer, shift, scale):
                for c in range(KE):
                    act.wait_ge(xT_sem, KE * n_b + c + 1)
                    ac.activation(hT[:, c, :], ps[:, c, :], ACT.Identity,
                                  bias=modT[:, layer, shift + c, bass.ds(n_b, 1)],
                                  scale=modT[:, layer, scale + c, bass.ds(n_b, 1)]).then_inc(h_sem, 1)

            def ffn_act(b, nf, sgbuf, k, ahead={}):
                for f in range(nf):
                    if f in ahead:
                        ahead[f]()
                    act.wait_ge(s[k + "_g"], nf * b + f + 1)
                    if f >= 2:
                        act.wait_ge(s[k + "_gt"], nf * b + f - 1)
                    ac.activation(sgbuf[:, f % 2, :], ps[:, 2 + 2 * (f % 3), :], ACT.Silu).then_inc(s[k + "_sg"], 1)

            act.wait_ge(s["in_c"], 16)
            ac.activation(scT[:, :, :, :].rearrange("p l c b -> p (l c b)"),
                          cT[:, :, :, :].rearrange("p l c b -> p (l c b)"), ACT.Silu).then_inc(s["silu_c"], 1)
            act.wait_ge(s["modT_done"], 2)


            def qk_part(b, i, a):
                if a == 0:
                    act.wait_ge(s["a_qk"], 4 * b + i + 1)
                    ac.copy(parts[:, i, 0, :], ps[:, 2 + i, :]).then_inc(s["a_p1"], 1)
                else:
                    act.wait_ge(s["a_r1"], 4 * b + i + 1)
                    ac.copy(parts[:, i, 1, :], resid[:, i, :]).then_inc(s["a_p2"], 1)

            def max_parts(b, g):
                bank = (0, 7)[g]
                act.wait_ge(s["a_mT"], 2 * b + g + 1)
                ac.copy(mparts[0:32, g, 0, :], ps[0:32, bank, 0:P]).then_inc(s["a_m1"], 1)
                act.wait_ge(s["a_m2"], 2 * b + g + 1)
                ac.copy(mparts[0:32, g, 1, :], mres[0:32, g, :]).then_inc(s["a_m3"], 1)

            def a_core(b, more):
                for h in range(H0):
                    if h == HG:
                        max_parts(b, 1)
                    act.wait_ge(s["a_s2"], H0 * b + h + 1)
                    if h >= 8:
                        act.wait_ge(s["a_pv"], 4 * b + (h - 8) // 4 + 1)
                    ac.activation(probs[:, h % 8, :], banks(3 * (h % 2), 3)[:, 0:KM], ACT.Exp,
                                  scale=float(D0) ** -0.5).then_inc(s["a_exp"], 1)
                if more:
                    h_out(b + 1, s["a_xT"], s["a_h"], 0, 0, 2)
                    qk_part(b + 1, 0, 0)
                    qk_part(b + 1, 0, 1)
                    qk_part(b + 1, 1, 0)
                for c in range(KE):
                    act.wait_ge(s["a_cT"], KE * b + c + 1)
                    ac.copy(ctxT[:, c, :], ps[:, c, :]).then_inc(s["a_cTe"], 1)
                if more:
                    qk_part(b + 1, 1, 1)
                    qk_part(b + 1, 2, 0)
                    qk_part(b + 1, 3, 0)
                    qk_part(b + 1, 2, 1)
                    qk_part(b + 1, 3, 1)

            def b_all(b):
                h_out(b, s["b_xT"], s["b_h"], 0, 6, 8)
                ffn_act(b, 8, sgT, "b")

            h_out(0, s["a_xT"], s["a_h"], 0, 0, 2)
            for i in range(4):
                qk_part(0, i, 0)
                qk_part(0, i, 1)
            max_parts(0, 0)
            act.wait_ge(s["modT_done"], 6)
            with act.Fori(0, B - 1) as b:
                a_core(b, True)
                b_all(b)
                max_parts(b + 1, 0)
            a_core(B - 1, False)
            b_all(B - 1)


            def d_turned(b):
                for c in range(KE):
                    act.wait_ge(s["d_yT"], KE * b + c + 1)
                    ac.copy(hT[:, c, :], ps[:, c, :]).then_inc(s["d_yh"], 1)

            def d_rows(b, bank=2):
                act.wait_ge(s["d_lr"], b + 1)
                ac.copy(lrows, ps[0:NEXP, bank, :]).then_inc(s["d_lx"], 1)

            def d_keep(b):
                act.wait_ge(s["d_h"], b + 1)
                ac.copy(h_all[:, bass.ds(b * (NT * E), NT * E)], hs.rearrange("p t e -> p (t e)"))\
                    .then_inc(s["d_hc"], 1)

            def c_in(b, d=None):
                act.wait_ge(s["c_gr"], b + 1)
                ac.activation(qn[0:H1, 1, 0:S], ps[0:H1, 0, :], ACT.Exp, bias=negbg[0:H1, 0:1], scale=-1.0)\
                    .then_inc(s["c_gx"], 1)

                def qk_out(u):
                    act.wait_ge(s["c_qT"], 2 * NT * b + u + 1)
                    dst, sc = (qT1, qscale) if u % 2 == 0 else (kT1, kscale)
                    t = u // 2
                    ac.activation(dst[:, :, t * P:(t + 1) * P], banks(6).rearrange("p (h n) -> p h n", h=H1),
                                  ACT.Copy, scale=sc[:, 0:1]).then_inc(s["c_qe"], 1)

                for u in range(2 * NT):
                    act.wait_ge(s["c_p"], 2 * NT * b + u + 1)
                    if u >= 2:
                        act.wait_ge(s["c_ss"], 2 * NT * b + u - 1)
                    ac.activation(sq[:, u % 2, :], banks(2 + 2 * (u % 2)), ACT.Square).then_inc(s["c_sq"], 1)
                    if u >= 2:
                        qk_out(u - 2)
                    if u % 2 == 1:
                        t = u // 2
                        act.wait_ge(s["c_v"], NT * b + t + 1)
                        ac.copy(v1[:, t, :], banks(0)).then_inc(s["c_ve"], 1)
                qk_out(2 * NT - 2)
                if d is not None:
                    d_turned(d)
                qk_out(2 * NT - 1)
                if d is not None:
                    d_rows(d)
                    d_keep(d)

            def c_core(b, more):
                for i in range(2 * NT + 2):
                    if i < 2 * NT:
                        t = i // 2
                        c0 = P if t == 0 else WIN
                        act.wait_ge(s["c_mx"], 2 * NT * b + i + 1)
                        if i >= 2:
                            act.wait_ge(s["c_pT"], 2 * NT * b + i - 1)
                        sc4 = banks(2 * (i % 2)).rearrange("p (h n) -> p h n", h=4)
                        for hh in range(4):
                            ac.activation(pr1[:, i % 2, hh, c0:], sc4[:, hh, c0:], ACT.Exp,
                                          bias=nmax1[:, i % 2, hh:hh + 1],
                                          accum_out=rsum1[:, i % 2, hh:hh + 1]).then_inc(s["c_e"], 1)
                    if i >= 2:
                        v = i - 2
                        act.wait_ge(s["c_o"], 2 * NT * b + v + 1)
                        ac.copy(oT1[:, (v // 2) % 2, 4 * (v % 2):4 * (v % 2) + 4, :].rearrange("p h n -> p (h n)"),
                                ps[:, 6, :]).then_inc(s["c_oe"], 1)
                    if i == 2 * NT and more:
                        h_out(b + 1, s["c_xT"], s["c_h"], 1, 0, 2)

            act.wait_ge(s["modT_done"], 6)
            act.wait_ge(s["setup_v"], 2)
            h_out(0, s["c_xT"], s["c_h"], 1, 0, 2)
            c_in(0)
            with act.Fori(0, B - 1) as b:
                c_core(b, True)
                c_in(b + 1, b)
            c_core(B - 1, False)

            def shared_h(m):
                if m == 0:
                    act.wait_ge(s["d_hc"], 1 + B)
                else:
                    act.wait_ge(s["d_xT"], KE * m)
                ac.copy(hs.rearrange("p t e -> p (t e)"), h_all[:, m * NT * E:(m + 1) * NT * E])\
                    .then_inc(s["d_hs"], 1)

            def shared_T(m):
                for c in range(KE):
                    act.wait_ge(s["d_xT"], KE * m + c + 1)
                    ac.copy(hT[:, c, :], ps[:, c, :]).then_inc(s["d_hT"], 1)

            def score_exp():
                act.wait_ge(s["r_v"], 1)
                ac.activation(score[:, :], r_m, ACT.Exp, scale=-1.0).then_inc(s["r_exp"], 1)

            ffn_act(0, 4, sgTs, "d")
            d_turned(B - 1)
            d_rows(B - 1, 0)
            d_keep(B - 1)
            shared_h(0)
            ffn_act(1, 4, sgTs, "d", {1: score_exp})
            for m in range(B - 2):
                shared_T(m)
                if m < B - 3:
                    shared_h(m + 1)
                ffn_act(m + 2, 4, sgTs, "d")

            def silu(slot, j):
                act.wait_ge(s["m_gu"], slot + 1)
                ac.activation(sgs[:, j, :], ps[:, 1 + 2 * j, :], ACT.Silu).then_inc(s["m_sg"], 1)

            def xT_out(slot, j):
                act.wait_ge(s["m_xT"], slot + 3)
                ac.copy(xsT[:, j, :, :].rearrange("p c n -> p (c n)"), ps[:, 0, 0:E]).then_inc(s["m_xTe"], 1)

            xT_out(0, 0)
            xT_out(1, 1)
            silu(0, 0)
            xT_out(2, 0)
            silu(1, 1)
            with act.Fori(0, SLOT_PAIRS) as i:
                xT_out(2 * i + 3, 1)
                silu(2 * i + 2, 0)
                xT_out(2 * i + 4, 0)
                silu(2 * i + 3, 1)
            silu(SLOTS - 1, 0)

        @block.vector
        def _(dve):
            v = nc.vector

            def ln_tiles(tile0, t0, t1):
                dve.sem_inc(s["x_settled"], 1)
                for t in range(t0, t1):
                    v.bn_stats(stats[:, t, :], x_all[:, bass.ds((tile0 + t) * E, E)]).then_inc(s["ln_stats"], 1)

            def ln_moments(n):
                dve.wait_ge(s["ln_stats"], NT * n + NT)
                v.tensor_tensor(lsum[:, :, :], stats[:, :, 1:3], stats[:, :, 4:6], ALU.add).then_inc(s["ln_mv"], 1)
                v.tensor_tensor(ldif[:, :], stats[:, :, 1], stats[:, :, 4], ALU.subtract).then_inc(s["ln_mv"], 1)
                dve.wait_ge(s["ln_mv"], 5 * n + 2)
                v.tensor_scalar(mean[:, :], lsum[:, :, 0], 0.5, None, ALU.mult).then_inc(s["ln_mv"], 1)
                v.tensor_scalar(lvar[:, :], lsum[:, :, 1], 1.0 / E, EPS, ALU.mult, ALU.add).then_inc(s["ln_mv"], 1)
                v.scalar_tensor_tensor(out=lsq[:, :], in0=ldif[:, :], scalar=0.25, in1=ldif[:, :], op0=ALU.mult,
                                       op1=ALU.mult).then_inc(s["ln_mv"], 1)
                dve.wait_ge(s["ln_mv"], 5 * n + 5)
                v.tensor_tensor(vareps[:, :], lvar[:, :], lsq[:, :], ALU.add).then_inc(s["ln_var"], 1)

            def ln_stats(n, tile0):
                ln_tiles(tile0, 0, NT)
                ln_moments(n)

            def ln_apply(n, tile0, t0=0, t1=NT):
                dve.wait_ge(s["ln_rstd"], n + 1)
                for t in range(t0, t1):
                    v.tensor_scalar(xhat[:, t, :], x_all[:, bass.ds((tile0 + t) * E, E)], mean[:, t:t + 1],
                                    rstd[:, t:t + 1], ALU.subtract, ALU.mult).then_inc(s["xhat_ready"], 1)

            def x_update(b, tile, src, gate, tmp_sem, x_sem, par, k):
                v.scalar_tensor_tensor(out=utmp[:, par, :], in0=src, scalar=4.0,
                                       in1=gates_bc[:, bass.ds(gate, 1), :].rearrange("p a e -> p (a e)"),
                                       op0=ALU.mult, op1=ALU.mult).then_inc(tmp_sem, 1)
                dve.wait_ge(tmp_sem, k + 1)
                xt = x_all[:, bass.ds(tile * E, E)]
                v.tensor_tensor(xt, xt, utmp[:, par, :], ALU.add).then_inc(x_sem, 1)

            def ffn_dve(b, nf, gbuf, sgbuf, k, gate0, n_ln=None, ln_tile=None, between=None, after_up=None,
                        ahead={}, batch=None):
                batch = b if batch is None else batch
                for f in range(nf):
                    if f in ahead:
                        ahead[f]()
                    if between is not None:
                        if f == 0:
                            between(0, 4)
                        if f < nf - 1:
                            between(4 * f + 4, 4 * f + 5)
                    dve.wait_ge(s[k + "_sg"], nf * b + f + 1)
                    dve.wait_ge(s[k + "_u"], nf * b + f + 1)
                    v.tensor_tensor(gbuf[:, f, :], sgbuf[:, f % 2, :], ps[:, 3 + 2 * (f % 3), :], ALU.mult)\
                        .then_inc(s[k + "_gt"], 1)
                    if between is not None and f < nf - 1:
                        between(4 * f + 5, 4 * f + 8)
                    if f == nf // 2 - 1 and ln_tile is not None:
                        ln_stats(n_ln, ln_tile)
                    if f == nf // 2 and ln_tile is not None:
                        ln_apply(n_ln, ln_tile)
                if after_up is not None:
                    after_up()
                for t in range(NT):
                    dve.wait_ge(s[k + "_o"], 2 * b + t // 2 + 1)
                    x_update(b, NT * batch + t, ps[:, 6 + t // 2, (t % 2) * E:(t % 2 + 1) * E], gate0 + 2 * batch,
                             s[k + "_tmp"], s[k + "_x"], t % 2, NT * b + t)

            for k in "abcd":
                dve.sem_inc(s[k + "_x"], 1)
            dve.sem_inc(s["d_hc"], 1)
            dve.sem_inc(s["d_lc"], 1)
            dve.wait_ge(s["in_x0"], 16)
            ln_stats(0, 0)
            ln_apply(0, 0)
            dve.wait_ge(s["silu_c"], 1)
            mod = ps[:, 7, 0:96].rearrange("p (l j b) -> p l j b", l=2, j=12)

            def mod_out(layer, j):
                v.tensor_copy(modT[:, layer, j:j + 2, :], mod[:, layer, j:j + 2, :]).then_inc(s["modT_done"], 1)
                v.tensor_scalar(modT[:, layer, j + 2:j + 4, :], mod[:, layer, j + 2:j + 4, :], 1.0, None, ALU.add)\
                    .then_inc(s["modT_done"], 1)

            dve.wait_ge(s["modT_ps"], 1)
            mod_out(0, 0)
            v.tensor_copy(sc_bc.rearrange("p l c b n -> p (l c b) n"),
                          scT[:, :, :, :].rearrange("p l c b -> p (l c b)").unsqueeze(2).to_broadcast([P, 16, P]))\
                .then_inc(s["scbc_done"], 1)

            def gate_rows(u):
                half_sign, size = guard[u % 2]
                g = ps[:, 2 + u % 2, :]
                v.tensor_scalar(half_sign, g, 0.0, 0.5, ALU.is_ge, ALU.subtract).then_inc(s["guard_v"], 1)
                dve.wait_ge(s["guard_v"], 2 * u + 1)
                v.tensor_tensor(size, g, half_sign, ALU.mult).then_inc(s["guard_v"], 1)
                dve.wait_ge(s["guard_v"], 2 * u + 2)
                v.scalar_tensor_tensor(out=gates_bc[:, 2 * u:2 * u + 2, :].rearrange("p k e -> p (k e)"), in0=size,
                                       scalar=0.125, in1=half_sign, op0=ALU.max, op1=ALU.mult)\
                    .then_inc(s["bc_sb"], 1)

            def shift_rows(u):
                g = ps[:, 2 + u % 2, :]
                v.tensor_copy(gates_bc[:, 2 * u, :], g[:, 0:E])
                v.tensor_scalar(gates_bc[:, 2 * u + 1, :], g[:, E:2 * E], 1.0, None, ALU.add)\
                    .then_inc(s["bc_sb"], 1)


            def resid_of(b, i):
                dve.wait_ge(s["a_p1"], 4 * b + i + 1)
                v.tensor_tensor(resid[:, i, :], ps[:, 2 + i, :], parts[:, i, 0, :], ALU.subtract)\
                    .then_inc(s["a_r1"], 1)

            def v_out(b, i):
                dve.wait_ge(s["a_v"], 2 * b + i + 1)
                v.tensor_copy(vaug[:, 2 * i:2 * i + 2, :, 0:D0],
                              ps[:, 6 + i, :].rearrange("p (t h d) -> p t h d", t=2, h=H0)).then_inc(s["a_vc"], 1)

            def head_maxima(b, g, bank, u0, u1):
                for u in range(u0, u1):
                    h, qt = HG * g + u // 4, u % 4
                    dve.wait_ge(s["a_s1"], 64 * b + 32 * g + u + 1)
                    v.reduce_max(rowmax[:, h:h + 1, qt], ps[:, bank + u % 2, 0:(qt + 1) * P], AX_X)\
                        .then_inc(s["a_max"], 1)

            def max_resid(b, g):
                dve.wait_ge(s["a_m1"], 2 * b + g + 1)
                v.tensor_tensor(mres[0:32, g, :], ps[0:32, (0, 7)[g], 0:P], mparts[0:32, g, 0, :], ALU.subtract)\
                    .then_inc(s["a_m2"], 1)

            def a_core(b, more):
                head_maxima(b, 1, 6, 0, 32)
                max_resid(b, 1)
                if more:
                    ln_stats(2 * b + 1, (b + 1) * NT)
                for n in range(4):
                    if more and n == 2:
                        ln_apply(2 * b + 1, (b + 1) * NT)
                    dve.wait_ge(s["a_pv"], 4 * b + n + 1)
                    v.tensor_copy(oTs[:, n % 2, :], ps[:, 6, :]).then_inc(s["a_oT"], 1)
                    if more and n == 3:
                        resid_of(b + 1, 0)
                    dve.wait_ge(s["a_oTT"], 4 * b + n + 1)
                    tok = ps[:, 7, :].rearrange("p (t j c) -> p t j c", t=NT, j=4)
                    rd = rden[:, n % 2, :].rearrange("p (t j) -> p t j", t=NT)
                    v.reciprocal(rd, tok[:, :, :, D0]).then_inc(s["a_rc"], 1)
                    dve.wait_ge(s["a_rc"], 4 * b + n + 1)
                    v.tensor_tensor(ctx0[:, :, 4 * n * D0:4 * (n + 1) * D0].rearrange("p t (j d) -> p t j d", j=4),
                                    tok[:, :, :, 0:D0], rd.unsqueeze(3).to_broadcast([P, NT, 4, D0]), ALU.mult)\
                        .then_inc(s["a_ctx"], 1)
                if more:
                    resid_of(b + 1, 1)
                dve.wait_ge(s["a_xb"], b + 1)
                for t in range(NT):
                    dve.wait_ge(s["a_o"], 2 * b + t // 2 + 1)
                    x_update(b, NT * b + t, ps[:, t // 2, (t % 2) * E:(t % 2 + 1) * E], G0 + 2 * b,
                             s["a_tmp"], s["a_x"], t % 2, NT * b + t)
                dve.wait_ge(s["a_x"], 1 + NT * b + NT)

            for i in range(4):
                resid_of(0, i)
            for i in range(2):
                v_out(0, i)
            dve.wait_ge(s["in_bo"], 16)
            for u in range(12):
                dve.wait_ge(s["bc_ps"], u + 1)
                if u < 8:
                    gate_rows(u)
                else:
                    shift_rows(u)
                if u == 3:
                    dve.wait_ge(s["bc_sb"], 4)
                    v.scalar_tensor_tensor(out=gabo, in0=gates_bc[:, 0:8:2, :], scalar=4.0,
                                           in1=bo_bc.unsqueeze(1).to_broadcast([P, B, E]), op0=ALU.mult,
                                           op1=ALU.mult).then_inc(s["gabo_done"], 1)
                    dve.wait_ge(s["modT_ps"], 3)
                    mod_out(0, 6)
                    mod_out(1, 0)
                if u >= 4:
                    head_maxima(0, 0, 0, 4 * (u - 4), 4 * (u - 3))
            max_resid(0, 0)
            dve.wait_ge(s["gabo_done"], 1)
            dve.wait_ge(s["bc_sb"], 12)
            dve.wait_ge(s["in_x"], 16 * (B - 1))
            with dve.Fori(0, B - 1) as b:
                a_core(b, True)
                ln_stats(2 * b + 2, b * NT)
                resid_of(b + 1, 2)
                resid_of(b + 1, 3)
                dve.wait_ge(s["a_xT"], KE * (b + 1) + KE)
                ln_apply(2 * b + 2, b * NT)
                v_out(b + 1, 0)
                v_out(b + 1, 1)
                ffn_dve(b, 8, gT, sgT, "b", G0 + 1, between=lambda u0, u1: head_maxima(b + 1, 0, 0, u0, u1),
                        after_up=lambda: max_resid(b + 1, 0))
            a_core(B - 1, False)
            ln_stats(2 * B - 1, (B - 1) * NT)
            ln_apply(2 * B - 1, (B - 1) * NT)
            dve.wait_ge(s["b_x"], 1 + NT)
            ffn_dve(B - 1, 8, gT, sgT, "b", G0 + 1, 2 * B, 0)
            dve.wait_ge(s["b_x"], 1 + TILES)
            dve.wait_ge(s["in_small1"], 16 * 5)
            v.tensor_scalar(qscale[:, :], qscale[:, :], 8.0, None, ALU.mult).then_inc(s["setup_v"], 1)
            v.tensor_scalar(negbg[0:H1, :], negbg[0:H1, :], -1.0, None, ALU.mult).then_inc(s["setup_v"], 1)
            dve.wait_ge(s["setup_v"], 2)


            def c_in(b, at_half=None):
                dve.wait_ge(s["c_gp"], b + 1)
                v.tensor_scalar(small[:, 0:32], ps[:, 1, 0:32], 1.0, None, ALU.add).then_inc(s["c_g1"], 1)
                dve.wait_ge(s["c_g1"], b + 1)
                v.reciprocal(g1[:, :], small[:, 0:32]).then_inc(s["c_gate"], 1)
                for u in range(2 * NT):
                    dve.wait_ge(s["c_sq"], 2 * NT * b + u + 1)
                    v.reduce_sum(ssq[:, u % 2, :], sq[:, u % 2, :].rearrange("p (h d) -> p h d", h=H1), AX_X)\
                        .then_inc(s["c_ss"], 1)
                    dve.wait_ge(s["c_ss"], 2 * NT * b + u + 1)
                    v.tensor_scalar(ssq[:, u % 2, :], ssq[:, u % 2, :], 1e-24, None, ALU.max)\
                        .then_inc(s["c_rk0"], 1)
                    dve.wait_ge(s["c_rk"], 2 * NT * b + u + 1)
                    if u >= 2:
                        dve.wait_ge(s["c_qT"], 2 * NT * b + u - 1)
                    v.tensor_tensor(qn[:, u % 2, :].rearrange("p (h d) -> p h d", h=H1),
                                    banks(2 + 2 * (u % 2)).rearrange("p (h d) -> p h d", h=H1),
                                    rnorm[:, u % 2, :].unsqueeze(2).to_broadcast([P, H1, D1]), ALU.mult)\
                        .then_inc(s["c_qn"], 1)
                    if u == NT and at_half is not None:
                        at_half()

            def c_core(b, more):
                for i in range(2 * NT + 3):
                    if 1 <= i <= 2 * NT:
                        w = i - 1
                        k0 = 1 if w < 2 else 0
                        t, hg = w // 2, w % 2
                        w0c = P if t == 0 else WIN
                        dve.wait_ge(s["c_e"], 8 * NT * b + 4 * w + 4)
                        v.reciprocal(rinv1[:, w % 2, :], rsum1[:, w % 2, :]).then_inc(s["c_ri"], 1)
                        dve.wait_ge(s["c_ri"], 2 * NT * b + w + 1)
                        for hh in range(4):
                            g = g1[:, t * H1 + 4 * hg + hh:t * H1 + 4 * hg + hh + 1]
                            v.tensor_scalar(pr1[:, w % 2, hh, w0c:], pr1[:, w % 2, hh, w0c:],
                                            rinv1[:, w % 2, hh:hh + 1], g, ALU.mult, ALU.mult).then_inc(s["c_pn"], 1)
                    if i < 2 * NT:
                        c0 = P if i < 2 else WIN
                        dve.wait_ge(s["c_s"], 2 * NT * b + i + 1)
                        v.reduce_max(nmax1[:, i % 2, :],
                                     banks(2 * (i % 2)).rearrange("p (h n) -> p h n", h=4)[:, :, c0:], AX_X,
                                     negate=True).then_inc(s["c_mx"], 1)
                    if i >= 4 and i % 2 == 0:
                        t = i // 2 - 2
                        dve.wait_ge(s["c_w"], NT * b + t + 1)
                        x_update(b, NT * b + t, ps[:, 7, 0:E], G1 + 2 * b, s["c_tmp"], s["c_x"], t % 2, NT * b + t)
                    if 1 <= i <= 2 * NT:
                        w = i - 1
                        k0 = 1 if w < 2 else 0
                        dve.wait_ge(s["c_pT"], 2 * NT * b + w + 1)
                        v.tensor_copy(pT1[:, w % 2, :, k0:, :],
                                      banks(4).rearrange("p (h k n) -> p h k n", h=4, k=2)[:, :, k0:, :])\
                            .then_inc(s["c_pTe"], 1)
                    if more:
                        n, tile0 = 2 * B + 1 + 2 * b, (b + 1) * NT
                        if i == 2:
                            ln_tiles(tile0, 0, NT // 2)
                        if i == 3:
                            ln_tiles(tile0, NT // 2, NT)
                        if i == 4:
                            ln_moments(n)
                        if i == 5:
                            ln_apply(n, tile0, 0, NT // 2)
                        if i == 6:
                            ln_apply(n, tile0, NT // 2, NT)
                dve.wait_ge(s["c_x"], 1 + NT * b + NT)

            def d_h(b, n):
                dve.wait_ge(s["xhat_ready"], NT * n + NT)
                dve.wait_ge(s["d_hc"], 1 + b)
                row = SC1 + 2 * b
                v.tensor_tensor(hs, xhat[:, :, :], gates_bc[:, bass.ds(row + 1, 1), :].to_broadcast([P, NT, E]),
                                ALU.mult).then_inc(s["d_h0"], 1)
                dve.wait_ge(s["d_h0"], b + 1)
                v.tensor_tensor(hs, hs, gates_bc[:, bass.ds(row, 1), :].to_broadcast([P, NT, E]), ALU.add)\
                    .then_inc(s["d_h"], 1)

            def d_logits(b, bank=4):
                dve.wait_ge(s["d_l"], b + 1)
                v.tensor_copy(logits[:, bass.ds(b * (NT * NEXP), NT * NEXP)], ps[:, bank, 0:NT * NEXP])\
                    .then_inc(s["d_lc"], 1)

            c_in(0)
            with dve.Fori(0, B - 1) as b:
                c_core(b, True)
                ln_stats(2 * B + 2 + 2 * b, b * NT)
                dve.wait_ge(s["c_xT"], KE * (b + 1) + KE)
                ln_apply(2 * B + 2 + 2 * b, b * NT)
                c_in(b + 1, lambda: d_h(b, 2 * B + 2 + 2 * b))
                d_logits(b)
            c_core(B - 1, False)
            ln_stats(4 * B - 1, (B - 1) * NT)
            ln_apply(4 * B - 1, (B - 1) * NT)
            d_h(B - 1, 4 * B - 1)

            step = [0]

            def then(ins):
                step[0] += 1
                ins.then_inc(s["r_v"], 1)
                dve.wait_ge(s["r_v"], step[0])

            lg = logits[:, :].rearrange("p (t e) -> p t e", e=NEXP)

            def over_e(a, n=TILES):
                return a.unsqueeze(2).to_broadcast([P, n, NEXP])

            def over_t(a, n=TILES):
                return a.unsqueeze(1).to_broadcast([P, n, NEXP])

            def top_expert():
                d_logits(B - 1, 1)
                dve.wait_ge(s["d_lc"], 1 + B)
                dve.wait_ge(s["in_rt"], 16 * 4)
                then(v.reduce_max(r_m, lg, AX_X))
                then(v.tensor_tensor(r_eq, lg, over_e(r_m), ALU.is_equal))
                then(v.tensor_tensor(r_eq, r_eq, r_w8, ALU.mult))
                then(v.reduce_max(r_pos, r_eq, AX_X))
                then(v.tensor_tensor(r_oh, r_eq, over_e(r_pos), ALU.is_equal))
                then(v.memset(r_ohx[:, TILES, :], 0.0))
                then(v.tensor_copy(r_ohx[:, 0:TILES, :], r_oh))

            def slots_and_scores():
                dve.wait_ge(s["r_R"], 1)
                rank = ps[:, 0, 0:(TILES + 1) * NEXP].rearrange("p (t e) -> p t e", e=NEXP)
                then(v.tensor_copy(r_n, rank[:, TILES, :]))
                a128 = r_a[:, 0:128].rearrange("p (e j) -> p e j", e=NEXP)
                then(v.tensor_tensor(a128, r_n.unsqueeze(2).to_broadcast([P, NEXP, TILES]), r_thr, ALU.is_gt))
                then(v.reduce_sum(r_nt, a128, AX_X))
                a64 = r_a[:, 0:64].rearrange("p (e j) -> p e j", e=NEXP)
                then(v.tensor_tensor(a64, over_t(r_nt, NEXP), r_incl, ALU.mult))
                then(v.reduce_sum(r_end, a64, AX_X))
                then(v.tensor_tensor(r_base, r_end, r_nt, ALU.subtract))
                then(v.tensor_scalar(r_base, r_base, float(P), None, ALU.mult))
                then(v.tensor_tensor(r_eq, rank[:, 0:TILES, :], over_t(r_base), ALU.add))
                v.sem_inc(s["r_read"], 1)
                then(v.tensor_tensor(r_eq, r_eq, r_oh, ALU.mult))
                then(v.reduce_sum(r_pos, r_eq, AX_X))
                then(v.tensor_copy(pos_i[:, :], r_pos))
                a192 = r_a[:, 0:SLOTS * NEXP].rearrange("p (s e) -> p s e", e=NEXP)
                then(v.tensor_tensor(a192, r_iota, over_t(r_end, SLOTS), ALU.is_ge))
                then(v.reduce_sum(r_f, a192, AX_X))
                then(v.tensor_scalar(r_f, r_f, float(NEXP - 1), None, ALU.min))
                then(v.tensor_copy(slot_e[:, :], r_f))
                dve.wait_ge(s["r_exp"], 1)
                then(v.tensor_scalar(score[:, :], score[:, :], 1.0, None, ALU.add))
                then(v.reciprocal(score[:, :], score[:, :]))
                v.sem_inc(s["r_pos_ok"], 1)

            ffn_dve(0, 4, gTs, sgTs, "d", G1 + 1, batch=B - 2)
            ffn_dve(1, 4, gTs, sgTs, "d", G1 + 1, batch=B - 1, ahead={0: top_expert, 2: slots_and_scores})
            dve.wait_ge(s["d_hc"], 1 + B)
            for t in range(TILES):
                v.tensor_scalar(xr_all[:, t * E:(t + 1) * E], h_all[:, t * E:(t + 1) * E], score[:, t:t + 1], None,
                                ALU.mult).then_inc(s["r_xr"], 1)
            for m in range(B - 2):
                ffn_dve(m + 2, 4, gTs, sgTs, "d", G1 + 1, batch=m)
            dve.wait_ge(s["d_x"], 1 + TILES)

            dve.wait_ge(s["r_xr"], TILES)

            def act_out(slot, j):
                dve.wait_ge(s["m_sg"], slot + 1)
                v.tensor_tensor(acts[:, j, :], sgs[:, j, :], ps[:, 2 + 2 * j, :], ALU.mult).then_inc(s["m_a"], 1)

            def actT_out(slot, j):
                dve.wait_ge(s["m_aT"], slot + 1)
                v.tensor_copy(actT[:, j, :, :].rearrange("p f n -> p (f n)"), ps[:, 5, :]).then_inc(s["m_aTe"], 1)

            def y_out(slot, j, stored):
                dve.wait_ge(s["m_d"], slot + 1)
                if stored is not None:
                    dve.wait_ge(s[f"m_out{j}"], stored)
                v.tensor_copy(ys[:, j, :], ps[:, 6 + j, 0:E]).then_inc(s["m_y"], 1)

            act_out(0, 0)
            act_out(1, 1)
            actT_out(0, 0)

            def pair(i, stored):
                act_out(2 * i + 2, 0)
                actT_out(2 * i + 1, 1)
                y_out(2 * i, 0, stored)
                act_out(2 * i + 3, 1)
                actT_out(2 * i + 2, 0)
                y_out(2 * i + 1, 1, stored)

            pair(0, None)
            with dve.Fori(0, SLOT_PAIRS - 1) as i:
                pair(i + 1, 16 * i + 16)
            act_out(SLOTS - 1, 0)
            actT_out(SLOTS - 2, 1)
            y_out(SLOTS - 3, 0, 16 * SLOT_PAIRS)
            actT_out(SLOTS - 1, 0)
            y_out(SLOTS - 2, 1, 16 * SLOT_PAIRS)
            y_out(SLOTS - 1, 0, 16 * (SLOT_PAIRS + 1))
            for t in range(TILES):
                b = t // NT
                dve.wait_ge(s[f"m_gather{t // 4}"], 16 * 4)
                x_update(b, t, yg[:, t, :], G1 + 1 + 2 * b, s["f_tmp"], s["f_x"], t % 2, t)

        @block.tensor
        def _(pe):
            mm, tr = nc.tensor.matmul, nc.tensor.transpose

            def xhat_T(b, n, src, xT_sem):
                for c in range(KE):
                    for t in range(NT):
                        last = tr(ps[:, c, t * P:(t + 1) * P], src[:, t, c * P:(c + 1) * P], ident[:, :])
                    last.then_inc(xT_sem, 1)

            def ffn_up(b, nf, gw, uw, k, before=(), between=None):
                for f in range(nf):
                    if f >= 3:
                        pe.wait_ge(s[k + "_gt"], nf * b + f - 2)
                    if f == 2:
                        pe.wait_ge(s[k + "_x"], NT * b + 1)
                    for name, count, at in before:
                        if at == f:
                            pe.wait_ge(s[name], count)
                    for i, (w, done) in enumerate(((gw, "_g"), (uw, "_u"))):
                        for c in range(KE):
                            last = mm(ps[:, 2 + i + 2 * (f % 3), :], w[:, c, f * P:(f + 1) * P], hT[:, c, :],
                                      start=(c == 0), stop=(c == KE - 1))
                            if c == KE - 1:
                                last.then_inc(s[k + done], 1)
                            if between is not None:
                                between(4 * f + KE * i + c)

            def ffn_down(b, nf, dw, gbuf, k, after_first=None):
                pe.wait_ge(s[k + "_gt"], nf * b + nf)
                for t in range(NT):
                    for f in range(nf):
                        last = mm(ps[:, 6 + t // 2, (t % 2) * E:(t % 2 + 1) * E], gbuf[:, f, t * P:(t + 1) * P],
                                  dw[:, f, :], start=(f == 0), stop=(f == nf - 1))
                    if t % 2 == 1:
                        last.then_inc(s[k + "_o"], 1)
                    if t == 0 and after_first is not None:
                        after_first()

            def mod_columns(layer, chunks_of_mod):
                for j in chunks_of_mod:
                    for c in range(KE):
                        at = (layer * 12 + j) * B
                        last = mm(ps[:, 7, at:at + B], wmod[layer][:, c, j * P:(j + 1) * P], scT[:, layer, c, :],
                                  start=(c == 0), stop=(c == KE - 1))
                last.then_inc(s["modT_ps"], 1)

            mod_jobs = [(0, b, (2, 5)) for b in range(B)] + [(1, b, (2, 5)) for b in range(B)]
            mod_jobs += [(1, b, (3, 4)) for b in range(B)]

            def mod_rows(u):
                layer, b, kinds = mod_jobs[u]
                if u >= 2:
                    pe.wait_ge(s["bc_sb"], u - 1)
                for i, kind in enumerate(kinds):
                    lo, hi = mod_cols(kind)
                    for c in range(KE):
                        last = mm(ps[:, 2 + u % 2, i * E:(i + 1) * E], sc_bc[:, layer, c, b, :],
                                  wmod[layer][:, c, lo:hi], start=(c == 0), stop=(c == KE - 1))
                last.then_inc(s["bc_ps"], 1)


            def project_qk(b, i):
                for c in range(KE):
                    last = mm(ps[:, 2 + i, :], w0[i % 2][:, c, (i // 2) * P:(i // 2 + 1) * P], hT[:, c, :],
                              start=(c == 0), stop=(c == KE - 1))
                last.then_inc(s["a_qk"], 1)

            def project_v(b):
                for t in range(NT):
                    for c in range(KE):
                        last = mm(ps[:, 6 + t // 2, (t % 2) * E:(t % 2 + 1) * E], hT[:, c, t * P:(t + 1) * P],
                                  w0[2][:, c, :], start=(c == 0), stop=(c == KE - 1))
                    if t % 2 == 1:
                        last.then_inc(s["a_v"], 1)

            def max_units(b, g, bank, u0, u1):
                for u in range(u0, u1):
                    h, qt = HG * g + u // 4, u % 4
                    if u == 0:
                        pe.wait_ge(s[f"a_stack{g}"], (16 * 12) * b + 16 * 12)
                    if u >= 2:
                        pe.wait_ge(s["a_max"], 64 * b + 32 * g + u - 1)
                    mm(ps[:, bank + u % 2, 0:(qt + 1) * P], qst[0:MAX_ROW, h, qt * P:(qt + 1) * P],
                       kst[0:MAX_ROW, h, 0:(qt + 1) * P], start=True, stop=False)
                    mm(ps[:, bank + u % 2, qt * P:(qt + 1) * P], identb[:, :], maskq[:, :], start=False, stop=True)\
                        .then_inc(s["a_s1"], 1)

            def turn_max(b, g):
                pe.wait_ge(s["a_max"], 64 * b + 32 * g + 32)
                tr(ps[0:32, (0, 7)[g], 0:P], rowmax[:, HG * g:HG * g + HG, :].rearrange("p h t -> p (h t)"),
                   ident[:, :]).then_inc(s["a_mT"], 1)

            def a_core(b, more):
                def pv(n):
                    pe.wait_ge(s["a_exp"], H0 * b + 4 * n + 4)
                    if n >= 1:
                        pe.wait_ge(s["a_oT"], 4 * b + n)
                    for kt in range(NT):
                        for j in range(4):
                            h = 4 * n + j
                            last = mm(ps[32 * j:32 * j + 32, 6, kt * P:S], vaug[:, kt, h, :],
                                      probs[:, h % 8, KM_OFF[kt]:KM_OFF[kt] + KM_W[kt]],
                                      start=(kt == 0), stop=(kt == NT - 1))
                    last.then_inc(s["a_pv"], 1)

                def turn(n):
                    pe.wait_ge(s["a_oT"], 4 * b + n + 1)
                    if n >= 1:
                        pe.wait_ge(s["a_ctx"], 4 * b + n)
                    else:
                        pe.wait_ge(s["a_m2"], 2 * b + 2)
                    for t in range(NT):
                        last = tr(ps[:, 7, t * P:(t + 1) * P], oTs[:, n % 2, t * P:(t + 1) * P], ident[:, :])
                    last.then_inc(s["a_oTT"], 1)

                def km_scores(h, between=None):
                    if h >= 2:
                        pe.wait_ge(s["a_exp"], H0 * b + h - 1)
                    if h % HG == 0:
                        pe.wait_ge(s[f"a_mrow{h // HG}"], 48 * b + 48)
                    sc = banks(3 * (h % 2), 3)
                    for i, kt in enumerate((0, 1, 3, 2)):
                        at = KM_OFF[kt]
                        mm(sc[:, at:at + KM_W[kt]], kst[0:STACK, h, kt * P:(kt + 1) * P], qst[0:STACK, h, kt * P:S],
                           start=True, stop=False)
                        last = mm(sc[:, at:at + P], identb[:, :], maskk[:, :], start=False, stop=True)
                        if i == NT - 1:
                            last.then_inc(s["a_s2"], 1)
                        if between is not None:
                            between(i)

                km_scores(0)
                pe.wait_ge(s["a_vc"], 2 * b + 2)
                pe.wait_ge(s["b_x"], NT * b + 1)
                max_units(b, 1, 6, 0, 4)
                for h in range(1, HG):
                    km_scores(h, lambda i, h=h: max_units(b, 1, 6, 4 * h + i, 4 * h + i + 1))
                turn_max(b, 1)
                pv(0)
                pv(1)
                for h in range(HG, H0):
                    km_scores(h)
                    if h == HG:
                        turn(0)
                    if h == HG + 1:
                        turn(1)
                    if h == HG + 5:
                        pv(2)
                turn(2)
                if more:
                    pe.wait_ge(s["xhat_ready"], NT * (2 * b + 2))
                    pe.wait_ge(s["a_exp"], H0 * b + H0 - 1)
                    xhat_T(b + 1, 0, xhat, s["a_xT"])
                pv(3)
                if more:
                    pe.wait_ge(s["a_h"], KE * (b + 1) + KE)
                    project_qk(b + 1, 0)
                turn(3)
                if more:
                    project_qk(b + 1, 1)
                pe.wait_ge(s["a_ctx"], 4 * b + 4)
                xhat_T(b, 0, ctx0, s["a_cT"])
                pe.wait_ge(s["a_cTe"], KE * b + KE)
                for t in range(NT):
                    for c in range(KE):
                        last = mm(ps[:, t // 2, (t % 2) * E:(t % 2 + 1) * E], ctxT[:, c, t * P:(t + 1) * P],
                                  w0[3][:, c, :], start=(c == 0), stop=(c == KE - 1))
                    if t % 2 == 1:
                        last.then_inc(s["a_o"], 1)
                if more:
                    project_qk(b + 1, 2)
                    project_qk(b + 1, 3)
                    project_v(b + 1)

            def b_all(b, more):
                pe.wait_ge(s["xhat_ready"], NT * (2 * b + 3) if more else NT * 2 * B)
                xhat_T(b, B + b, xhat, s["b_xT"])
                pe.wait_ge(s["b_h"], KE * b + KE)
                if more:
                    ffn_up(b, 8, wgate, wup, "b", [("a_r1", 4 * b + 8, 0), ("a_vc", 2 * b + 4, 2)],
                           lambda u: max_units(b + 1, 0, 0, u, u + 1))
                    ffn_down(b, 8, wdown, gT, "b", lambda: turn_max(b + 1, 0))
                else:
                    ffn_up(b, 8, wgate, wup, "b")
                    ffn_down(b, 8, wdown, gT, "b")

            pe.wait_ge(s["in_mod0"], 16)
            pe.wait_ge(s["silu_c"], 1)
            mod_columns(0, range(4))
            pe.wait_ge(s["in_ident"], 16)
            pe.wait_ge(s["xhat_ready"], NT)
            xhat_T(0, 0, xhat, s["a_xT"])
            pe.wait_ge(s["in_wqkv"], 48)
            pe.wait_ge(s["a_h"], KE)
            for i in range(4):
                project_qk(0, i)
            project_v(0)
            pe.wait_ge(s["scbc_done"], 1)
            pe.wait_ge(s["a_r1"], 2)
            pe.wait_ge(s["in_mod0r"], 16)
            for u in range(12):
                if u == 4:
                    pe.wait_ge(s["in_mod1"], 16)
                    pe.wait_ge(s["a_vc"], 2)
                    mod_columns(0, range(6, 10))
                    mod_columns(1, range(4))
                    pe.wait_ge(s["in_const"], 16 * 5)
                    pe.wait_ge(s["in_kaug"], 16)
                    pe.wait_ge(s["preset"], 3)
                mod_rows(u)
                if u >= 4:
                    max_units(0, 0, 0, 4 * (u - 4), 4 * (u - 3))
            turn_max(0, 0)
            pe.wait_ge(s["bc_sb"], 12)
            pe.wait_ge(s["a_r1"], 4)
            pe.wait_ge(s["modT_done"], 6)
            pe.wait_ge(s["in_wo0"], 16)
            pe.wait_ge(s["in_ffn"], 48)
            pe.wait_ge(s["pre_pool"], 2)
            with pe.Fori(0, B - 1) as b:
                a_core(b, True)
                b_all(b, True)
            a_core(B - 1, False)
            b_all(B - 1, False)

            pe.wait_ge(s["in_w1"], 48)
            pe.wait_ge(s["in_small1"], 16 * 5)
            pe.wait_ge(s["b_x"], 1 + TILES)
            pe.wait_ge(s["preset"], 5)

            def rows_of_heads(bank, w, made):
                for c in range(KE):
                    last = mm(ps[0:8, bank, :], w[:, c, :], hT[:, c, :], start=(c == 0), stop=(c == KE - 1))
                last.then_inc(s[made], 1)

            def turn_rows(bank, buf, moved, done, n):
                pe.wait_ge(s[moved], n + 1)
                pe.sem_inc(s["heads_settled"], 1)
                for t in range(NT):
                    last = tr(ps[:, bank, 8 * t:8 * t + 8], buf[:, t * P:(t + 1) * P], ident[0:8, 0:8])
                last.then_inc(s[done], 1)

            def d_turn(b):
                pe.wait_ge(s["d_h"], b + 1)
                xhat_T(b, 0, hs, s["d_yT"])

            def d_rows(b, bank=2):
                pe.wait_ge(s["d_yh"], KE * b + KE)
                rows_of_heads(bank, router, "d_lr")

            def c_turn(b, ready):
                pe.wait_ge(s["xhat_ready"], ready)
                xhat_T(b, 0, xhat, s["c_xT"])

            def c_gates(b):
                pe.wait_ge(s["c_h"], KE * b + KE)
                rows_of_heads(0, wg1, "c_gr")

            def scores(b, i):
                t, hg = i // 2, i % 2
                c0 = P if t == 0 else WIN
                sc4 = banks(2 * (i % 2)).rearrange("p (h n) -> p h n", h=4)
                for hh in range(4):
                    h = 4 * hg + hh
                    mm(sc4[:, hh, c0:], qT1[:, h, t * P:(t + 1) * P], kT1[:, h, t * P - (P - c0):(t + 1) * P],
                       start=True, stop=False)
                    last = mm(sc4[:, hh, c0:], identb[:, :], maskw[:, c0 - WIN:], start=False, stop=True)
                last.then_inc(s["c_s"], 1)

            def c_in(b, d=None):

                def project(bank, w, col, t):
                    for half in range(2):
                        for c in range(KE):
                            last = mm(ps[:, bank + half, :], hT[:, c, t * P:(t + 1) * P],
                                      w[:, c, col + half * 512:col + half * 512 + 512],
                                      start=(c == 0), stop=(c == KE - 1))
                    return last

                def qk_T(u):
                    pe.wait_ge(s["c_qn"], 2 * NT * b + u + 1)
                    if u >= 1:
                        pe.wait_ge(s["c_qe"], 2 * NT * b + u)
                    else:
                        pe.wait_ge(s["c_x"], NT * b + 1)
                    for h in range(H1):
                        last = tr(ps[:, 6 + h // 4, (h % 4) * P:(h % 4 + 1) * P], qn[:, u % 2, h * P:(h + 1) * P],
                                  ident[:, :])
                    last.then_inc(s["c_qT"], 1)

                for t in range(NT):
                    for u, w, col in ((2 * t, wq1, 0), (2 * t + 1, wkv1, 0)):
                        if u >= 2:
                            pe.wait_ge(s["c_qn"], 2 * NT * b + u - 1)
                        project(2 + 2 * (u % 2), w, col, t).then_inc(s["c_p"], 1)
                        if u == 0:
                            turn_rows(1, qn[0:H1, 1, 0:S], "c_gx", "c_gp", b)
                        if u >= 2:
                            qk_T(u - 2)
                    if t == 0:
                        pe.wait_ge(s["c_g1"], b + 1)
                    else:
                        pe.wait_ge(s["c_ve"], NT * b + t)
                    project(0, wkv1, INNER, t).then_inc(s["c_v"], 1)
                qk_T(2 * NT - 2)
                pe.wait_ge(s["c_ve"], NT * b + NT)
                if d is not None:
                    d_turn(d)
                qk_T(2 * NT - 1)
                if d is not None:
                    d_rows(d)
                scores(b, 0)
                if d is not None:
                    turn_rows(4, lrows, "d_lx", "d_l", d)

            def c_core(b, more):
                for i in range(1, 2 * NT + 3):
                    if i < 2 * NT:
                        if i == 1:
                            pe.wait_ge(s["c_qe"], 2 * NT * b + 2 * NT)
                        if i >= 2:
                            pe.wait_ge(s["c_e"], 8 * NT * b + 4 * (i - 1))
                        scores(b, i)
                    if 2 <= i <= 2 * NT + 1:
                        w = i - 2
                        t, hg = w // 2, w % 2
                        k0 = 1 if t == 0 else 0
                        pe.wait_ge(s["c_pTe"], 2 * NT * b + w + 1)
                        if w >= 1:
                            pe.wait_ge(s["c_oe"], 2 * NT * b + w)
                        for hh in range(4):
                            h = 4 * hg + hh
                            for k in range(k0, 2):
                                last = mm(ps[:, 6, hh * P:(hh + 1) * P], v1[:, t - 1 + k, h * P:(h + 1) * P],
                                          pT1[:, w % 2, hh, k, :], start=(k == k0), stop=(k == 1))
                        last.then_inc(s["c_o"], 1)
                    if i >= 4 and i % 2 == 0:
                        t = i // 2 - 2
                        pe.wait_ge(s["c_oe"], 2 * NT * b + 2 * t + 2)
                        pe.wait_ge(s["c_x"], NT * b + t + 1)
                        for h in range(H1):
                            last = mm(ps[:, 7, 0:E], oT1[:, t % 2, h, :], wo1[:, h, :],
                                      start=(h == 0), stop=(h == H1 - 1))
                        last.then_inc(s["c_w"], 1)
                    if 1 <= i <= 2 * NT:
                        w = i - 1
                        k0 = 1 if w < 2 else 0
                        pe.wait_ge(s["c_pn"], 8 * NT * b + 4 * w + 4)
                        if w >= 1:
                            pe.wait_ge(s["c_pTe"], 2 * NT * b + w)
                        else:
                            pe.wait_ge(s["d_lc"], b + 1)
                        for hh in range(4):
                            for k in range(k0, 2):
                                last = tr(banks(4)[:, (2 * hh + k) * P:(2 * hh + k + 1) * P],
                                          pr1[:, w % 2, hh, k * P:(k + 1) * P], ident[:, :])
                        last.then_inc(s["c_pT"], 1)
                    if more and i == 2 * NT:
                        c_turn(b + 1, NT * (2 * B + 2 + 2 * b))
                    if more and i == 2 * NT + 1:
                        c_gates(b + 1)

            c_turn(0, NT * (2 * B + 1))
            c_gates(0)
            c_in(0)
            with pe.Fori(0, B - 1) as b:
                c_core(b, True)
                c_in(b + 1, b)
            c_core(B - 1, False)

            def ranks():
                pe.wait_ge(s["r_v"], 7)
                last = mm(ps[:, 0, 0:(TILES + 1) * NEXP], before[:, :], r_ohx.rearrange("p t e -> p (t e)"),
                          start=True, stop=False)
                for t in range(TILES):
                    n = TILES - t
                    last = mm(ps[:, 0, (t + 1) * NEXP:(TILES + 1) * NEXP].rearrange("p (t e) -> p t e", e=NEXP),
                              ones_b[:, :], r_ohx[:, t:t + 1, :].to_broadcast([P, n, NEXP]),
                              start=False, stop=(t == TILES - 1))
                last.then_inc(s["r_R"], 1)

            def shared_T(m):
                pe.wait_ge(s["d_hs"], m + 1)
                xhat_T(m, 0, hs, s["d_xT"])

            def route_between(u):
                if u == 3:
                    turn_rows(1, lrows, "d_lx", "d_l", B - 1)
                if u == 7:
                    ranks()

            pe.wait_ge(s["in_sh"], 48)
            ffn_up(0, 4, shg, shu, "d", [("c_x", 1 + TILES, 2)])
            d_turn(B - 1)
            ffn_down(0, 4, shd, gTs, "d")
            d_rows(B - 1, 0)
            ffn_up(1, 4, shg, shu, "d", between=route_between)
            for m in range(B - 2):
                if m == 0:
                    pe.wait_ge(s["r_read"], 1)
                shared_T(m)
                ffn_down(m + 1, 4, shd, gTs, "d")
                pe.wait_ge(s["d_hT"], KE * m + KE)
                ffn_up(m + 2, 4, shg, shu, "d")
            ffn_down(B - 1, 4, shd, gTs, "d")

            pe.sem_inc(s["m_xT"], 2)
            pe.wait_ge(s["in_exp"], 16 * 2 * NEXP)
            pe.wait_ge(s["r_pos_ok"], 1)

            def slot_T(slot, j, i, first=False):
                if not first:
                    pe.wait_ge(s["m_xTe"], slot)
                pe.wait_ge(s[f"m_in{j}"], 16 * i + 16)
                for c in range(KE):
                    last = tr(ps[:, 0, c * P:(c + 1) * P], xs[:, j, c * P:(c + 1) * P], ident[:, :])
                last.then_inc(s["m_xT"], 1)

            def expert_of(slot):
                return pe.value_load(slot_e[0:1, bass.ds(slot, 1)], min_val=0, max_val=NEXP - 1)

            def slot_gu(slot, j):
                e = expert_of(slot)
                pe.wait_ge(s["m_xTe"], slot + 1)
                for half in range(2):
                    for c in range(KE):
                        last = mm(ps[:, 1 + 2 * j + half, :], xsT[:, j, c, :],
                                  wgu[:, c, bass.ds(e * (2 * FE) + half * FE, FE)],
                                  start=(c == 0), stop=(c == KE - 1))
                last.then_inc(s["m_gu"], 1)

            def slot_aT(slot, j, first=False):
                pe.wait_ge(s["m_a"], slot + 1)
                if not first:
                    pe.wait_ge(s["m_aTe"], slot)
                for f in range(4):
                    last = tr(ps[:, 5, f * P:(f + 1) * P], acts[:, j, f * P:(f + 1) * P], ident[:, :])
                last.then_inc(s["m_aT"], 1)

            def slot_down(slot, j):
                e = expert_of(slot)
                pe.wait_ge(s["m_aTe"], slot + 1)
                for f in range(4):
                    last = mm(ps[:, 6 + j, 0:E], actT[:, j, f, :], wdn[:, f, bass.ds(e * E, E)],
                              start=(f == 0), stop=(f == 3))
                last.then_inc(s["m_d"], 1)

            slot_T(0, 0, 0, first=True)
            slot_T(1, 1, 0)
            slot_gu(0, 0)
            slot_T(2, 0, 1)
            slot_gu(1, 1)
            slot_aT(0, 0, first=True)
            with pe.Fori(0, SLOT_PAIRS) as i:
                slot_T(2 * i + 3, 1, i + 1)
                slot_gu(2 * i + 2, 0)
                slot_aT(2 * i + 1, 1)
                slot_down(2 * i, 0)
                slot_T(2 * i + 4, 0, i + 2)
                slot_gu(2 * i + 3, 1)
                slot_aT(2 * i + 2, 0)
                slot_down(2 * i + 1, 1)
            slot_gu(SLOTS - 1, 0)
            slot_aT(SLOTS - 2, 1)
            slot_down(SLOTS - 3, 0)
            slot_aT(SLOTS - 1, 0)
            slot_down(SLOTS - 2, 1)
            slot_down(SLOTS - 1, 0)


def _bf16_bits(v):
    import numpy as np
    return (np.ascontiguousarray(v, dtype=np.float32).view(np.uint32) >> 16).astype(np.uint16)


def _alibi_rows():
    import numpy as np
    slopes = (2.0 ** (-8.0 * np.arange(1, H0 + 1) / H0)).astype(np.float32)
    left = slopes[:, None] * np.arange(S, dtype=np.float32)[None, :]
    rows = np.full((STACK - BIAS_ROW, H0, S), -1.0, dtype=np.float32)
    for a in range(3):
        rows[a] = (left.view(np.uint32) & np.uint32(0xFFFF0000)).view(np.float32)
        left = left - rows[a]
    return _bf16_bits(rows)


def _constants():
    import numpy as np
    i, j = np.arange(P)[:, None], np.arange(P)[None, :]
    far = np.float32(-1e30)
    jw = np.arange(-WIN, P)[None, :]
    cond = {
        "maskq": np.where(j <= i, 0, far),
        "maskk": np.where(i <= j, 0, far),
        "maskw": np.where((i - jw >= 0) & (i - jw <= WIN), 0, far),
        "before": np.where(i < j, 1, 0),
        "identb": np.eye(P),
    }
    c = {k: _bf16_bits(v) for k, v in cond.items()}
    c["ident"] = np.eye(P, dtype=np.float32)
    c["kaug"] = _alibi_rows()

    def rows(a):
        return np.ascontiguousarray(np.broadcast_to(a.astype(np.float32)[None], (P,) + a.shape))

    c["thr"] = rows(np.broadcast_to(P * np.arange(TILES), (NEXP, TILES)))
    c["iota"] = rows(np.broadcast_to(np.arange(SLOTS)[:, None], (SLOTS, NEXP)))
    c["incl"] = rows(np.tril(np.ones((NEXP, NEXP))))
    c["w8"] = rows(np.broadcast_to(NEXP - np.arange(NEXP), (TILES, NEXP)))
    return c


def kernel(**inputs):
    import numpy as np
    import concourse.bacc as bacc
    from concourse.bass_utils import run_bass_kernel_spmd

    a = {k: np.asarray(v) for k, v in inputs.items()}
    c = _constants()

    def by_dim(w):
        return w.reshape(E, 2, HG, D0).transpose(0, 1, 3, 2).reshape(E, E)

    def per_partition(v):
        return np.broadcast_to(v[None, :], (P, v.shape[0]))

    cT = np.stack([a["L0_c"].T.reshape(KE, P, B), a["L1_c"].T.reshape(KE, P, B)]).transpose(2, 0, 1, 3)
    arrays = [
        ("x", a["L0_attn_x"]), ("cT", cT), ("wmod0", a["L0_wmod"]), ("wmod1", a["L1_wmod"]),
        ("wq0", by_dim(a["L0_attn_Wq"])), ("wk0", by_dim(a["L0_attn_Wk"])), ("wv0", a["L0_attn_Wv"]),
        ("wo0", a["L0_attn_Wo"]), ("bo", per_partition(a["L0_attn_bo"])),
        ("wgate", a["L0_ffn_w_gate"].T), ("wup", a["L0_ffn_w_up"].T), ("wdown", a["L0_ffn_w_down"].T),
        ("wq1", a["L1_attn_Wq"].T), ("wkv1", a["L1_attn_Wkv"].T),
        ("qs", a["L1_attn_q_scale"][:, None]), ("ks", a["L1_attn_k_scale"][:, None]),
        ("wg1", a["L1_attn_Wg"].T), ("bg", a["L1_attn_bg"][:, None]), ("wo1", a["L1_attn_Wo"].T),
        ("router", a["L1_ffn_router_w"].T), ("gu", a["L1_ffn_gate_up_proj"]), ("dn", a["L1_ffn_down_proj"]),
        ("sg", a["L1_ffn_shared_gate_w"]), ("su", a["L1_ffn_shared_up_w"]), ("sd", a["L1_ffn_shared_down_w"]),
        ("ident", c["ident"]), ("identb", c["identb"]), ("maskq", c["maskq"]), ("maskk", c["maskk"]),
        ("maskw", c["maskw"]), ("before", c["before"]), ("kaug", c["kaug"]), ("thr", c["thr"]),
        ("iota", c["iota"]), ("incl", c["incl"]), ("w8", c["w8"]),
    ]
    nc = bacc.Bacc("TRN2", target_bir_lowering=False, num_devices=1)
    feeds, aps = {}, []
    for name, v in arrays:
        v = np.ascontiguousarray(v)
        feeds[f"in_{name}"] = v
        aps.append(nc.dram_tensor(f"in_{name}", v.shape, mybir.dt.from_np(v.dtype), kind="ExternalInput").ap())
    out = nc.dram_tensor("out_x", (B, S, E), F32, kind="ExternalOutput").ap()
    program(nc, *aps, out)
    r = run_bass_kernel_spmd(nc, [feeds], core_ids=[0])
    return r.results[0]["out_x"]
```

```python
from contextlib import ExitStack

import concourse.bass as bass
from concourse import mybir

ALU = mybir.AluOpType
ACT = mybir.ActivationFunctionType
AX_X = mybir.AxisListType.X
F32 = mybir.dt.float32
BF16 = mybir.dt.bfloat16
F32R = mybir.dt.float32r
I32 = mybir.dt.int32

P = 128
B, S, E = 4, 512, 256
NT = S // P
TILES = B * NT
KE = E // P
H0, D0 = 16, 16
HG = H0 // 2
F0 = 1024
H1, D1 = 8, 128
INNER = H1 * D1
WIN = 64
NEXP, FE = 8, 512
SLOTS = TILES + NEXP - 1
SLOT_PAIRS = (SLOTS - 3) // 2
EPS = 1e-5

Q_PARTS = [0, 0, 1, 1, 0, 2]
K_PARTS = [0, 1, 0, 1, 2, 0]
BIAS_ROW = 16 * len(Q_PARTS)
MAX_ROW = BIAS_ROW + 3
STACK = MAX_ROW + 3

QT_ORDER = (3, 1, 0, 2)
KM_W = [S - P * kt for kt in range(NT)]
KM_OFF = [0, 512, 1024, 896]
KM = sum(KM_W)

GATHERS = (0, 5, 10, 14, TILES)


def gather_group(t):
    return max(g for g in range(4) if GATHERS[g] <= t)


def program(nc, x_d, cT_d, wmod0_d, wmod1_d, wq0_d, wk0_d, wv0_d, wo0_d, bo_d, wgate_d, wup_d, wdown_d,
            wq1_d, wkv1_d, qs_d, ks_d, wg1_d, bg_d, wo1_d, router_d, gu_d, dn_d, sg_d, su_d, sd_d,
            ident_d, identb_d, maskq_d, maskk_d, maskw_d, before_d, kaug_d, thr_d, iota_d, incl_d, w8_d, out_d):
    rows_d = nc.dram_tensor("routed_rows", (SLOTS * P, E), F32).ap()
    yrows_d = nc.dram_tensor("routed_out", (SLOTS * P, E), F32).ap()
    mod_rows_d = nc.dram_tensor("mod_rows_kept", (1, 16 * E), F32).ap()
    h_kept_d = nc.dram_tensor("h_kept", ((B - 1) * P, NT * E), F32).ap()

    with ExitStack() as ctx:
        def sb(name, shape, dt=F32):
            return ctx.enter_context(nc.sbuf_tensor(name, shape, dt))

        def sb_both(name, words, parts):
            with nc.sbuf_tensor(name, [P, words], F32) as full:
                pass
            views, at = [], 0
            for first, n in parts:
                if first > at:
                    sb(f"{name}_f32_{at}", [P, first - at])
                views.append(sb(f"{name}_parts_{first}", [P, n], F32R))
                at = first + n
            if at < words:
                sb(f"{name}_f32_{at}", [P, words - at])
            return [full] + views

        def sem(name):
            return ctx.enter_context(nc.semaphore(name))

        x_all = sb("x_all", [P, TILES * E])
        xhat = sb("xhat", [P, NT, E])
        hT = sb("hT", [P, KE, S])
        gates_flat, hT_hi, w0_hi = sb_both("gates_bc", 24 * E, [(0, KE * S), (8 * E, 16 * E)])
        gates_bc = gates_flat[:, :].rearrange("p (k e) -> p k e", e=E)
        modT = sb("modT", [P, 2, 12, B])
        ident = sb("ident", [P, P])
        identb = sb("identb", [P, P], BF16)
        maskq = sb("maskq", [P, P], BF16)
        maskk = sb("maskk", [P, P], BF16)
        maskw = sb("maskw", [P, WIN + P], BF16)
        before = sb("before", [P, P], BF16)
        ones_b = sb("ones_b", [P, P], BF16)
        stats = sb("stats", [P, NT, 6])
        lsum = sb("lsum", [P, NT, 2])
        ldif = sb("ldif", [P, NT])
        lvar = sb("lvar", [P, NT])
        lsq = sb("lsq", [P, NT])
        mean = sb("mean", [P, NT])
        vareps = sb("vareps", [P, NT])
        rstd = sb("rstd", [P, NT])
        minus_half = sb("minus_half", [P, 8])
        qscale = sb("qscale", [P, 1])
        kscale = sb("kscale", [P, 1])
        scT = sb("scT", [P, 2, KE, B])
        cT = sb("cT", [P, 2, KE, B])
        small = sb("small", [P, 256])

        AR = 30720
        arena, arena_r, h0_parts = sb_both("arena", AR, [(0, 2 * 6144), (20480, 2 * KE * S)])

        def ar(off, n):
            return arena[:, off:off + n]

        o = 0
        qst = ar(o, 4096).bitcast(BF16).rearrange("p (h n) -> p h n", h=H0); o += 4096
        kst = ar(o, 4096).bitcast(BF16).rearrange("p (h n) -> p h n", h=H0); o += 4096
        parts = ar(o, 3072).bitcast(BF16).rearrange("p (i a n) -> p i a n", i=4, a=3); o += 3072
        resid = ar(o, 2048).rearrange("p (i n) -> p i n", i=4); o += 2048
        vaug = ar(o, 2048).rearrange("p (t h c) -> p t h c", t=NT, h=H0); o += 2048
        probs = ar(o, 8 * KM).rearrange("p (h n) -> p h n", h=8); o += 8 * KM
        ctx0 = ar(o, 1024).rearrange("p (t e) -> p t e", t=NT); o += 1024
        ctxT = ar(o, 1024).rearrange("p (c n) -> p c n", c=KE); o += 1024
        oTs = ar(o, 1024).rearrange("p (i n) -> p i n", i=2); o += 1024
        gabo = ar(o, 1024).rearrange("p (b e) -> p b e", b=B); o += 1024
        rowmax = ar(o, 64).rearrange("p (h t) -> p h t", h=H0); o += 64
        rden = ar(o, 32).rearrange("p (i n) -> p i n", i=2); o += 32
        mres = ar(o, 256).rearrange("p (g n) -> p g n", g=2); o += 256
        mparts = ar(o, 384).bitcast(BF16).rearrange("p (g a n) -> p g a n", g=2, a=3); o += 384
        assert o <= AR
        zero_rows = ar(AR - 256, 256)
        assert o <= AR - 256
        bo_bc = ctxT[:, 0, 0:256]
        wmod = [ar(15360 + 3072 * i, 3072).rearrange("p (c n) -> p c n", c=KE) for i in range(2)]
        sc_bc = ar(21504, 2048).rearrange("p (l c b n) -> p l c b n", l=2, c=KE, b=B)
        guard = [oTs[:, 0, :], oTs[:, 1, :]], [ctx0[:, 0:2, :].rearrange("p t e -> p (t e)"),
                                               ctx0[:, 2:4, :].rearrange("p t e -> p (t e)")]
        gT = ar(15360, 4096).rearrange("p (f n) -> p f n", f=8)
        sgT = ar(19456, 1024).rearrange("p (i n) -> p i n", i=2)
        utmp = sb("utmp", [P, 2, E])
        o = 0
        w1_hi = arena_r[:, 0:6144].rearrange("p (c n) -> p c n", c=KE); o += 6144
        w1_raw, w1_lo = (a[:, o:o + 6144] for a in (arena, arena_r)); o += 6144
        w1_pieces = [(w1_raw[:, i:i + 1024], arena_r[:, i:i + 1024], w1_lo[:, i:i + 1024])
                     for i in range(0, 6144, 1024)]
        w1_raw = w1_raw.rearrange("p (c n) -> p c n", c=KE)
        w1_lo = w1_lo.rearrange("p (c n) -> p c n", c=KE)
        wo1 = ar(o, 2048).rearrange("p (h n) -> p h n", h=H1); o += 2048
        kT1 = ar(o, 4096).rearrange("p (h n) -> p h n", h=H1); o += 4096
        v1 = ar(o, 4096).rearrange("p (t n) -> p t n", t=NT); o += 4096
        qn = ar(o, 2048).rearrange("p (i n) -> p i n", i=2); o += 2048
        sq = ar(o, 2048).rearrange("p (i n) -> p i n", i=2); o += 2048
        pr1 = ar(o, 2048).rearrange("p (i h n) -> p i h n", i=2, h=4); o += 2048
        pT1 = ar(o, 2048).rearrange("p (i h k n) -> p i h k n", i=2, h=4, k=2); o += 2048
        assert o <= AR
        o = 0
        shg = ar(o, 1024).rearrange("p (c n) -> p c n", c=KE); o += 1024
        shu = ar(o, 1024).rearrange("p (c n) -> p c n", c=KE); o += 1024
        shd = ar(o, 1024).rearrange("p (f n) -> p f n", f=4); o += 1024
        h_all = ar(o, 4096); o += 4096
        h_of = h_all.rearrange("p (b t e) -> p b t e", b=B, t=NT)
        gTs = ar(o, 2048).rearrange("p (f n) -> p f n", f=4); o += 2048
        xr_all = ar(o, 4096); o += 4096
        assert o <= 14336
        wgu = ar(14336, 16384).rearrange("p (c n) -> p c n", c=KE)
        sgs = ar(0, 1024).rearrange("p (j n) -> p j n", j=2)
        acts = ar(1024, 1024).rearrange("p (j n) -> p j n", j=2)
        actT = ar(2048, 1024).rearrange("p (j f n) -> p j f n", j=2, f=4)
        yg = h_all.rearrange("p (t e) -> p t e", t=TILES)

        WA, w0_lo, hT_lo = sb_both("WA", 8192, [(2048, 4096), (6144, KE * S)])

        def wa(off, n):
            return WA[:, off:off + n]

        w0 = [wa(512 * i, 512).rearrange("p (c n) -> p c n", c=KE) for i in range(4)]
        wgate = wa(2048, 2048).rearrange("p (c n) -> p c n", c=KE)
        wup = wa(4096, 2048).rearrange("p (c n) -> p c n", c=KE)
        w0_pieces = [(wa(2048 + i, 1024), w0_hi[:, i:i + 1024], w0_lo[:, i:i + 1024]) for i in range(0, 4096, 1024)]
        wgate_parts, wup_parts = ([w[:, i:i + 2048].rearrange("p (c n) -> p c n", c=KE) for w in (w0_hi, w0_lo)]
                                  for i in (0, 2048))
        h0_hi, h0_lo = (h0_parts[:, i:i + KE * S].rearrange("p (c n) -> p c n", c=KE) for i in (0, KE * S))
        wdown = wa(6144, 2048).rearrange("p (f n) -> p f n", f=8)
        qT1 = wa(0, 4096).rearrange("p (h n) -> p h n", h=H1)
        oT1 = wa(4096, 2048).rearrange("p (i h n) -> p i h n", i=2, h=H1)
        hT_lo, hT_hi = (a[:, :].rearrange("p (c n) -> p c n", c=KE) for a in (hT_lo, hT_hi))
        hs = wa(7168, 1024).rearrange("p (t e) -> p t e", t=NT)
        wdn = wa(0, 8192).rearrange("p (c n) -> p c n", c=4)
        sgTs = gates_bc[:, 16:20, :].rearrange("p k e -> p (k e)").rearrange("p (i n) -> p i n", i=2)
        old = gates_bc[:, 0:8, :].rearrange("p k e -> p (k e)")
        xs = old[:, 0:512].rearrange("p (j e) -> p j e", j=2)
        xsT = old[:, 512:1024].rearrange("p (j c n) -> p j c n", j=2, c=KE)
        lrows = old[0:NEXP, 1024:1536]
        ys = old[:, 1024:1536].rearrange("p (j e) -> p j e", j=2)
        wg1 = sb("wg1", [P, KE, H1])
        negbg = sb("negbg", [P, 1])
        router = sb("router", [P, KE, NEXP])
        logits = sb("logits", [P, TILES * NEXP])
        g1 = sb("g1", [P, NT * H1])
        ssq = sb("ssq", [P, 2, H1])
        rnorm = sb("rnorm", [P, 2, H1])
        nmax1 = sb("nmax1", [P, 2, 4])
        rsum1 = sb("rsum1", [P, 2, 4])
        rinv1 = sb("rinv1", [P, 2, 4])
        pos_i = sb("pos_i", [P, TILES], I32)
        slot_e = sb("slot_e", [P, SLOTS], I32)
        score = sb("score", [P, TILES])
        r_eq = small[:, 0:128].rearrange("p (t e) -> p t e", t=TILES)
        r_oh = small[:, 128:256].rearrange("p (t e) -> p t e", t=TILES)
        r_ohx = old[:, 0:68].bitcast(BF16).rearrange("p (t e) -> p t e", t=TILES + 1)
        r_a = old[:, 256:512]
        r_n, r_nt, r_end, r_base = (old[:, 512 + 8 * i:520 + 8 * i] for i in range(4))
        r_m, r_pos, r_f = old[:, 544:560], old[:, 560:576], old[:, 576:576 + SLOTS]
        r_thr = old[:, 1536:1664].rearrange("p (e j) -> p e j", e=NEXP)
        r_iota = old[:, 1664:1664 + SLOTS * NEXP].rearrange("p (s e) -> p s e", e=NEXP)
        r_incl = old[:, 1856:1920].rearrange("p (e j) -> p e j", e=NEXP)
        r_w8 = old[:, 1920:2048].rearrange("p (t e) -> p t e", t=TILES)

        ps = ctx.enter_context(nc.psum_tensor("ps", [P, 8, 512], F32))
        ps_flat = ps[:, :, :].rearrange("p b n -> p (b n)")

        def banks(i, n=2):
            return ps_flat[:, 512 * i:512 * (i + n)]

        def mod_cols(kind):
            return kind * E, kind * E + E
        G0, G1, SC1 = 0, 8, 16

        names = """in_x0 in_x in_c in_mod0 in_mod1 in_ident in_const in_wqkv in_wo0 in_ffn in_w1 w_high w_low in_sh
        rows_kept in_exp in_rt zfill setup_v settled silu_c scbc_done modT_ps modT_done bc_ps bc_sb bc_sb2
        guard_v size_ready gabo_done pre_pool preset ln_stats ln_mv ln_var ln_rstd xhat_ready a_xT a_h a_qk a_p1
        a_r1 a_p2 a_p3 a_stack0 a_stack1 a_v a_vc a_s1 a_max a_mT a_m1 a_m2 a_m3 a_m4 a_mrow0 a_mrow1 a_s2 a_exp
        a_pv a_oT a_oTT a_rc a_ctx a_cT a_cTe a_o a_tmp a_x a_xb b_xT b_h b_g b_u b_sg b_gt b_o b_tmp b_x c_xT
        h_high c_h h_low c_gr c_gx c_gp c_g1 c_gate c_p c_sq c_ss c_rk0 c_rk c_qn c_qT c_qe c_v c_ve c_s c_mx
        c_e c_ri c_pn c_pT c_pTe c_o c_oe c_w c_tmp c_x d_h0 d_h d_kept d_yT d_yh d_lr d_lx d_l d_lc d_xT d_hT
        d_g d_u d_sg d_gt d_o d_tmp d_x r_v r_read r_R r_exp r_xr r_scatter r_pos_ok m_in0 m_in1 m_xT m_xTe m_gu
        m_sg m_a m_aT m_aTe m_d m_y m_out0 m_out1 m_gather0 m_gather1 m_gather2 m_gather3 f_tmp f_x f_out""".split()
        identb_d, maskq_d, maskk_d, maskw_d, before_d, kaug_d = (
            a.bitcast(BF16) for a in (identb_d, maskq_d, maskk_d, maskw_d, before_d, kaug_d))
        s = {n: sem("s_" + n) for n in names}

        block = ctx.enter_context(nc.Block())

        x_rows = x_d.rearrange("b (t p) e -> p b t e", p=P)
        out_rows = out_d.rearrange("b (t p) e -> p (b t) e", p=P)

        def chunks(w):
            return w.rearrange("(c p) n -> p c n", p=P)

        @block.sync
        def _(sp):
            sp.dma_start(cT[:, :, :, :], cT_d).then_inc(s["in_c"], 16)
            sp.dma_start(x_all[:, 0:NT * E].rearrange("p (t e) -> p t e", e=E), x_rows[:, 0]).then_inc(s["in_x0"], 16)
            sp.dma_start(ident[:, :], ident_d).then_inc(s["in_ident"], 16)
            sp.dma_start(wmod[0][:, :, 0:2 * E], chunks(wmod0_d)[:, :, 0:2 * E]).then_inc(s["in_mod0"], 16)
            for i, w in enumerate((wq0_d, wk0_d, wv0_d)):
                sp.dma_start(w0[i], chunks(w)).then_inc(s["in_wqkv"], 16)
            sp.dma_start(wmod[0][:, :, 2 * E:], chunks(wmod0_d)[:, :, 2 * E:]).then_inc(s["in_mod1"], 16)
            sp.dma_start(kst[BIAS_ROW:STACK], kaug_d).then_inc(s["in_const"], 16)
            for dst, src in ((identb[:, :], identb_d), (maskq[:, :], maskq_d), (maskk[:, :], maskk_d),
                             (maskw[:, :], maskw_d), (before[:, :], before_d)):
                sp.dma_start(dst, src).then_inc(s["in_const"], 16)
            sp.dma_start(wmod[1], chunks(wmod1_d)).then_inc(s["in_mod1"], 16)
            sp.dma_start(w0[3], chunks(wo0_d)).then_inc(s["in_wo0"], 16)
            sp.dma_start(bo_bc, bo_d).then_inc(s["in_wo0"], 16)

            def stack(b):
                for i in range(4):
                    g, st, pt = i // 2, (qst, kst)[i % 2], (Q_PARTS, K_PARTS)[i % 2]
                    sp.wait_ge(s["a_p3"], 4 * b + i + 1)
                    for r, part in enumerate(pt):
                        sp.dma_start(st[16 * r:16 * r + 16, HG * g:HG * g + HG, :], parts[:, i, part, :])\
                            .then_inc(s[f"a_stack{g}"], 16)

            def max_rows(b, g):
                sp.wait_ge(s["a_m4"], 2 * b + g + 1)
                for a in range(3):
                    sp.dma_start(qst[MAX_ROW + a:MAX_ROW + a + 1, HG * g:HG * g + HG, :],
                                 mparts[0:32, g, a, :]).then_inc(s[f"a_mrow{g}"], 16)

            stack(0)
            for b in range(1, B):
                sp.dma_start(x_all[:, b * NT * E:(b + 1) * NT * E].rearrange("p (t e) -> p t e", e=E),
                             x_rows[:, b]).then_inc(s["in_x"], 16)
            sp.dma_start(wgate, chunks(wgate_d)).then_inc(s["in_ffn"], 16)
            sp.dma_start(wup, chunks(wup_d)).then_inc(s["in_ffn"], 16)
            sp.dma_start(wdown, chunks(wdown_d)).then_inc(s["in_ffn"], 16)
            sp.wait_ge(s["bc_sb"], 4)
            sp.wait_ge(s["bc_sb2"], 4)
            sp.dma_start(mod_rows_d, gates_flat[0:1, 8 * E:24 * E]).then_inc(s["rows_kept"], 16)
            max_rows(0, 0)
            for dst, src in ((wg1[:, :, :], chunks(wg1_d)), (negbg[0:H1, :], bg_d), (qscale[:, :], qs_d),
                             (kscale[:, :], ks_d), (router[:, :, :], chunks(router_d))):
                sp.dma_start(dst, src).then_inc(s["in_w1"], 16)
            sp.wait_ge(s["pre_pool"], 3)
            for j in range(SLOTS):
                sp.dma_start(rows_d[j * P:(j + 1) * P, :], zero_rows).then_inc(s["zfill"], 16)
            with sp.Fori(0, B - 1) as b:
                max_rows(b, 1)
                stack(b + 1)
                max_rows(b + 1, 0)
            max_rows(B - 1, 1)

            sp.wait_ge(s["a_x"], 1 + TILES)
            sp.wait_ge(s["zfill"], 16 * SLOTS)
            sp.dma_start(w1_raw[:, :, 0:INNER], chunks(wq1_d)).then_inc(s["in_w1"], 16)
            sp.dma_start(w1_raw[:, :, INNER:], chunks(wkv1_d)).then_inc(s["in_w1"], 16)
            sp.dma_start(wo1, chunks(wo1_d)).then_inc(s["in_w1"], 16)
            sp.wait_ge(s["b_u"], 8 * B)
            sp.wait_ge(s["rows_kept"], 16)
            sp.dma_start(gates_flat[:, 8 * E:24 * E], mod_rows_d.to_broadcast([P, 16 * E]))\
                .then_inc(s["rows_kept"], 16)
            sp.wait_ge(s["b_x"], 1 + TILES)
            for dst, src in ((r_thr, thr_d), (r_iota, iota_d), (r_incl, incl_d), (r_w8, w8_d)):
                sp.dma_start(dst, src).then_inc(s["in_rt"], 16)
            with sp.Fori(0, B - 1) as b:
                sp.wait_ge(s["d_h"], 2 * b + 2)
                sp.dma_start(h_kept_d[bass.ds(b * P, P), :], hs.rearrange("p t e -> p (t e)"))\
                    .then_inc(s["d_kept"], 16)
            sp.wait_ge(s["c_v"], TILES)
            sp.dma_start(shg, chunks(sg_d)).then_inc(s["in_sh"], 16)
            sp.dma_start(shu, chunks(su_d)).then_inc(s["in_sh"], 16)
            sp.dma_start(shd, chunks(sd_d)).then_inc(s["in_sh"], 16)
            sp.wait_ge(s["d_kept"], 16 * B)
            sp.dma_start(h_all[:, 0:(B - 1) * NT * E].rearrange("p (b n) -> p b n", b=B - 1),
                         h_kept_d.rearrange("(b p) n -> p b n", p=P)).then_inc(s["in_rt"], 16)
            sp.wait_ge(s["c_x"], 1 + TILES)
            for e in range(NEXP):
                sp.dma_start(wgu[:, :, e * 2 * FE:(e + 1) * 2 * FE], chunks(gu_d[e])).then_inc(s["in_exp"], 16)
                sp.dma_start(wdn[:, :, e * E:(e + 1) * E], chunks(dn_d[e])).then_inc(s["in_exp"], 16)

            sp.wait_ge(s["r_scatter"], 16 * TILES)

            def rows_in(slot, j):
                sp.wait_ge(s["m_xT"], slot + 1)
                sp.dma_start(xs[:, j, :], rows_d[bass.ds(slot * P, P), :]).then_inc(s[f"m_in{j}"], 16)

            for slot in range(3):
                rows_in(slot, slot % 2)
            with sp.Fori(0, SLOT_PAIRS) as i:
                rows_in(2 * i + 3, 1)
                rows_in(2 * i + 4, 0)

            for t in range(TILES):
                sp.wait_ge(s["f_x"], t + 1)
                sp.dma_start(out_rows[:, t], x_all[:, t * E:(t + 1) * E]).then_inc(s["f_out"], 16)
            sp.wait_ge(s["f_out"], 16 * TILES)

        @block.gpsimd
        def _(pool):
            gp = nc.gpsimd

            def ln_pool(n):
                pool.wait_ge(s["ln_var"], n + 1)
                gp.tensor_tensor(rstd[:, :], vareps[:, :], minus_half[:, 0:NT], ALU.pow).then_inc(s["ln_rstd"], 1)

            gp.memset(minus_half[:, :], -0.5).then_inc(s["pre_pool"], 1)
            gp.memset(zero_rows, 0.0).then_inc(s["pre_pool"], 1)
            gp.memset(ones_b[:, :], 1.0).then_inc(s["pre_pool"], 1)
            pool.wait_ge(s["pre_pool"], 3)
            ln_pool(0)
            pool.wait_ge(s["ln_rstd"], 1)
            gp.memset(qst[BIAS_ROW:MAX_ROW], 1.0).then_inc(s["preset"], 1)
            pool.wait_ge(s["preset"], 1)
            gp.memset(vaug[:, :, :, D0:32], 0.0).then_inc(s["preset"], 1)
            pool.wait_ge(s["preset"], 2)
            gp.memset(vaug[:, :, :, D0:D0 + 1], 1.0).then_inc(s["preset"], 1)

            def third_parts(b, ln=None):
                for i in range(4):
                    if i == 2 and ln is not None:
                        ln_pool(ln)
                    pool.wait_ge(s["a_p2"], 4 * b + i + 1)
                    gp.tensor_tensor(parts[:, i, 2, :], resid[:, i, :], parts[:, i, 1, :], ALU.subtract)\
                        .then_inc(s["a_p3"], 1)

            def residual_bias(b, ready):
                xb = x_all[:, bass.ds(b * (NT * E), NT * E)].rearrange("p (t e) -> p t e", e=E)
                pool.wait_ge(s["xhat_ready"], ready)
                gp.tensor_tensor(xb, xb, gabo[:, bass.ds(b, 1), :].to_broadcast([P, NT, E]), ALU.add)\
                    .then_inc(s["a_xb"], 1)

            def third_max_part(b, g):
                pool.wait_ge(s["a_m3"], 2 * b + g + 1)
                gp.tensor_tensor(mparts[0:32, g, 2, :], mres[0:32, g, :], mparts[0:32, g, 1, :], ALU.subtract)\
                    .then_inc(s["a_m4"], 1)

            third_parts(0)
            third_max_part(0, 0)
            pool.wait_ge(s["gabo_done"], 1)
            residual_bias(0, NT)
            for i, (raw, high, low) in enumerate(w0_pieces):
                pool.wait_ge(s["w_high"], i + 1)
                gp.tensor_tensor(low, raw, high, ALU.subtract).then_inc(s["w_low"], 1)
            with pool.Fori(0, B - 1) as b:
                third_max_part(b, 1)
                ln_pool(2 * b + 1)
                third_parts(b + 1, 2 * b + 2)
                residual_bias(b + 1, NT * (2 * b + 2))
                third_max_part(b + 1, 0)
            third_max_part(B - 1, 1)
            ln_pool(2 * B - 1)
            ln_pool(2 * B)
            pool.wait_ge(s["b_x"], 1 + TILES)
            for i in range(2):
                gp.memset(pr1[:, i, :, 0:WIN], 0.0).then_inc(s["preset"], 1)

            def norms(b, ln=None):
                for u in range(2 * NT):
                    if u == 2 and ln is not None:
                        ln_pool(ln)
                    pool.wait_ge(s["c_rk0"], 2 * NT * b + u + 1)
                    gp.tensor_tensor(rnorm[:, u % 2, :], ssq[:, u % 2, :], minus_half[:, :], ALU.pow)\
                        .then_inc(s["c_rk"], 1)

            norms(0)
            with pool.Fori(0, B - 1) as b:
                ln_pool(2 * B + 1 + 2 * b)
                norms(b + 1, 2 * B + 2 + 2 * b)
            ln_pool(4 * B - 1)
            pool.wait_ge(s["zfill"], 16 * SLOTS)
            pool.wait_ge(s["r_pos_ok"], 1)
            for t in range(TILES):
                pool.wait_ge(s["r_xr"], t + 1)
                gp.indirect_dma_start(rows_d, bass.IndirectOffsetOnAxis(ap=pos_i[:, t:t + 1], axis=0),
                                      xr_all[:, t * E:(t + 1) * E], None).then_inc(s["r_scatter"], 16)

            def rows_out(slot, j):
                pool.wait_ge(s["m_y"], slot + 1)
                gp.dma_start(yrows_d[bass.ds(slot * P, P), :], ys[:, j, :]).then_inc(s[f"m_out{j}"], 16)

            with pool.Fori(0, SLOT_PAIRS + 1) as i:
                rows_out(2 * i, 0)
                rows_out(2 * i + 1, 1)
            rows_out(SLOTS - 1, 0)
            pool.wait_ge(s["r_scatter"], 16 * TILES)
            pool.wait_ge(s["m_out0"], 16 * (SLOTS // 2 + 1))
            pool.wait_ge(s["m_out1"], 16 * (SLOTS // 2))
            for t in range(TILES):
                gp.indirect_dma_start(yg[:, t, :], None, yrows_d,
                                      bass.IndirectOffsetOnAxis(ap=pos_i[:, t:t + 1], axis=0))\
                    .then_inc(s[f"m_gather{gather_group(t)}"], 16)

        @block.scalar
        def _(act):
            ac = nc.scalar

            def h_out(n_b, xT_sem, h_sem, layer, shift, scale, hi=None, hi_sem=None):
                for dst, done in ((hi, hi_sem), (hT, h_sem)):
                    if dst is None:
                        continue
                    for c in range(KE):
                        if dst is hi or hi is None:
                            act.wait_ge(xT_sem, KE * n_b + c + 1)
                        ac.activation(dst[:, c, :], ps[:, c, :], ACT.Identity,
                                      bias=modT[:, layer, shift + c, bass.ds(n_b, 1)],
                                      scale=modT[:, layer, scale + c, bass.ds(n_b, 1)]).then_inc(done, 1)

            def ffn_act(b, nf, sgbuf, k, ahead={}):
                for f in range(nf):
                    if f in ahead:
                        ahead[f]()
                    act.wait_ge(s[k + "_g"], nf * b + f + 1)
                    if f >= 2:
                        act.wait_ge(s[k + "_gt"], nf * b + f - 1)
                    ac.activation(sgbuf[:, f % 2, :], ps[:, 2 + 2 * (f % 3), :], ACT.Silu).then_inc(s[k + "_sg"], 1)

            act.wait_ge(s["in_c"], 16)
            ac.activation(scT[:, :, :, :].rearrange("p l c b -> p (l c b)"),
                          cT[:, :, :, :].rearrange("p l c b -> p (l c b)"), ACT.Silu).then_inc(s["silu_c"], 1)
            act.wait_ge(s["modT_done"], 2)


            def qk_part(b, i, a):
                if a == 0:
                    act.wait_ge(s["a_qk"], 4 * b + i + 1)
                    ac.copy(parts[:, i, 0, :], ps[:, 2 + i, :]).then_inc(s["a_p1"], 1)
                else:
                    act.wait_ge(s["a_r1"], 4 * b + i + 1)
                    ac.copy(parts[:, i, 1, :], resid[:, i, :]).then_inc(s["a_p2"], 1)

            def max_parts(b, g):
                bank = (0, 7)[g]
                act.wait_ge(s["a_mT"], 2 * b + g + 1)
                ac.copy(mparts[0:32, g, 0, :], ps[0:32, bank, 0:P]).then_inc(s["a_m1"], 1)
                act.wait_ge(s["a_m2"], 2 * b + g + 1)
                ac.copy(mparts[0:32, g, 1, :], mres[0:32, g, :]).then_inc(s["a_m3"], 1)

            def a_core(b, more):
                for h in range(H0):
                    if h == HG:
                        max_parts(b, 1)
                    act.wait_ge(s["a_s2"], H0 * b + h + 1)
                    if h >= 8:
                        act.wait_ge(s["a_pv"], 4 * b + (h - 8) // 4 + 1)
                    ac.activation(probs[:, h % 8, :], banks(3 * (h % 2), 3)[:, 0:KM], ACT.Exp,
                                  scale=float(D0) ** -0.5).then_inc(s["a_exp"], 1)
                if more:
                    h_out(b + 1, s["a_xT"], s["a_h"], 0, 0, 2)
                    qk_part(b + 1, 0, 0)
                    qk_part(b + 1, 0, 1)
                    qk_part(b + 1, 1, 0)
                for c in range(KE):
                    act.wait_ge(s["a_cT"], KE * b + c + 1)
                    ac.copy(ctxT[:, c, :], ps[:, c, :]).then_inc(s["a_cTe"], 1)
                if more:
                    qk_part(b + 1, 1, 1)
                    qk_part(b + 1, 2, 0)
                    qk_part(b + 1, 3, 0)
                    qk_part(b + 1, 2, 1)
                    qk_part(b + 1, 3, 1)

            def b_all(b):
                h_out(b, s["b_xT"], s["b_h"], 0, 6, 8, h0_hi, s["h_high"])
                ffn_act(b, 8, sgT, "b")

            h_out(0, s["a_xT"], s["a_h"], 0, 0, 2)
            for i in range(4):
                qk_part(0, i, 0)
                qk_part(0, i, 1)
            for u in range(B):
                act.wait_ge(s["bc_ps"], u + 1)
                row, g = SC1 + 2 * u, ps[:, 2 + u % 2, :]
                ac.copy(gates_bc[:, row, :], g[:, 0:E])
                ac.activation(gates_bc[:, row + 1, :], g[:, E:2 * E], ACT.Copy, bias=1.0).then_inc(s["bc_sb2"], 1)

            def gate_size(u):
                act.wait_ge(s["bc_ps"], B + u + 1)
                if u >= 2:
                    act.wait_ge(s["bc_sb"], u - 1)
                ac.activation(guard[u % 2][1], ps[:, 2 + u % 2, :], ACT.Abs, scale=0.5).then_inc(s["size_ready"], 1)

            for u in range(6):
                gate_size(u)
            act.wait_ge(s["in_ffn"], 48)
            act.wait_ge(s["rows_kept"], 16)
            for raw, high, low in w0_pieces:
                ac.copy(high, raw).then_inc(s["w_high"], 1)
            max_parts(0, 0)
            gate_size(6)
            gate_size(7)
            act.wait_ge(s["modT_done"], 6)
            with act.Fori(0, B - 1) as b:
                a_core(b, True)
                b_all(b)
                max_parts(b + 1, 0)
            a_core(B - 1, False)
            b_all(B - 1)
            act.wait_ge(s["in_w1"], 16 * 8)
            for raw, high, low in w1_pieces:
                ac.copy(high, raw).then_inc(s["w_high"], 1)


            def d_turned(b, bank=2):
                for c in range(KE):
                    act.wait_ge(s["d_yT"], KE * b + c + 1)
                    ac.copy(hT[:, c, :], ps[:, bank + c, :]).then_inc(s["d_yh"], 1)

            def d_rows(b, bank=2):
                act.wait_ge(s["d_lr"], b + 1)
                ac.copy(lrows, ps[0:NEXP, bank, :]).then_inc(s["d_lx"], 1)

            def c_in(b, d=None):
                act.wait_ge(s["c_gr"], b + 1)
                ac.activation(qn[0:H1, 1, 0:S], ps[0:H1, 0, :], ACT.Exp, bias=negbg[0:H1, 0:1], scale=-1.0)\
                    .then_inc(s["c_gx"], 1)

                def qk_out(u):
                    act.wait_ge(s["c_qT"], 2 * NT * b + u + 1)
                    dst, sc = (qT1, qscale) if u % 2 == 0 else (kT1, kscale)
                    t = u // 2
                    ac.activation(dst[:, :, t * P:(t + 1) * P], banks(6).rearrange("p (h n) -> p h n", h=H1),
                                  ACT.Copy, scale=sc[:, 0:1]).then_inc(s["c_qe"], 1)

                for u in range(2 * NT):
                    act.wait_ge(s["c_p"], 2 * NT * b + u + 1)
                    if u >= 2:
                        act.wait_ge(s["c_ss"], 2 * NT * b + u - 1)
                    ac.activation(sq[:, u % 2, :], banks(2 + 2 * (u % 2)), ACT.Square).then_inc(s["c_sq"], 1)
                    if u >= 2:
                        qk_out(u - 2)
                    if u % 2 == 1:
                        t = u // 2
                        act.wait_ge(s["c_v"], NT * b + t + 1)
                        ac.copy(v1[:, t, :], banks(0)).then_inc(s["c_ve"], 1)
                qk_out(2 * NT - 2)
                if d is not None:
                    d_turned(d)
                qk_out(2 * NT - 1)
                if d is not None:
                    d_rows(d)

            def c_core(b, more):
                for i in range(2 * NT + 2):
                    if i < 2 * NT:
                        t = i // 2
                        c0 = P if t == 0 else WIN
                        act.wait_ge(s["c_mx"], 2 * NT * b + i + 1)
                        if i >= 2:
                            act.wait_ge(s["c_pT"], 2 * NT * b + i - 1)
                        sc4 = banks(2 * (i % 2)).rearrange("p (h n) -> p h n", h=4)
                        for hh in range(4):
                            ac.activation(pr1[:, i % 2, hh, c0:], sc4[:, hh, c0:], ACT.Exp,
                                          bias=nmax1[:, i % 2, hh:hh + 1],
                                          accum_out=rsum1[:, i % 2, hh:hh + 1]).then_inc(s["c_e"], 1)
                    if i == 2 * NT and more:
                        h_out(b + 1, s["c_xT"], s["c_h"], 1, 0, 2, hT_hi, s["h_high"])
                    if i >= 2:
                        v = i - 2
                        act.wait_ge(s["c_o"], 2 * NT * b + v + 1)
                        ac.copy(oT1[:, (v // 2) % 2, 4 * (v % 2):4 * (v % 2) + 4, :].rearrange("p h n -> p (h n)"),
                                ps[:, 6, :]).then_inc(s["c_oe"], 1)

            act.wait_ge(s["modT_done"], 6)
            act.wait_ge(s["setup_v"], 2)
            h_out(0, s["c_xT"], s["c_h"], 1, 0, 2, hT_hi, s["h_high"])
            c_in(0)
            with act.Fori(0, B - 1) as b:
                c_core(b, True)
                c_in(b + 1, b)
            c_core(B - 1, False)

            def shared_T(m):
                for c in range(KE):
                    act.wait_ge(s["d_xT"], KE * m + c + 1)
                    ac.copy(hT[:, c, :], ps[:, c, :]).then_inc(s["d_hT"], 1)

            def score_exp():
                act.wait_ge(s["r_v"], 1)
                ac.activation(score[:, :], r_m, ACT.Exp, scale=-1.0).then_inc(s["r_exp"], 1)

            ffn_act(0, 4, sgTs, "d")
            d_turned(B - 1, 0)
            d_rows(B - 1, 0)
            ffn_act(1, 4, sgTs, "d", {1: score_exp})
            for m in range(B - 2):
                shared_T(m)
                ffn_act(m + 2, 4, sgTs, "d")

            def silu(slot, j):
                act.wait_ge(s["m_gu"], slot + 1)
                ac.activation(sgs[:, j, :], ps[:, 1 + 2 * j, :], ACT.Silu).then_inc(s["m_sg"], 1)

            def xT_out(slot, j):
                act.wait_ge(s["m_xT"], slot + 3)
                ac.copy(xsT[:, j, :, :].rearrange("p c n -> p (c n)"), ps[:, 0, 0:E]).then_inc(s["m_xTe"], 1)

            xT_out(0, 0)
            xT_out(1, 1)
            silu(0, 0)
            xT_out(2, 0)
            silu(1, 1)
            with act.Fori(0, SLOT_PAIRS) as i:
                xT_out(2 * i + 3, 1)
                silu(2 * i + 2, 0)
                xT_out(2 * i + 4, 0)
                silu(2 * i + 3, 1)
            silu(SLOTS - 1, 0)

        @block.vector
        def _(dve):
            v = nc.vector

            def ln_tiles(tile0, t0, t1):
                dve.sem_inc(s["settled"], 1)
                for t in range(t0, t1):
                    v.bn_stats(stats[:, t, :], x_all[:, bass.ds((tile0 + t) * E, E)]).then_inc(s["ln_stats"], 1)

            def ln_moments(n):
                dve.wait_ge(s["ln_stats"], NT * n + NT)
                v.tensor_tensor(lsum[:, :, :], stats[:, :, 1:3], stats[:, :, 4:6], ALU.add).then_inc(s["ln_mv"], 1)
                v.tensor_tensor(ldif[:, :], stats[:, :, 1], stats[:, :, 4], ALU.subtract).then_inc(s["ln_mv"], 1)
                dve.wait_ge(s["ln_mv"], 5 * n + 2)
                v.tensor_scalar(mean[:, :], lsum[:, :, 0], 0.5, None, ALU.mult).then_inc(s["ln_mv"], 1)
                v.tensor_scalar(lvar[:, :], lsum[:, :, 1], 1.0 / E, EPS, ALU.mult, ALU.add).then_inc(s["ln_mv"], 1)
                v.scalar_tensor_tensor(out=lsq[:, :], in0=ldif[:, :], scalar=0.25, in1=ldif[:, :], op0=ALU.mult,
                                       op1=ALU.mult).then_inc(s["ln_mv"], 1)
                dve.wait_ge(s["ln_mv"], 5 * n + 5)
                v.tensor_tensor(vareps[:, :], lvar[:, :], lsq[:, :], ALU.add).then_inc(s["ln_var"], 1)

            def ln_stats(n, tile0):
                ln_tiles(tile0, 0, NT)
                ln_moments(n)

            def ln_apply(n, tile0, t0=0, t1=NT):
                dve.wait_ge(s["ln_rstd"], n + 1)
                for t in range(t0, t1):
                    v.tensor_scalar(xhat[:, t, :], x_all[:, bass.ds((tile0 + t) * E, E)], mean[:, t:t + 1],
                                    rstd[:, t:t + 1], ALU.subtract, ALU.mult).then_inc(s["xhat_ready"], 1)

            def x_update(b, tile, src, gate, tmp_sem, x_sem, par, k):
                v.scalar_tensor_tensor(out=utmp[:, par, :], in0=src, scalar=4.0,
                                       in1=gates_bc[:, bass.ds(gate, 1), :].rearrange("p a e -> p (a e)"),
                                       op0=ALU.mult, op1=ALU.mult).then_inc(tmp_sem, 1)
                dve.wait_ge(tmp_sem, k + 1)
                xt = x_all[:, bass.ds(tile * E, E)]
                v.tensor_tensor(xt, xt, utmp[:, par, :], ALU.add).then_inc(x_sem, 1)

            def ffn_dve(b, nf, gbuf, sgbuf, k, gate0, n_ln=None, ln_tile=None, between=None, after_up=None,
                        ahead={}, batch=None):
                batch = b if batch is None else batch
                for f in range(nf):
                    if f in ahead:
                        ahead[f]()
                    if between is not None:
                        if f == 0:
                            between(0, 4)
                        if f < nf - 1:
                            between(4 * f + 4, 4 * f + 5)
                    dve.wait_ge(s[k + "_sg"], nf * b + f + 1)
                    dve.wait_ge(s[k + "_u"], nf * b + f + 1)
                    v.tensor_tensor(gbuf[:, f, :], sgbuf[:, f % 2, :], ps[:, 3 + 2 * (f % 3), :], ALU.mult)\
                        .then_inc(s[k + "_gt"], 1)
                    if between is not None and f < nf - 1:
                        between(4 * f + 5, 4 * f + 8)
                    if f == nf // 2 - 1 and ln_tile is not None:
                        ln_stats(n_ln, ln_tile)
                    if f == nf // 2 and ln_tile is not None:
                        ln_apply(n_ln, ln_tile)
                if after_up is not None:
                    after_up()
                for t in range(NT):
                    dve.wait_ge(s[k + "_o"], 2 * b + t // 2 + 1)
                    x_update(b, NT * batch + t, ps[:, 6 + t // 2, (t % 2) * E:(t % 2 + 1) * E], gate0 + 2 * batch,
                             s[k + "_tmp"], s[k + "_x"], t % 2, NT * b + t)

            for k in "abcd":
                dve.sem_inc(s[k + "_x"], 1)
            dve.sem_inc(s["d_kept"], 16)
            dve.sem_inc(s["d_lc"], 1)
            dve.wait_ge(s["in_x0"], 16)
            ln_stats(0, 0)
            ln_apply(0, 0)
            dve.wait_ge(s["silu_c"], 1)
            mod = ps[:, 7, 0:96].rearrange("p (l j b) -> p l j b", l=2, j=12)

            def mod_out(layer, j):
                v.tensor_copy(modT[:, layer, j:j + 2, :], mod[:, layer, j:j + 2, :]).then_inc(s["modT_done"], 1)
                v.tensor_scalar(modT[:, layer, j + 2:j + 4, :], mod[:, layer, j + 2:j + 4, :], 1.0, None, ALU.add)\
                    .then_inc(s["modT_done"], 1)

            dve.wait_ge(s["modT_ps"], 1)
            mod_out(0, 0)
            v.tensor_copy(sc_bc.rearrange("p l c b n -> p (l c b) n"),
                          scT[:, :, :, :].rearrange("p l c b -> p (l c b)").unsqueeze(2).to_broadcast([P, 16, P]))\
                .then_inc(s["scbc_done"], 1)

            def gate_rows(u):
                row = G1 + 2 * u if u < B else G0 + 2 * (u - B)
                half_sign, size = guard[u % 2]
                g = ps[:, 2 + u % 2, :]
                dve.wait_ge(s["size_ready"], u + 1)
                v.tensor_scalar(half_sign, g, 0.0, 0.5, ALU.is_ge, ALU.subtract).then_inc(s["guard_v"], 1)
                dve.wait_ge(s["guard_v"], u + 1)
                v.scalar_tensor_tensor(out=gates_bc[:, row:row + 2, :].rearrange("p k e -> p (k e)"), in0=size,
                                       scalar=0.125, in1=half_sign, op0=ALU.max, op1=ALU.mult)\
                    .then_inc(s["bc_sb"], 1)


            def resid_of(b, i):
                dve.wait_ge(s["a_p1"], 4 * b + i + 1)
                v.tensor_tensor(resid[:, i, :], ps[:, 2 + i, :], parts[:, i, 0, :], ALU.subtract)\
                    .then_inc(s["a_r1"], 1)

            def v_out(b, i):
                dve.wait_ge(s["a_v"], 2 * b + i + 1)
                v.tensor_copy(vaug[:, 2 * i:2 * i + 2, :, 0:D0],
                              ps[:, 6 + i, :].rearrange("p (t h d) -> p t h d", t=2, h=H0)).then_inc(s["a_vc"], 1)

            def lower_part(h_sem, b, hi, lo):
                for c in range(KE):
                    dve.wait_ge(h_sem, KE * b + c + 1)
                    v.tensor_tensor(lo[:, c, :], hT[:, c, :], hi[:, c, :], ALU.subtract).then_inc(s["h_low"], 1)

            def head_maxima(b, g, banks_of, u0, u1):
                for u in range(u0, u1):
                    h, qt = HG * g + u // 4, QT_ORDER[u % 4]
                    dve.wait_ge(s["a_s1"], 64 * b + 32 * g + u + 1)
                    v.reduce_max(rowmax[:, h:h + 1, qt], ps[:, banks_of[u % len(banks_of)], 0:(qt + 1) * P], AX_X)\
                        .then_inc(s["a_max"], 1)

            def max_resid(b, g):
                dve.wait_ge(s["a_m1"], 2 * b + g + 1)
                v.tensor_tensor(mres[0:32, g, :], ps[0:32, (0, 7)[g], 0:P], mparts[0:32, g, 0, :], ALU.subtract)\
                    .then_inc(s["a_m2"], 1)

            def a_core(b, more):
                head_maxima(b, 1, (6, 7), 0, 32)
                max_resid(b, 1)
                if more:
                    ln_stats(2 * b + 1, (b + 1) * NT)
                for n in range(4):
                    if more and n == 2:
                        ln_apply(2 * b + 1, (b + 1) * NT)
                    dve.wait_ge(s["a_pv"], 4 * b + n + 1)
                    v.tensor_copy(oTs[:, n % 2, :], ps[:, 6, :]).then_inc(s["a_oT"], 1)
                    if more and n == 3:
                        resid_of(b + 1, 0)
                    dve.wait_ge(s["a_oTT"], 4 * b + n + 1)
                    tok = ps[:, 7, :].rearrange("p (t j c) -> p t j c", t=NT, j=4)
                    rd = rden[:, n % 2, :].rearrange("p (t j) -> p t j", t=NT)
                    v.reciprocal(rd, tok[:, :, :, D0]).then_inc(s["a_rc"], 1)
                    dve.wait_ge(s["a_rc"], 4 * b + n + 1)
                    v.tensor_tensor(ctx0[:, :, 4 * n * D0:4 * (n + 1) * D0].rearrange("p t (j d) -> p t j d", j=4),
                                    tok[:, :, :, 0:D0], rd.unsqueeze(3).to_broadcast([P, NT, 4, D0]), ALU.mult)\
                        .then_inc(s["a_ctx"], 1)
                if more:
                    resid_of(b + 1, 1)
                dve.wait_ge(s["a_xb"], b + 1)
                for t in range(NT):
                    dve.wait_ge(s["a_o"], 2 * b + t // 2 + 1)
                    x_update(b, NT * b + t, ps[:, t // 2, (t % 2) * E:(t % 2 + 1) * E], G0 + 2 * b,
                             s["a_tmp"], s["a_x"], t % 2, NT * b + t)
                dve.wait_ge(s["a_x"], 1 + NT * b + NT)

            for i in range(4):
                resid_of(0, i)
            for i in range(2):
                v_out(0, i)
            dve.wait_ge(s["in_wo0"], 32)
            for u in range(8):
                gate_rows(u)
                if u == 0:
                    dve.wait_ge(s["modT_ps"], 3)
                    mod_out(0, 6)
                    mod_out(1, 0)
                if u in (4, 5):
                    head_maxima(0, 0, (0, 1, 4, 5), 16 * (u - 4), 16 * (u - 3))
                if u == 5:
                    max_resid(0, 0)
            dve.wait_ge(s["bc_sb"], 8)
            v.scalar_tensor_tensor(out=gabo, in0=gates_bc[:, 0:8:2, :], scalar=4.0,
                                   in1=bo_bc.unsqueeze(1).to_broadcast([P, B, E]), op0=ALU.mult, op1=ALU.mult)\
                .then_inc(s["gabo_done"], 1)
            dve.wait_ge(s["gabo_done"], 1)
            dve.wait_ge(s["bc_sb2"], B)
            dve.wait_ge(s["in_x"], 16 * (B - 1))
            with dve.Fori(0, B - 1) as b:
                a_core(b, True)
                ln_stats(2 * b + 2, b * NT)
                resid_of(b + 1, 2)
                resid_of(b + 1, 3)
                dve.wait_ge(s["a_xT"], KE * (b + 1) + KE)
                ln_apply(2 * b + 2, b * NT)
                v_out(b + 1, 0)
                v_out(b + 1, 1)
                lower_part(s["b_h"], b, h0_hi, h0_lo)
                ffn_dve(b, 8, gT, sgT, "b", G0 + 1, between=lambda u0, u1: head_maxima(b + 1, 0, (0, 1), u0, u1),
                        after_up=lambda: max_resid(b + 1, 0))
            a_core(B - 1, False)
            ln_stats(2 * B - 1, (B - 1) * NT)
            ln_apply(2 * B - 1, (B - 1) * NT)
            dve.wait_ge(s["b_x"], 1 + NT)

            def w1_lower_parts():
                for i, (raw, high, low) in enumerate(w1_pieces):
                    dve.wait_ge(s["w_high"], len(w0_pieces) + i + 1)
                    v.tensor_tensor(low, raw, high, ALU.subtract).then_inc(s["w_low"], 1)

            lower_part(s["b_h"], B - 1, h0_hi, h0_lo)
            ffn_dve(B - 1, 8, gT, sgT, "b", G0 + 1, 2 * B, 0, after_up=w1_lower_parts)
            dve.wait_ge(s["b_x"], 1 + TILES)
            dve.wait_ge(s["in_w1"], 16 * 8)
            v.tensor_scalar(qscale[:, :], qscale[:, :], 8.0, None, ALU.mult).then_inc(s["setup_v"], 1)
            v.tensor_scalar(negbg[0:H1, :], negbg[0:H1, :], -1.0, None, ALU.mult).then_inc(s["setup_v"], 1)
            dve.wait_ge(s["setup_v"], 2)
            dve.wait_ge(s["rows_kept"], 32)


            def h_lower(b):
                lower_part(s["c_h"], b, hT_hi, hT_lo)

            def max1(b, i):
                c0 = P if i < 2 else WIN
                dve.wait_ge(s["c_s"], 2 * NT * b + i + 1)
                v.reduce_max(nmax1[:, i % 2, :],
                             banks(2 * (i % 2)).rearrange("p (h n) -> p h n", h=4)[:, :, c0:], AX_X,
                             negate=True).then_inc(s["c_mx"], 1)

            def c_in(b, between=None):
                dve.wait_ge(s["c_gp"], b + 1)
                v.tensor_scalar(small[:, 0:32], ps[:, 1, 0:32], 1.0, None, ALU.add).then_inc(s["c_g1"], 1)
                dve.wait_ge(s["c_g1"], b + 1)
                v.reciprocal(g1[:, :], small[:, 0:32]).then_inc(s["c_gate"], 1)
                for t in range(NT):
                    for u in (2 * t, 2 * t + 1):
                        dve.wait_ge(s["c_sq"], 2 * NT * b + u + 1)
                        v.reduce_sum(ssq[:, u % 2, :], sq[:, u % 2, :].rearrange("p (h d) -> p h d", h=H1), AX_X)\
                            .then_inc(s["c_ss"], 1)
                        dve.wait_ge(s["c_ss"], 2 * NT * b + u + 1)
                        v.tensor_scalar(ssq[:, u % 2, :], ssq[:, u % 2, :], 1e-24, None, ALU.max)\
                            .then_inc(s["c_rk0"], 1)
                    for u in (2 * t, 2 * t + 1):
                        dve.wait_ge(s["c_rk"], 2 * NT * b + u + 1)
                        if u >= 2:
                            dve.wait_ge(s["c_qT"], 2 * NT * b + u - 1)
                        v.tensor_tensor(qn[:, u % 2, :].rearrange("p (h d) -> p h d", h=H1),
                                        banks(2 + 2 * (u % 2)).rearrange("p (h d) -> p h d", h=H1),
                                        rnorm[:, u % 2, :].unsqueeze(2).to_broadcast([P, H1, D1]), ALU.mult)\
                            .then_inc(s["c_qn"], 1)
                        if between is not None:
                            between(u)
                max1(b, 0)

            def c_core(b, more):
                for i in range(2 * NT + 3):
                    if 1 <= i <= 2 * NT:
                        w = i - 1
                        k0 = 1 if w < 2 else 0
                        t, hg = w // 2, w % 2
                        w0c = P if t == 0 else WIN
                        dve.wait_ge(s["c_e"], 8 * NT * b + 4 * w + 4)
                        v.reciprocal(rinv1[:, w % 2, :], rsum1[:, w % 2, :]).then_inc(s["c_ri"], 1)
                        dve.wait_ge(s["c_ri"], 2 * NT * b + w + 1)
                        for hh in range(4):
                            g = g1[:, t * H1 + 4 * hg + hh:t * H1 + 4 * hg + hh + 1]
                            v.tensor_scalar(pr1[:, w % 2, hh, w0c:], pr1[:, w % 2, hh, w0c:],
                                            rinv1[:, w % 2, hh:hh + 1], g, ALU.mult, ALU.mult).then_inc(s["c_pn"], 1)
                    if 1 <= i < 2 * NT:
                        max1(b, i)
                    if i >= 4 and i % 2 == 0:
                        t = i // 2 - 2
                        dve.wait_ge(s["c_w"], NT * b + t + 1)
                        x_update(b, NT * b + t, ps[:, 7, 0:E], G1 + 2 * b, s["c_tmp"], s["c_x"], t % 2, NT * b + t)
                    if 1 <= i <= 2 * NT:
                        w = i - 1
                        k0 = 1 if w < 2 else 0
                        dve.wait_ge(s["c_pT"], 2 * NT * b + w + 1)
                        v.tensor_copy(pT1[:, w % 2, :, k0:, :],
                                      banks(4).rearrange("p (h k n) -> p h k n", h=4, k=2)[:, :, k0:, :])\
                            .then_inc(s["c_pTe"], 1)
                    if more:
                        n, tile0 = 2 * B + 1 + 2 * b, (b + 1) * NT
                        if i == 0:
                            ln_tiles(tile0, 0, NT // 2)
                        if i == 1:
                            ln_tiles(tile0, NT // 2, NT)
                        if i == 2:
                            ln_moments(n)
                        if 3 <= i < 3 + NT:
                            ln_apply(n, tile0, i - 3, i - 2)
                        if i == 2 * NT + 1:
                            h_lower(b + 1)
                dve.wait_ge(s["c_x"], 1 + NT * b + NT)

            def d_h(b, n, h, piece):
                half, add = piece // 2, piece % 2
                if piece == 0:
                    dve.wait_ge(s["xhat_ready"], NT * n + NT)
                    if h is hs:
                        dve.wait_ge(s["d_kept"], 16 + 16 * b)
                row = SC1 + 2 * b + 1 - add
                rows = gates_bc[:, bass.ds(row, 1), :].to_broadcast([P, NT // 2, E])
                tiles = slice(half * NT // 2, (half + 1) * NT // 2)
                if add:
                    dve.wait_ge(s["d_h0"], 2 * b + half + 1)
                    v.tensor_tensor(h[:, tiles, :], h[:, tiles, :], rows, ALU.add).then_inc(s["d_h"], 1)
                else:
                    v.tensor_tensor(h[:, tiles, :], xhat[:, tiles, :], rows, ALU.mult).then_inc(s["d_h0"], 1)

            def d_logits(b, bank=4):
                dve.wait_ge(s["d_l"], b + 1)
                v.tensor_copy(logits[:, bass.ds(b * (NT * NEXP), NT * NEXP)], ps[:, bank, 0:NT * NEXP])\
                    .then_inc(s["d_lc"], 1)

            h_lower(0)
            c_in(0)
            with dve.Fori(0, B - 1) as b:
                c_core(b, True)

                def between(u):
                    n = 2 * B + 2 + 2 * b
                    if u == 0:
                        ln_tiles(b * NT, 0, NT)
                    if u == 1:
                        ln_moments(n)
                    if u == 2:
                        dve.wait_ge(s["c_xT"], KE * (b + 1) + KE)
                        ln_apply(n, b * NT)
                    if 3 <= u < 7:
                        d_h(b, n, hs, u - 3)

                c_in(b + 1, between)
                d_logits(b)
            c_core(B - 1, False)
            ln_stats(4 * B - 1, (B - 1) * NT)
            ln_apply(4 * B - 1, (B - 1) * NT)
            dve.wait_ge(s["c_v"], TILES)
            for piece in range(4):
                d_h(B - 1, 4 * B - 1, h_of[:, B - 1], piece)

            step = [0]

            def then(ins):
                step[0] += 1
                ins.then_inc(s["r_v"], 1)
                dve.wait_ge(s["r_v"], step[0])

            lg = logits[:, :].rearrange("p (t e) -> p t e", e=NEXP)

            def over_e(a, n=TILES):
                return a.unsqueeze(2).to_broadcast([P, n, NEXP])

            def over_t(a, n=TILES):
                return a.unsqueeze(1).to_broadcast([P, n, NEXP])

            def top_expert():
                d_logits(B - 1, 1)
                dve.wait_ge(s["d_lc"], 1 + B)
                dve.wait_ge(s["in_rt"], 16 * 5)
                then(v.reduce_max(r_m, lg, AX_X))
                then(v.tensor_tensor(r_eq, lg, over_e(r_m), ALU.is_equal))
                then(v.tensor_tensor(r_eq, r_eq, r_w8, ALU.mult))
                then(v.reduce_max(r_pos, r_eq, AX_X))
                then(v.tensor_tensor(r_oh, r_eq, over_e(r_pos), ALU.is_equal))
                then(v.memset(r_ohx[:, TILES, :], 0.0))
                then(v.tensor_copy(r_ohx[:, 0:TILES, :], r_oh))

            def slots_and_scores():
                dve.wait_ge(s["r_R"], 1)
                rank = ps[:, 0, 0:(TILES + 1) * NEXP].rearrange("p (t e) -> p t e", e=NEXP)
                then(v.tensor_copy(r_n, rank[:, TILES, :]))
                a128 = r_a[:, 0:128].rearrange("p (e j) -> p e j", e=NEXP)
                then(v.tensor_tensor(a128, r_n.unsqueeze(2).to_broadcast([P, NEXP, TILES]), r_thr, ALU.is_gt))
                then(v.reduce_sum(r_nt, a128, AX_X))
                a64 = r_a[:, 0:64].rearrange("p (e j) -> p e j", e=NEXP)
                then(v.tensor_tensor(a64, over_t(r_nt, NEXP), r_incl, ALU.mult))
                then(v.reduce_sum(r_end, a64, AX_X))
                then(v.tensor_tensor(r_base, r_end, r_nt, ALU.subtract))
                then(v.tensor_scalar(r_base, r_base, float(P), None, ALU.mult))
                then(v.tensor_tensor(r_eq, rank[:, 0:TILES, :], over_t(r_base), ALU.add))
                v.sem_inc(s["r_read"], 1)
                then(v.tensor_tensor(r_eq, r_eq, r_oh, ALU.mult))
                then(v.reduce_sum(r_pos, r_eq, AX_X))
                then(v.tensor_copy(pos_i[:, :], r_pos))
                a192 = r_a[:, 0:SLOTS * NEXP].rearrange("p (s e) -> p s e", e=NEXP)
                then(v.tensor_tensor(a192, r_iota, over_t(r_end, SLOTS), ALU.is_ge))
                then(v.reduce_sum(r_f, a192, AX_X))
                then(v.tensor_scalar(r_f, r_f, float(NEXP - 1), None, ALU.min))
                then(v.tensor_copy(slot_e[:, :], r_f))
                dve.wait_ge(s["r_exp"], 1)
                then(v.tensor_scalar(score[:, :], score[:, :], 1.0, None, ALU.add))
                then(v.reciprocal(score[:, :], score[:, :]))
                v.sem_inc(s["r_pos_ok"], 1)

            ffn_dve(0, 4, gTs, sgTs, "d", G1 + 1, batch=B - 2)
            ffn_dve(1, 4, gTs, sgTs, "d", G1 + 1, batch=B - 1, ahead={0: top_expert, 2: slots_and_scores})
            dve.wait_ge(s["in_rt"], 16 * 5)
            dve.wait_ge(s["d_h"], 2 * B)
            for t in range(TILES):
                v.tensor_scalar(xr_all[:, t * E:(t + 1) * E], h_all[:, t * E:(t + 1) * E], score[:, t:t + 1], None,
                                ALU.mult).then_inc(s["r_xr"], 1)
            for m in range(B - 2):
                ffn_dve(m + 2, 4, gTs, sgTs, "d", G1 + 1, batch=m)
            dve.wait_ge(s["d_x"], 1 + TILES)

            dve.wait_ge(s["r_xr"], TILES)

            def act_out(slot, j):
                dve.wait_ge(s["m_sg"], slot + 1)
                v.tensor_tensor(acts[:, j, :], sgs[:, j, :], ps[:, 2 + 2 * j, :], ALU.mult).then_inc(s["m_a"], 1)

            def actT_out(slot, j):
                dve.wait_ge(s["m_aT"], slot + 1)
                v.tensor_copy(actT[:, j, :, :].rearrange("p f n -> p (f n)"), ps[:, 5, :]).then_inc(s["m_aTe"], 1)

            def y_out(slot, j, stored):
                dve.wait_ge(s["m_d"], slot + 1)
                if stored is not None:
                    dve.wait_ge(s[f"m_out{j}"], stored)
                v.tensor_copy(ys[:, j, :], ps[:, 6 + j, 0:E]).then_inc(s["m_y"], 1)

            act_out(0, 0)
            act_out(1, 1)
            actT_out(0, 0)

            def pair(i, stored):
                act_out(2 * i + 2, 0)
                actT_out(2 * i + 1, 1)
                y_out(2 * i, 0, stored)
                act_out(2 * i + 3, 1)
                actT_out(2 * i + 2, 0)
                y_out(2 * i + 1, 1, stored)

            pair(0, None)
            with dve.Fori(0, SLOT_PAIRS - 1) as i:
                pair(i + 1, 16 * i + 16)
            act_out(SLOTS - 1, 0)
            actT_out(SLOTS - 2, 1)
            y_out(SLOTS - 3, 0, 16 * SLOT_PAIRS)
            actT_out(SLOTS - 1, 0)
            y_out(SLOTS - 2, 1, 16 * SLOT_PAIRS)
            y_out(SLOTS - 1, 0, 16 * (SLOT_PAIRS + 1))
            for t in range(TILES):
                b = t // NT
                group = gather_group(t)
                dve.wait_ge(s[f"m_gather{group}"], 16 * (GATHERS[group + 1] - GATHERS[group]))
                x_update(b, t, yg[:, t, :], G1 + 1 + 2 * b, s["f_tmp"], s["f_x"], t % 2, t)

        @block.tensor
        def _(pe):
            mm, tr = nc.tensor.matmul, nc.tensor.transpose

            def xhat_T(b, n, src, xT_sem, bank=0):
                for c in range(KE):
                    for t in range(NT):
                        last = tr(ps[:, bank + c, t * P:(t + 1) * P], src[:, t, c * P:(c + 1) * P], ident[:, :])
                    last.then_inc(xT_sem, 1)

            def ffn_up(b, nf, gw, uw, k, before=(), between=None, in_parts=None):
                for f in range(nf):
                    if f >= 3:
                        pe.wait_ge(s[k + "_gt"], nf * b + f - 2)
                    if f == 2:
                        pe.wait_ge(s[k + "_x"], NT * b + 1)
                    for name, count, at in before:
                        if at == f:
                            pe.wait_ge(s[name], count)
                    for i, (w, done) in enumerate(((gw, "_g"), (uw, "_u"))):
                        if in_parts is None:
                            products = [(w, hT, c) for c in range(KE)]
                        else:
                            hi, lo = in_parts
                            products = [(a, h, c) for a, h in ((w[0], hi), (w[1], hi), (w[0], lo))
                                        for c in range(KE)]
                        n = len(products)
                        for m, (a, h, c) in enumerate(products):
                            if in_parts is not None and f == 0 and i == 0 and 1 <= m < KE:
                                pe.wait_ge(s["h_high"], KE * b + m + 1)
                            if in_parts is not None and f == 0 and i == 0 and m == KE:
                                pe.wait_ge(s[k + "_h"], KE * b + KE)
                            if in_parts is not None and f == 0 and i == 0 and m == 2 * KE:
                                pe.wait_ge(s["h_low"], KE * b + KE)
                            last = mm(ps[:, 2 + i + 2 * (f % 3), :], a[:, c, f * P:(f + 1) * P], h[:, c, :],
                                      start=(m == 0), stop=(m == n - 1))
                            if m == n - 1:
                                last.then_inc(s[k + done], 1)
                            if between is not None and (m + 1) % (n // 2) == 0:
                                between(4 * f + 2 * i + (m + 1) // (n // 2) - 1)

            def ffn_down(b, nf, dw, gbuf, k, after_first=None):
                pe.wait_ge(s[k + "_gt"], nf * b + nf - 1)
                for t in range(NT):
                    for f in range(nf):
                        if t == 0 and f == nf - 1:
                            pe.wait_ge(s[k + "_gt"], nf * b + nf)
                        last = mm(ps[:, 6 + t // 2, (t % 2) * E:(t % 2 + 1) * E], gbuf[:, f, t * P:(t + 1) * P],
                                  dw[:, f, :], start=(f == 0), stop=(f == nf - 1))
                    if t % 2 == 1:
                        last.then_inc(s[k + "_o"], 1)
                    if t == 0 and after_first is not None:
                        after_first()

            def mod_columns(layer, chunks_of_mod):
                for j in chunks_of_mod:
                    for c in range(KE):
                        at = (layer * 12 + j) * B
                        last = mm(ps[:, 7, at:at + B], wmod[layer][:, c, j * P:(j + 1) * P], scT[:, layer, c, :],
                                  start=(c == 0), stop=(c == KE - 1))
                last.then_inc(s["modT_ps"], 1)

            mod_jobs = [(1, b, (3, 4)) for b in range(B)] + [(1, b, (2, 5)) for b in range(B)]
            mod_jobs += [(0, b, (2, 5)) for b in range(B)]

            def mod_rows(u):
                layer, b, kinds = mod_jobs[u]
                if u >= B + 2:
                    pe.wait_ge(s["bc_sb"], u - B - 1)
                elif u >= 2:
                    pe.wait_ge(s["bc_sb2"], u - 1)
                for i, kind in enumerate(kinds):
                    lo, hi = mod_cols(kind)
                    for c in range(KE):
                        last = mm(ps[:, 2 + u % 2, i * E:(i + 1) * E], sc_bc[:, layer, c, b, :],
                                  wmod[layer][:, c, lo:hi], start=(c == 0), stop=(c == KE - 1))
                last.then_inc(s["bc_ps"], 1)


            def project_qk(b, i):
                for c in range(KE):
                    last = mm(ps[:, 2 + i, :], w0[i % 2][:, c, (i // 2) * P:(i // 2 + 1) * P], hT[:, c, :],
                              start=(c == 0), stop=(c == KE - 1))
                last.then_inc(s["a_qk"], 1)

            def project_v(b):
                for t in range(NT):
                    for c in range(KE):
                        last = mm(ps[:, 6 + t // 2, (t % 2) * E:(t % 2 + 1) * E], hT[:, c, t * P:(t + 1) * P],
                                  w0[2][:, c, :], start=(c == 0), stop=(c == KE - 1))
                    if t % 2 == 1:
                        last.then_inc(s["a_v"], 1)

            def max_units(b, g, banks_of, u0, u1):
                for u in range(u0, u1):
                    h, qt = HG * g + u // 4, QT_ORDER[u % 4]
                    n = len(banks_of)
                    bank = banks_of[u % n]
                    if u == 0:
                        pe.wait_ge(s[f"a_stack{g}"], (16 * 12) * b + 16 * 12)
                    if u >= n:
                        pe.wait_ge(s["a_max"], 64 * b + 32 * g + u - n + 1)
                    mm(ps[:, bank, 0:(qt + 1) * P], qst[0:MAX_ROW, h, qt * P:(qt + 1) * P],
                       kst[0:MAX_ROW, h, 0:(qt + 1) * P], start=True, stop=False)
                    mm(ps[:, bank, qt * P:(qt + 1) * P], identb[:, :], maskq[:, :], start=False, stop=True)\
                        .then_inc(s["a_s1"], 1)

            def turn_max(b, g):
                pe.wait_ge(s["a_max"], 64 * b + 32 * g + 32)
                tr(ps[0:32, (0, 7)[g], 0:P], rowmax[:, HG * g:HG * g + HG, :].rearrange("p h t -> p (h t)"),
                   ident[:, :]).then_inc(s["a_mT"], 1)

            def a_core(b, more):
                def pv(n):
                    pe.wait_ge(s["a_exp"], H0 * b + 4 * n + 4)
                    if n >= 1:
                        pe.wait_ge(s["a_oT"], 4 * b + n)
                    for kt in range(NT):
                        for j in range(4):
                            h = 4 * n + j
                            last = mm(ps[32 * j:32 * j + 32, 6, kt * P:S], vaug[:, kt, h, :],
                                      probs[:, h % 8, KM_OFF[kt]:KM_OFF[kt] + KM_W[kt]],
                                      start=(kt == 0), stop=(kt == NT - 1))
                    last.then_inc(s["a_pv"], 1)

                def turn(n):
                    pe.wait_ge(s["a_oT"], 4 * b + n + 1)
                    if n >= 1:
                        pe.wait_ge(s["a_ctx"], 4 * b + n)
                    else:
                        pe.wait_ge(s["a_m2"], 2 * b + 2)
                    for t in range(NT):
                        last = tr(ps[:, 7, t * P:(t + 1) * P], oTs[:, n % 2, t * P:(t + 1) * P], ident[:, :])
                    last.then_inc(s["a_oTT"], 1)

                def km_scores(h, between=None):
                    if h >= 2:
                        pe.wait_ge(s["a_exp"], H0 * b + h - 1)
                    if h % HG == 0:
                        pe.wait_ge(s[f"a_mrow{h // HG}"], 48 * b + 48)
                    sc = banks(3 * (h % 2), 3)
                    for i, kt in enumerate((0, 1, 3, 2)):
                        at = KM_OFF[kt]
                        mm(sc[:, at:at + KM_W[kt]], kst[0:STACK, h, kt * P:(kt + 1) * P], qst[0:STACK, h, kt * P:S],
                           start=True, stop=False)
                        last = mm(sc[:, at:at + P], identb[:, :], maskk[:, :], start=False, stop=True)
                        if i == NT - 1:
                            last.then_inc(s["a_s2"], 1)
                        if between is not None:
                            between(i)

                km_scores(0)
                pe.wait_ge(s["a_vc"], 2 * b + 2)
                pe.wait_ge(s["b_x"], NT * b + 1)
                max_units(b, 1, (6, 7), 0, 4)
                for h in range(1, HG):
                    km_scores(h, lambda i, h=h: max_units(b, 1, (6, 7), 4 * h + i, 4 * h + i + 1))
                turn_max(b, 1)
                pv(0)
                pv(1)
                for h in range(HG, H0):
                    km_scores(h)
                    if h == HG:
                        turn(0)
                    if h == HG + 1:
                        turn(1)
                    if h == HG + 5:
                        pv(2)
                turn(2)
                if more:
                    pe.wait_ge(s["xhat_ready"], NT * (2 * b + 2))
                    pe.wait_ge(s["a_exp"], H0 * b + H0 - 1)
                    xhat_T(b + 1, 0, xhat, s["a_xT"])
                pv(3)
                if more:
                    pe.wait_ge(s["a_h"], KE * (b + 1) + KE)
                    project_qk(b + 1, 0)
                turn(3)
                if more:
                    project_qk(b + 1, 1)
                pe.wait_ge(s["a_ctx"], 4 * b + 4)
                xhat_T(b, 0, ctx0, s["a_cT"])
                pe.wait_ge(s["a_cTe"], KE * b + KE)
                for t in range(NT):
                    for c in range(KE):
                        last = mm(ps[:, t // 2, (t % 2) * E:(t % 2 + 1) * E], ctxT[:, c, t * P:(t + 1) * P],
                                  w0[3][:, c, :], start=(c == 0), stop=(c == KE - 1))
                    if t % 2 == 1:
                        last.then_inc(s["a_o"], 1)
                if more:
                    project_qk(b + 1, 2)
                    project_qk(b + 1, 3)
                    project_v(b + 1)

            def b_all(b, more):
                pe.wait_ge(s["xhat_ready"], NT * (2 * b + 3) if more else NT * 2 * B)
                xhat_T(b, B + b, xhat, s["b_xT"])
                pe.wait_ge(s["in_ffn"], 48)
                pe.wait_ge(s["w_low"], len(w0_pieces))
                pe.wait_ge(s["h_high"], KE * b + 1)
                if more:
                    ffn_up(b, 8, wgate_parts, wup_parts, "b", [("a_r1", 4 * b + 8, 0), ("a_vc", 2 * b + 4, 2)],
                           lambda u: max_units(b + 1, 0, (0, 1), u, u + 1), in_parts=(h0_hi, h0_lo))
                    ffn_down(b, 8, wdown, gT, "b", lambda: turn_max(b + 1, 0))
                else:
                    ffn_up(b, 8, wgate_parts, wup_parts, "b", in_parts=(h0_hi, h0_lo))
                    ffn_down(b, 8, wdown, gT, "b")

            pe.wait_ge(s["in_mod0"], 16)
            pe.wait_ge(s["silu_c"], 1)
            mod_columns(0, range(4))
            pe.wait_ge(s["in_ident"], 16)
            pe.wait_ge(s["xhat_ready"], NT)
            xhat_T(0, 0, xhat, s["a_xT"])
            pe.wait_ge(s["in_wqkv"], 48)
            pe.wait_ge(s["a_h"], KE)
            for i in range(4):
                project_qk(0, i)
            project_v(0)
            pe.wait_ge(s["scbc_done"], 1)
            pe.wait_ge(s["a_r1"], 2)
            pe.wait_ge(s["in_mod1"], 32)
            for u in range(12):
                if u == 4:
                    pe.wait_ge(s["a_vc"], 2)
                    mod_columns(0, range(6, 10))
                    mod_columns(1, range(4))
                    pe.wait_ge(s["in_const"], 16 * 6)
                    pe.wait_ge(s["preset"], 3)
                mod_rows(u)
                if u in (8, 9):
                    max_units(0, 0, (0, 1, 4, 5), 16 * (u - 8), 16 * (u - 7))
                if u == 9:
                    turn_max(0, 0)
            pe.wait_ge(s["bc_sb"], 8)
            pe.wait_ge(s["a_r1"], 4)
            pe.wait_ge(s["modT_done"], 6)
            pe.wait_ge(s["in_wo0"], 32)
            pe.wait_ge(s["pre_pool"], 3)
            with pe.Fori(0, B - 1) as b:
                a_core(b, True)
                b_all(b, True)
            a_core(B - 1, False)
            b_all(B - 1, False)

            pe.wait_ge(s["w_low"], len(w0_pieces) + len(w1_pieces))
            pe.wait_ge(s["in_w1"], 16 * 8)
            pe.wait_ge(s["in_w1"], 16 * 8)
            pe.wait_ge(s["b_x"], 1 + TILES)
            pe.wait_ge(s["preset"], 5)

            def rows_of_heads(bank, w, made):
                for c in range(KE):
                    last = mm(ps[0:8, bank, :], w[:, c, :], hT[:, c, :], start=(c == 0), stop=(c == KE - 1))
                last.then_inc(s[made], 1)

            def turn_rows(bank, buf, moved, done, n):
                pe.wait_ge(s[moved], n + 1)
                pe.sem_inc(s["settled"], 1)
                for t in range(NT):
                    last = tr(ps[:, bank, 8 * t:8 * t + 8], buf[:, t * P:(t + 1) * P], ident[0:8, 0:8])
                last.then_inc(s[done], 1)

            def d_turn(b, h, bank=2):
                pe.wait_ge(s["d_h"], 2 * b + 2)
                xhat_T(b, 0, h, s["d_yT"], bank)

            def d_rows(b, bank=2):
                pe.wait_ge(s["d_yh"], KE * b + KE)
                rows_of_heads(bank, router, "d_lr")

            def c_turn(b, ready):
                pe.wait_ge(s["xhat_ready"], ready)
                xhat_T(b, 0, xhat, s["c_xT"])

            def c_gates(b):
                pe.wait_ge(s["c_h"], KE * b + KE)
                rows_of_heads(0, wg1, "c_gr")

            def scores(b, i):
                t, hg = i // 2, i % 2
                c0 = P if t == 0 else WIN
                sc4 = banks(2 * (i % 2)).rearrange("p (h n) -> p h n", h=4)
                for hh in range(4):
                    h = 4 * hg + hh
                    mm(sc4[:, hh, c0:], qT1[:, h, t * P:(t + 1) * P], kT1[:, h, t * P - (P - c0):(t + 1) * P],
                       start=True, stop=False)
                    last = mm(sc4[:, hh, c0:], identb[:, :], maskw[:, c0 - WIN:], start=False, stop=True)
                last.then_inc(s["c_s"], 1)

            def c_in(b, d=None):

                def project(bank, col, t):
                    for half in range(2):
                        products = [(h, w, c) for h, w in ((hT_hi, w1_hi), (hT_hi, w1_lo), (hT_lo, w1_hi))
                                    for c in range(KE)]
                        for i, (h, w, c) in enumerate(products):
                            last = mm(ps[:, bank + half, :], h[:, c, t * P:(t + 1) * P],
                                      w[:, c, col + half * 512:col + half * 512 + 512],
                                      start=(i == 0), stop=(i == len(products) - 1))
                    return last

                def qk_T(u):
                    pe.wait_ge(s["c_qn"], 2 * NT * b + u + 1)
                    if u >= 1:
                        pe.wait_ge(s["c_qe"], 2 * NT * b + u)
                    else:
                        pe.wait_ge(s["c_x"], NT * b + 1)
                    for h in range(H1):
                        last = tr(ps[:, 6 + h // 4, (h % 4) * P:(h % 4 + 1) * P], qn[:, u % 2, h * P:(h + 1) * P],
                                  ident[:, :])
                    last.then_inc(s["c_qT"], 1)

                pe.wait_ge(s["h_low"], KE * (B + b) + KE)
                for t in range(NT):
                    for u, col in ((2 * t, 0), (2 * t + 1, INNER)):
                        if u >= 2:
                            pe.wait_ge(s["c_qn"], 2 * NT * b + u - 1)
                        project(2 + 2 * (u % 2), col, t).then_inc(s["c_p"], 1)
                        if u == 0:
                            turn_rows(1, qn[0:H1, 1, 0:S], "c_gx", "c_gp", b)
                        if u >= 2:
                            qk_T(u - 2)
                    if t == 0:
                        pe.wait_ge(s["c_g1"], b + 1)
                    else:
                        pe.wait_ge(s["c_ve"], NT * b + t)
                    project(0, 2 * INNER, t).then_inc(s["c_v"], 1)
                qk_T(2 * NT - 2)
                pe.wait_ge(s["c_ve"], NT * b + NT)
                scores(b, 0)
                if d is not None:
                    d_turn(d, hs)
                qk_T(2 * NT - 1)
                if d is not None:
                    d_rows(d)
                if d is not None:
                    turn_rows(4, lrows, "d_lx", "d_l", d)

            def c_core(b, more):
                for i in range(1, 2 * NT + 3):
                    if i < 2 * NT:
                        if i == 1:
                            pe.wait_ge(s["c_qe"], 2 * NT * b + 2 * NT)
                        if i >= 2:
                            pe.wait_ge(s["c_e"], 8 * NT * b + 4 * (i - 1))
                        scores(b, i)
                    if more and i == 2 * NT:
                        c_turn(b + 1, NT * (2 * B + 2 + 2 * b))
                    if more and i == 2 * NT + 1:
                        c_gates(b + 1)
                    if 2 <= i <= 2 * NT + 1:
                        w = i - 2
                        t, hg = w // 2, w % 2
                        k0 = 1 if t == 0 else 0
                        pe.wait_ge(s["c_pTe"], 2 * NT * b + w + 1)
                        if w >= 1:
                            pe.wait_ge(s["c_oe"], 2 * NT * b + w)
                        for hh in range(4):
                            h = 4 * hg + hh
                            for k in range(k0, 2):
                                last = mm(ps[:, 6, hh * P:(hh + 1) * P], v1[:, t - 1 + k, h * P:(h + 1) * P],
                                          pT1[:, w % 2, hh, k, :], start=(k == k0), stop=(k == 1))
                        last.then_inc(s["c_o"], 1)
                    if i >= 4 and i % 2 == 0:
                        t = i // 2 - 2
                        pe.wait_ge(s["c_oe"], 2 * NT * b + 2 * t + 2)
                        pe.wait_ge(s["c_x"], NT * b + t + 1)
                        for h in range(H1):
                            last = mm(ps[:, 7, 0:E], oT1[:, t % 2, h, :], wo1[:, h, :],
                                      start=(h == 0), stop=(h == H1 - 1))
                        last.then_inc(s["c_w"], 1)
                    if 1 <= i <= 2 * NT:
                        w = i - 1
                        k0 = 1 if w < 2 else 0
                        pe.wait_ge(s["c_pn"], 8 * NT * b + 4 * w + 4)
                        if w >= 1:
                            pe.wait_ge(s["c_pTe"], 2 * NT * b + w)
                        else:
                            pe.wait_ge(s["d_lc"], b + 1)
                        for hh in range(4):
                            for k in range(k0, 2):
                                last = tr(banks(4)[:, (2 * hh + k) * P:(2 * hh + k + 1) * P],
                                          pr1[:, w % 2, hh, k * P:(k + 1) * P], ident[:, :])
                        last.then_inc(s["c_pT"], 1)

            c_turn(0, NT * (2 * B + 1))
            c_gates(0)
            c_in(0)
            with pe.Fori(0, B - 1) as b:
                c_core(b, True)
                c_in(b + 1, b)
            c_core(B - 1, False)

            def ranks():
                pe.wait_ge(s["r_v"], 7)
                last = mm(ps[:, 0, 0:(TILES + 1) * NEXP], before[:, :], r_ohx.rearrange("p t e -> p (t e)"),
                          start=True, stop=False)
                for t in range(TILES):
                    n = TILES - t
                    last = mm(ps[:, 0, (t + 1) * NEXP:(TILES + 1) * NEXP].rearrange("p (t e) -> p t e", e=NEXP),
                              ones_b[:, :], r_ohx[:, t:t + 1, :].to_broadcast([P, n, NEXP]),
                              start=False, stop=(t == TILES - 1))
                last.then_inc(s["r_R"], 1)

            def shared_T(m):
                xhat_T(m, 0, h_of[:, m], s["d_xT"])

            def route_between(u):
                if u == 3:
                    turn_rows(1, lrows, "d_lx", "d_l", B - 1)
                if u == 7:
                    ranks()

            pe.wait_ge(s["in_sh"], 48)
            ffn_up(0, 4, shg, shu, "d", [("c_x", 1 + TILES, 2)])
            d_turn(B - 1, h_of[:, B - 1], 0)
            ffn_down(0, 4, shd, gTs, "d")
            d_rows(B - 1, 0)
            ffn_up(1, 4, shg, shu, "d", between=route_between)
            for m in range(B - 2):
                if m == 0:
                    pe.wait_ge(s["in_rt"], 16 * 5)
                    pe.wait_ge(s["r_read"], 1)
                shared_T(m)
                ffn_down(m + 1, 4, shd, gTs, "d")
                pe.wait_ge(s["d_hT"], KE * m + KE)
                ffn_up(m + 2, 4, shg, shu, "d")
            ffn_down(B - 1, 4, shd, gTs, "d")

            pe.sem_inc(s["m_xT"], 2)
            pe.wait_ge(s["in_exp"], 16 * 2 * NEXP)
            pe.wait_ge(s["r_pos_ok"], 1)

            def slot_T(slot, j, i, first=False):
                if not first:
                    pe.wait_ge(s["m_xTe"], slot)
                pe.wait_ge(s[f"m_in{j}"], 16 * i + 16)
                for c in range(KE):
                    last = tr(ps[:, 0, c * P:(c + 1) * P], xs[:, j, c * P:(c + 1) * P], ident[:, :])
                last.then_inc(s["m_xT"], 1)

            def expert_of(slot):
                return pe.value_load(slot_e[0:1, bass.ds(slot, 1)], min_val=0, max_val=NEXP - 1)

            def slot_gu(slot, j):
                e = expert_of(slot)
                pe.wait_ge(s["m_xTe"], slot + 1)
                for half in range(2):
                    for c in range(KE):
                        last = mm(ps[:, 1 + 2 * j + half, :], xsT[:, j, c, :],
                                  wgu[:, c, bass.ds(e * (2 * FE) + half * FE, FE)],
                                  start=(c == 0), stop=(c == KE - 1))
                last.then_inc(s["m_gu"], 1)

            def slot_aT(slot, j, first=False):
                pe.wait_ge(s["m_a"], slot + 1)
                if not first:
                    pe.wait_ge(s["m_aTe"], slot)
                for f in range(4):
                    last = tr(ps[:, 5, f * P:(f + 1) * P], acts[:, j, f * P:(f + 1) * P], ident[:, :])
                last.then_inc(s["m_aT"], 1)

            def slot_down(slot, j):
                e = expert_of(slot)
                pe.wait_ge(s["m_aTe"], slot + 1)
                for f in range(4):
                    last = mm(ps[:, 6 + j, 0:E], actT[:, j, f, :], wdn[:, f, bass.ds(e * E, E)],
                              start=(f == 0), stop=(f == 3))
                last.then_inc(s["m_d"], 1)

            slot_T(0, 0, 0, first=True)
            slot_T(1, 1, 0)
            slot_gu(0, 0)
            slot_T(2, 0, 1)
            slot_gu(1, 1)
            slot_aT(0, 0, first=True)
            with pe.Fori(0, SLOT_PAIRS) as i:
                slot_T(2 * i + 3, 1, i + 1)
                slot_gu(2 * i + 2, 0)
                slot_aT(2 * i + 1, 1)
                slot_down(2 * i, 0)
                slot_T(2 * i + 4, 0, i + 2)
                slot_gu(2 * i + 3, 1)
                slot_aT(2 * i + 2, 0)
                slot_down(2 * i + 1, 1)
            slot_gu(SLOTS - 1, 0)
            slot_aT(SLOTS - 2, 1)
            slot_down(SLOTS - 3, 0)
            slot_aT(SLOTS - 1, 0)
            slot_down(SLOTS - 2, 1)
            slot_down(SLOTS - 1, 0)


def _bf16_bits(v):
    import numpy as np
    return (np.ascontiguousarray(v, dtype=np.float32).view(np.uint32) >> 16).astype(np.uint16)


def _alibi_rows():
    import numpy as np
    slopes = (2.0 ** (-8.0 * np.arange(1, H0 + 1) / H0)).astype(np.float32)
    left = slopes[:, None] * np.arange(S, dtype=np.float32)[None, :]
    rows = np.full((STACK - BIAS_ROW, H0, S), -1.0, dtype=np.float32)
    for a in range(3):
        rows[a] = (left.view(np.uint32) & np.uint32(0xFFFF0000)).view(np.float32)
        left = left - rows[a]
    return _bf16_bits(rows)


def _constants():
    import numpy as np
    i, j = np.arange(P)[:, None], np.arange(P)[None, :]
    far = np.float32(-1e30)
    jw = np.arange(-WIN, P)[None, :]
    cond = {
        "maskq": np.where(j <= i, 0, far),
        "maskk": np.where(i <= j, 0, far),
        "maskw": np.where((i - jw >= 0) & (i - jw <= WIN), 0, far),
        "before": np.where(i < j, 1, 0),
        "identb": np.eye(P),
    }
    c = {k: _bf16_bits(v) for k, v in cond.items()}
    c["ident"] = np.eye(P, dtype=np.float32)
    c["kaug"] = _alibi_rows()

    def rows(a):
        return np.ascontiguousarray(np.broadcast_to(a.astype(np.float32)[None], (P,) + a.shape))

    c["thr"] = rows(np.broadcast_to(P * np.arange(TILES), (NEXP, TILES)))
    c["iota"] = rows(np.broadcast_to(np.arange(SLOTS)[:, None], (SLOTS, NEXP)))
    c["incl"] = rows(np.tril(np.ones((NEXP, NEXP))))
    c["w8"] = rows(np.broadcast_to(NEXP - np.arange(NEXP), (TILES, NEXP)))
    return c


def kernel(**inputs):
    import numpy as np
    import concourse.bacc as bacc
    from concourse.bass_utils import run_bass_kernel_spmd

    a = {k: np.asarray(v) for k, v in inputs.items()}
    c = _constants()

    def by_dim(w):
        return w.reshape(E, 2, HG, D0).transpose(0, 1, 3, 2).reshape(E, E)

    def per_partition(v):
        return np.broadcast_to(v[None, :], (P, v.shape[0]))

    cT = np.stack([a["L0_c"].T.reshape(KE, P, B), a["L1_c"].T.reshape(KE, P, B)]).transpose(2, 0, 1, 3)
    arrays = [
        ("x", a["L0_attn_x"]), ("cT", cT), ("wmod0", a["L0_wmod"]), ("wmod1", a["L1_wmod"]),
        ("wq0", by_dim(a["L0_attn_Wq"])), ("wk0", by_dim(a["L0_attn_Wk"])), ("wv0", a["L0_attn_Wv"]),
        ("wo0", a["L0_attn_Wo"]), ("bo", per_partition(a["L0_attn_bo"])),
        ("wgate", a["L0_ffn_w_gate"].T), ("wup", a["L0_ffn_w_up"].T), ("wdown", a["L0_ffn_w_down"].T),
        ("wq1", a["L1_attn_Wq"].T), ("wkv1", a["L1_attn_Wkv"].T),
        ("qs", a["L1_attn_q_scale"][:, None]), ("ks", a["L1_attn_k_scale"][:, None]),
        ("wg1", a["L1_attn_Wg"].T), ("bg", a["L1_attn_bg"][:, None]), ("wo1", a["L1_attn_Wo"].T),
        ("router", a["L1_ffn_router_w"].T), ("gu", a["L1_ffn_gate_up_proj"]), ("dn", a["L1_ffn_down_proj"]),
        ("sg", a["L1_ffn_shared_gate_w"]), ("su", a["L1_ffn_shared_up_w"]), ("sd", a["L1_ffn_shared_down_w"]),
        ("ident", c["ident"]), ("identb", c["identb"]), ("maskq", c["maskq"]), ("maskk", c["maskk"]),
        ("maskw", c["maskw"]), ("before", c["before"]), ("kaug", c["kaug"]), ("thr", c["thr"]),
        ("iota", c["iota"]), ("incl", c["incl"]), ("w8", c["w8"]),
    ]
    nc = bacc.Bacc("TRN2", target_bir_lowering=False, num_devices=1)
    feeds, aps = {}, []
    for name, v in arrays:
        v = np.ascontiguousarray(v)
        feeds[f"in_{name}"] = v
        aps.append(nc.dram_tensor(f"in_{name}", v.shape, mybir.dt.from_np(v.dtype), kind="ExternalInput").ap())
    out = nc.dram_tensor("out_x", (B, S, E), F32, kind="ExternalOutput").ap()
    program(nc, *aps, out)
    r = run_bass_kernel_spmd(nc, [feeds], core_ids=[0])
    return r.results[0]["out_x"]
```
